# Optimizing a Trainium2 kernel written in Bass

```python
import numpy as np
import jax
import jax.numpy as jnp

def _softmax(x, axis=-1):
    return jax.nn.softmax(x, axis=axis)

def _gelu(x):
    return jax.nn.gelu(x, approximate=True)

def _silu(x):
    return jax.nn.silu(x)

def _sigmoid(x):
    return jax.nn.sigmoid(x)

def _layernorm(x, axis=-1, eps=1e-05):
    m = jnp.mean(x, axis=axis, keepdims=True)
    v = jnp.var(x, axis=axis, keepdims=True)
    return (x - m) / jnp.sqrt(v + eps)

def _scatter_add(tgt, idx, src, axis=0):
    return tgt.at[idx].add(src)

def _segment_sum(src, seg, n):
    return jax.ops.segment_sum(src, seg, n)
kernel_name = 'mk_macaron_d2_jaxref_r8_496692'

def setup_inputs(seed: int=0):
    np.random.seed(seed)
    _w = jnp.asarray

    def _L0_attn_setup():
        import jax, jax.numpy as jnp
        import numpy as np
        DT_MAX = 10.0
        RATE_EPS = 0.0001

        def _ssm_forward(x, W_in, W_state, W_dt, b_dt, A_log, W_C, D, W_out):
            B, L, d_model = x.shape
            ug = jnp.einsum('bld,ed->ble', x, W_in)
            u, gate = jnp.split(ug, 2, axis=-1)
            b_t = jnp.einsum('bld,nd->bln', u, W_state)
            dt_t = jnp.minimum(jax.nn.softplus(jnp.einsum('bld,nd->bln', u, W_dt) + b_dt), DT_MAX)
            rate = jax.nn.softplus(A_log) + RATE_EPS
            decay = jnp.clip(jnp.exp(-dt_t * rate), 0.0, 1.0)

            def step(h, inp):
                d_t, bt = inp
                h = d_t * h + (1.0 - d_t) * bt
                return (h, h)
            h0 = jnp.zeros((B, b_t.shape[-1]), x.dtype)
            xs = (jnp.swapaxes(decay, 0, 1), jnp.swapaxes(b_t, 0, 1))
            _, hs = jax.lax.scan(step, h0, xs)
            hs = jnp.swapaxes(hs, 0, 1)
            y = jnp.einsum('bln,dn->bld', hs, W_C)
            z = y * jax.nn.silu(gate) + x * D
            return jnp.einsum('bld,ed->ble', z, W_out)
        key = jax.random.key(seed)
        ks = jax.random.split(key, 8)
        B, L, D_MODEL, D_STATE = (4, 256, 128, 128)
        s = lambda fan_in: 1.0 / np.sqrt(fan_in)
        return {'x': jax.random.normal(ks[0], (B, L, D_MODEL), jnp.float32), 'W_in': jax.random.normal(ks[1], (2 * D_MODEL, D_MODEL), jnp.float32) * s(D_MODEL), 'W_state': jax.random.normal(ks[2], (D_STATE, D_MODEL), jnp.float32) * s(D_MODEL), 'W_dt': jax.random.normal(ks[3], (D_STATE, D_MODEL), jnp.float32) * s(D_MODEL), 'b_dt': jax.random.normal(ks[4], (D_STATE,), jnp.float32) * s(D_MODEL), 'A_log': jnp.zeros((D_STATE,), jnp.float32), 'W_C': jax.random.normal(ks[5], (D_MODEL, D_STATE), jnp.float32) * s(D_STATE), 'D': jnp.ones((D_MODEL,), jnp.float32), 'W_out': jax.random.normal(ks[6], (D_MODEL, D_MODEL), jnp.float32) * s(D_MODEL)}
    _L0_attn_in = _L0_attn_setup()

    def _L0_ffn_setup():
        import jax, jax.numpy as jnp
        import numpy as np
        TOP_K = 2
        TEMP = 0.9
        EPS = 1e-05
        B, S, D, F, E = (2, 256, 128, 512, 8)

        def _moe_forward(x, gate_w, gate_b, w1, b1, w2, b2, ln_g, ln_b):
            logits = (x @ gate_w + gate_b) / TEMP
            topk_vals, topk_idx = jax.lax.top_k(logits, TOP_K)
            keep = jax.nn.one_hot(topk_idx, E, dtype=jnp.bool_).any(-2)
            masked = jnp.where(keep, logits, -jnp.inf)
            gate_probs = jax.nn.softmax(masked, axis=-1)
            h = jnp.einsum('bsd,edf->bsef', x, w1) + b1
            h = jax.nn.gelu(h, approximate=False)
            expert_out = jnp.einsum('bsef,efd->bsed', h, w2) + b2
            out = jnp.einsum('bse,bsed->bsd', gate_probs, expert_out)
            mu = out.mean(-1, keepdims=True)
            var = out.var(-1, keepdims=True)
            out = (out - mu) / jnp.sqrt(var + EPS) * ln_g + ln_b
            return out
        key = jax.random.key(seed)
        ks = jax.random.split(key, 4)
        scale_in = 1.0 / np.sqrt(D)
        scale_ff = 1.0 / np.sqrt(F)
        return {'x': jax.random.normal(ks[0], (B, S, D), jnp.float32), 'gate_w': jax.random.normal(ks[1], (D, E), jnp.float32) * scale_in, 'gate_b': jnp.zeros((E,), jnp.float32), 'w1': jax.random.normal(ks[2], (E, D, F), jnp.float32) * scale_in, 'b1': jnp.zeros((E, F), jnp.float32), 'w2': jax.random.normal(ks[3], (E, F, D), jnp.float32) * scale_ff, 'b2': jnp.zeros((E, D), jnp.float32), 'ln_g': jnp.ones((D,), jnp.float32), 'ln_b': jnp.zeros((D,), jnp.float32)}
    _L0_ffn_in = _L0_ffn_setup()

    def _L1_attn_setup():
        import jax, jax.numpy as jnp
        import numpy as np
        B, T, D, H, LORA = (4, 128, 128, 16, 64)
        HD = D // H
        BLOCK_ID, N_BLOCKS = (6, 12)

        def _ln(x, w, b, eps=1e-05):
            m = x.mean(-1, keepdims=True)
            v = ((x - m) ** 2).mean(-1, keepdims=True)
            return (x - m) * jax.lax.rsqrt(v + eps) * w + b

        def _lora(z, a, b, l):
            return l + jnp.tanh(z @ a.T) @ b.T

        def _reference_tuple_inner(x, xw, rW, kW, vW, gW, r_la, r_lb, r_ll, k_la, k_lb, k_ll, v_la, v_lb, v_ll, g_la, g_lb, g_ll, d_la, d_lb, d_ll, ln_w, ln_b, oW, init_state, u):
            b, t, d = x.shape
            h = init_state.shape[0]
            hd = d // h
            xx = jnp.concatenate([jnp.zeros_like(x[:, :1]), x[:, :-1]], axis=1)
            dx = xx - x
            lerpx = x + dx * xw
            r = (x + dx * _lora(lerpx, r_la, r_lb, r_ll)) @ rW.T
            k = (x + dx * _lora(lerpx, k_la, k_lb, k_ll)) @ kW.T
            v = (x + dx * _lora(lerpx, v_la, v_lb, v_ll)) @ vW.T
            g = (x + dx * _lora(lerpx, g_la, g_lb, g_ll)) @ gW.T
            w = jnp.exp(-jnp.exp(_lora(x + dx * _lora(lerpx, d_la, d_lb, d_ll), d_la, d_lb, d_ll)))
            split = lambda z: z.reshape(b, t, h, hd).transpose(1, 0, 2, 3)
            rs, ws, ks, vs = (split(r), split(w), split(k), split(v))
            uh = u.reshape(h, hd)
            st0 = jnp.broadcast_to(init_state, (b, h, hd, hd))

            def step(st, inp):
                rt, wt, kt, vt = inp
                kv = jnp.einsum('bhi,bhj->bhij', kt, vt)
                y = jnp.einsum('bhi,bhij->bhj', rt, st + uh[None, :, :, None] * kv)
                return (wt[..., None] * st + kv, y)
            st1, ys = jax.lax.scan(step, st0, (rs, ws, ks, vs))
            o = jax.nn.silu(g.reshape(b, t, h, hd)) * _ln(ys.transpose(1, 0, 2, 3), ln_w, ln_b)
            return (o.reshape(b, t, d) @ oW.T, st1)
        key = jax.random.key(seed)
        ks = iter(jax.random.split(key, 64))
        rn = lambda shape, s: jax.random.normal(next(ks), shape, jnp.float32) * s
        inp = {}
        inp['x'] = rn((B, T, D), 1.0)
        r1 = 1.0 - BLOCK_ID / N_BLOCKS
        i = np.arange(D)
        inp['xw'] = jnp.asarray(1.0 - (i / D) ** r1, jnp.float32)
        for nm in ('rW', 'kW', 'vW', 'gW'):
            inp[nm] = rn((D, D), 0.02)
        for p in ('r', 'k', 'v', 'g', 'd'):
            inp[p + '_la'] = rn((LORA, D), 0.001)
            inp[p + '_lb'] = rn((D, LORA), 0.001)
            inp[p + '_ll'] = rn((D,), 1.0)
        inp['ln_w'] = jnp.full((HD,), ((1 + BLOCK_ID) / N_BLOCKS) ** 0.7, jnp.float32)
        inp['ln_b'] = jnp.zeros((HD,), jnp.float32)
        inp['oW'] = rn((D, D), 0.02)
        inp['init_state'] = rn((H, HD, HD), 1.0)
        r0 = BLOCK_ID / (N_BLOCKS - 1)
        ih = i % HD
        inp['u'] = jnp.asarray(r0 * (1 - ih / (D - 1)) + np.remainder(0.1 * (ih + 1), 3.0), jnp.float32)
        return inp
    _L1_attn_in = _L1_attn_setup()

    def _L1_ffn_setup():
        import jax, jax.numpy as jnp
        import numpy as np
        TOP_K = 2
        key = jax.random.key(seed)
        k0, k1, k2, k3, k4 = jax.random.split(key, 5)
        B, S, H, I, E = (1, 512, 128, 256, 8)
        hidden_states = jax.random.normal(k0, (B, S, H), dtype=jnp.float32)
        wg = jax.random.normal(k1, (E, H), dtype=jnp.float32) * 0.02
        w1 = jax.random.normal(k2, (E, I, H), dtype=jnp.float32) * 0.02
        w3 = jax.random.normal(k3, (E, I, H), dtype=jnp.float32) * 0.02
        w2 = jax.random.normal(k4, (E, H, I), dtype=jnp.float32) * 0.02
        return {'hidden_states': hidden_states, 'wg': wg, 'w1': w1, 'w3': w3, 'w2': w2}
    _L1_ffn_in = _L1_ffn_setup()
    _d = {'L0_attn_x': _L0_attn_in['x'], 'L0_attn_W_in': _L0_attn_in['W_in'], 'L0_attn_W_state': _L0_attn_in['W_state'], 'L0_attn_W_dt': _L0_attn_in['W_dt'], 'L0_attn_b_dt': _L0_attn_in['b_dt'], 'L0_attn_A_log': _L0_attn_in['A_log'], 'L0_attn_W_C': _L0_attn_in['W_C'], 'L0_attn_D': _L0_attn_in['D'], 'L0_attn_W_out': _L0_attn_in['W_out'], 'L0_ffn_gate_w': _L0_ffn_in['gate_w'], 'L0_ffn_gate_b': _L0_ffn_in['gate_b'], 'L0_ffn_w1': _L0_ffn_in['w1'], 'L0_ffn_b1': _L0_ffn_in['b1'], 'L0_ffn_w2': _L0_ffn_in['w2'], 'L0_ffn_b2': _L0_ffn_in['b2'], 'L0_ffn_ln_g': _L0_ffn_in['ln_g'], 'L0_ffn_ln_b': _L0_ffn_in['ln_b'], 'L1_attn_xw': _L1_attn_in['xw'], 'L1_attn_rW': _L1_attn_in['rW'], 'L1_attn_kW': _L1_attn_in['kW'], 'L1_attn_vW': _L1_attn_in['vW'], 'L1_attn_gW': _L1_attn_in['gW'], 'L1_attn_r_la': _L1_attn_in['r_la'], 'L1_attn_r_lb': _L1_attn_in['r_lb'], 'L1_attn_r_ll': _L1_attn_in['r_ll'], 'L1_attn_k_la': _L1_attn_in['k_la'], 'L1_attn_k_lb': _L1_attn_in['k_lb'], 'L1_attn_k_ll': _L1_attn_in['k_ll'], 'L1_attn_v_la': _L1_attn_in['v_la'], 'L1_attn_v_lb': _L1_attn_in['v_lb'], 'L1_attn_v_ll': _L1_attn_in['v_ll'], 'L1_attn_g_la': _L1_attn_in['g_la'], 'L1_attn_g_lb': _L1_attn_in['g_lb'], 'L1_attn_g_ll': _L1_attn_in['g_ll'], 'L1_attn_d_la': _L1_attn_in['d_la'], 'L1_attn_d_lb': _L1_attn_in['d_lb'], 'L1_attn_d_ll': _L1_attn_in['d_ll'], 'L1_attn_ln_w': _L1_attn_in['ln_w'], 'L1_attn_ln_b': _L1_attn_in['ln_b'], 'L1_attn_oW': _L1_attn_in['oW'], 'L1_attn_init_state': _L1_attn_in['init_state'], 'L1_attn_u': _L1_attn_in['u'], 'L1_ffn_wg': _L1_ffn_in['wg'], 'L1_ffn_w1': _L1_ffn_in['w1'], 'L1_ffn_w3': _L1_ffn_in['w3'], 'L1_ffn_w2': _L1_ffn_in['w2']}
    _x0 = _d['L0_attn_x']
    _d['L0_attn_x'] = jax.random.normal(jax.random.fold_in(jax.random.key(seed), 1), (4, 1024, 128), dtype=_x0.dtype)
    del _x0
    return _d

def reference(L0_attn_x, L0_attn_W_in, L0_attn_W_state, L0_attn_W_dt, L0_attn_b_dt, L0_attn_A_log, L0_attn_W_C, L0_attn_D, L0_attn_W_out, L0_ffn_gate_w, L0_ffn_gate_b, L0_ffn_w1, L0_ffn_b1, L0_ffn_w2, L0_ffn_b2, L0_ffn_ln_g, L0_ffn_ln_b, L1_attn_xw, L1_attn_rW, L1_attn_kW, L1_attn_vW, L1_attn_gW, L1_attn_r_la, L1_attn_r_lb, L1_attn_r_ll, L1_attn_k_la, L1_attn_k_lb, L1_attn_k_ll, L1_attn_v_la, L1_attn_v_lb, L1_attn_v_ll, L1_attn_g_la, L1_attn_g_lb, L1_attn_g_ll, L1_attn_d_la, L1_attn_d_lb, L1_attn_d_ll, L1_attn_ln_w, L1_attn_ln_b, L1_attn_oW, L1_attn_init_state, L1_attn_u, L1_ffn_wg, L1_ffn_w1, L1_ffn_w3, L1_ffn_w2):

    def _L0_attn_ref(x, W_in, W_state, W_dt, b_dt, A_log, W_C, D, W_out):
        import jax, jax.numpy as jnp
        import numpy as np
        DT_MAX = 10.0
        RATE_EPS = 0.0001

        def _ssm_forward(x, W_in, W_state, W_dt, b_dt, A_log, W_C, D, W_out):
            B, L, d_model = x.shape
            ug = jnp.einsum('bld,ed->ble', x, W_in)
            u, gate = jnp.split(ug, 2, axis=-1)
            b_t = jnp.einsum('bld,nd->bln', u, W_state)
            dt_t = jnp.minimum(jax.nn.softplus(jnp.einsum('bld,nd->bln', u, W_dt) + b_dt), DT_MAX)
            rate = jax.nn.softplus(A_log) + RATE_EPS
            decay = jnp.clip(jnp.exp(-dt_t * rate), 0.0, 1.0)

            def step(h, inp):
                d_t, bt = inp
                h = d_t * h + (1.0 - d_t) * bt
                return (h, h)
            h0 = jnp.zeros((B, b_t.shape[-1]), x.dtype)
            xs = (jnp.swapaxes(decay, 0, 1), jnp.swapaxes(b_t, 0, 1))
            _, hs = jax.lax.scan(step, h0, xs)
            hs = jnp.swapaxes(hs, 0, 1)
            y = jnp.einsum('bln,dn->bld', hs, W_C)
            z = y * jax.nn.silu(gate) + x * D
            return jnp.einsum('bld,ed->ble', z, W_out)
        return _ssm_forward(x, W_in, W_state, W_dt, b_dt, A_log, W_C, D, W_out)

    def _L0_ffn_ref(x, gate_w, gate_b, w1, b1, w2, b2, ln_g, ln_b):
        import jax, jax.numpy as jnp
        import numpy as np
        TOP_K = 2
        TEMP = 0.9
        EPS = 1e-05
        B, S, D, F, E = (2, 256, 128, 512, 8)

        def _moe_forward(x, gate_w, gate_b, w1, b1, w2, b2, ln_g, ln_b):
            logits = (x @ gate_w + gate_b) / TEMP
            topk_vals, topk_idx = jax.lax.top_k(logits, TOP_K)
            keep = jax.nn.one_hot(topk_idx, E, dtype=jnp.bool_).any(-2)
            masked = jnp.where(keep, logits, -jnp.inf)
            gate_probs = jax.nn.softmax(masked, axis=-1)
            h = jnp.einsum('bsd,edf->bsef', x, w1) + b1
            h = jax.nn.gelu(h, approximate=False)
            expert_out = jnp.einsum('bsef,efd->bsed', h, w2) + b2
            out = jnp.einsum('bse,bsed->bsd', gate_probs, expert_out)
            mu = out.mean(-1, keepdims=True)
            var = out.var(-1, keepdims=True)
            out = (out - mu) / jnp.sqrt(var + EPS) * ln_g + ln_b
            return out
        return _moe_forward(x, gate_w, gate_b, w1, b1, w2, b2, ln_g, ln_b)

    def _L1_attn_ref(x, xw, rW, kW, vW, gW, r_la, r_lb, r_ll, k_la, k_lb, k_ll, v_la, v_lb, v_ll, g_la, g_lb, g_ll, d_la, d_lb, d_ll, ln_w, ln_b, oW, init_state, u):
        import jax, jax.numpy as jnp
        import numpy as np
        B, T, D, H, LORA = (4, 128, 128, 16, 64)
        HD = D // H
        BLOCK_ID, N_BLOCKS = (6, 12)

        def _ln(x, w, b, eps=1e-05):
            m = x.mean(-1, keepdims=True)
            v = ((x - m) ** 2).mean(-1, keepdims=True)
            return (x - m) * jax.lax.rsqrt(v + eps) * w + b

        def _lora(z, a, b, l):
            return l + jnp.tanh(z @ a.T) @ b.T

        def _reference_tuple_inner(x, xw, rW, kW, vW, gW, r_la, r_lb, r_ll, k_la, k_lb, k_ll, v_la, v_lb, v_ll, g_la, g_lb, g_ll, d_la, d_lb, d_ll, ln_w, ln_b, oW, init_state, u):
            b, t, d = x.shape
            h = init_state.shape[0]
            hd = d // h
            xx = jnp.concatenate([jnp.zeros_like(x[:, :1]), x[:, :-1]], axis=1)
            dx = xx - x
            lerpx = x + dx * xw
            r = (x + dx * _lora(lerpx, r_la, r_lb, r_ll)) @ rW.T
            k = (x + dx * _lora(lerpx, k_la, k_lb, k_ll)) @ kW.T
            v = (x + dx * _lora(lerpx, v_la, v_lb, v_ll)) @ vW.T
            g = (x + dx * _lora(lerpx, g_la, g_lb, g_ll)) @ gW.T
            w = jnp.exp(-jnp.exp(_lora(x + dx * _lora(lerpx, d_la, d_lb, d_ll), d_la, d_lb, d_ll)))
            split = lambda z: z.reshape(b, t, h, hd).transpose(1, 0, 2, 3)
            rs, ws, ks, vs = (split(r), split(w), split(k), split(v))
            uh = u.reshape(h, hd)
            st0 = jnp.broadcast_to(init_state, (b, h, hd, hd))

            def step(st, inp):
                rt, wt, kt, vt = inp
                kv = jnp.einsum('bhi,bhj->bhij', kt, vt)
                y = jnp.einsum('bhi,bhij->bhj', rt, st + uh[None, :, :, None] * kv)
                return (wt[..., None] * st + kv, y)
            st1, ys = jax.lax.scan(step, st0, (rs, ws, ks, vs))
            o = jax.nn.silu(g.reshape(b, t, h, hd)) * _ln(ys.transpose(1, 0, 2, 3), ln_w, ln_b)
            return (o.reshape(b, t, d) @ oW.T, st1)
        return _reference_tuple_inner(x, xw, rW, kW, vW, gW, r_la, r_lb, r_ll, k_la, k_lb, k_ll, v_la, v_lb, v_ll, g_la, g_lb, g_ll, d_la, d_lb, d_ll, ln_w, ln_b, oW, init_state, u)[0]

    def _L1_ffn_ref(hidden_states, wg, w1, w3, w2):
        import jax, jax.numpy as jnp
        import numpy as np
        TOP_K = 2
        orig_shape = hidden_states.shape
        H = orig_shape[-1]
        E = wg.shape[0]
        x = hidden_states.reshape(-1, H)
        router_logits = x @ wg.T
        probs = jax.nn.softmax(router_logits, axis=-1)
        topk_w, topk_idx = jax.lax.top_k(probs, TOP_K)
        topk_w = topk_w / jnp.sum(topk_w, axis=-1, keepdims=True)
        expert_w = jnp.sum(jax.nn.one_hot(topk_idx, E, dtype=x.dtype) * topk_w[..., None], axis=1)
        h1 = jnp.einsum('th,eih->tei', x, w1)
        h3 = jnp.einsum('th,eih->tei', x, w3)
        y = jnp.einsum('tei,ehi->teh', jax.nn.silu(h1) * h3, w2)
        out = jnp.einsum('te,teh->th', expert_w, y)
        return out.reshape(orig_shape)
    x = L0_attn_x
    x = x + 0.5 * _L0_ffn_ref(_layernorm(x, axis=-1), L0_ffn_gate_w, L0_ffn_gate_b, L0_ffn_w1, L0_ffn_b1, L0_ffn_w2, L0_ffn_b2, L0_ffn_ln_g, L0_ffn_ln_b)
    x = x + _L0_attn_ref(_layernorm(x, axis=-1), L0_attn_W_in, L0_attn_W_state, L0_attn_W_dt, L0_attn_b_dt, L0_attn_A_log, L0_attn_W_C, L0_attn_D, L0_attn_W_out)
    x = x + 0.5 * _L0_ffn_ref(_layernorm(x, axis=-1), L0_ffn_gate_w, L0_ffn_gate_b, L0_ffn_w1, L0_ffn_b1, L0_ffn_w2, L0_ffn_b2, L0_ffn_ln_g, L0_ffn_ln_b)
    x = x + 0.5 * _L1_ffn_ref(_layernorm(x, axis=-1), L1_ffn_wg, L1_ffn_w1, L1_ffn_w3, L1_ffn_w2)
    x = x + _L1_attn_ref(_layernorm(x, axis=-1), L1_attn_xw, L1_attn_rW, L1_attn_kW, L1_attn_vW, L1_attn_gW, L1_attn_r_la, L1_attn_r_lb, L1_attn_r_ll, L1_attn_k_la, L1_attn_k_lb, L1_attn_k_ll, L1_attn_v_la, L1_attn_v_lb, L1_attn_v_ll, L1_attn_g_la, L1_attn_g_lb, L1_attn_g_ll, L1_attn_d_la, L1_attn_d_lb, L1_attn_d_ll, L1_attn_ln_w, L1_attn_ln_b, L1_attn_oW, L1_attn_init_state, L1_attn_u)
    x = x + 0.5 * _L1_ffn_ref(_layernorm(x, axis=-1), L1_ffn_wg, L1_ffn_w1, L1_ffn_w3, L1_ffn_w2)
    return x

_drawn_inputs = setup_inputs


def setup_inputs(seed=0):
    import zlib

    import numpy as np

    out = dict(_drawn_inputs(seed))
    spreads = {'L0_attn_A_log': (0.0, 0.286),
     'L0_attn_D': (1.0, 0.2),
     'L0_ffn_gate_b': (0.0, 0.1),
     'L0_ffn_b1': (0.0, 0.1),
     'L0_ffn_b2': (0.0, 0.1),
     'L0_ffn_ln_g': (1.0, 0.2),
     'L0_ffn_ln_b': (0.0, 0.1),
     'L1_attn_ln_w': (0.6857119798660278, 0.6),
     'L1_attn_ln_b': (0.0, 0.8)}
    factors = {'L0_attn_b_dt': 2.705,
     'L1_attn_xw': 22.593,
     'L1_attn_rW': 3.018,
     'L1_attn_kW': 3.048,
     'L1_attn_vW': 2.993,
     'L1_attn_gW': 3.007,
     'L1_attn_r_la': 23.334,
     'L1_attn_r_lb': 26.266,
     'L1_attn_r_ll': 3.543,
     'L1_attn_k_la': 36.191,
     'L1_attn_k_lb': 43.101,
     'L1_attn_k_ll': 3.507,
     'L1_attn_v_la': 36.064,
     'L1_attn_v_lb': 37.973,
     'L1_attn_v_ll': 3.623,
     'L1_attn_g_la': 28.235,
     'L1_attn_g_lb': 23.074,
     'L1_attn_g_ll': 3.627,
     'L1_attn_d_la': 181.469,
     'L1_attn_d_lb': 64.0,
     'L1_attn_d_ll': 7.383,
     'L1_attn_oW': 2.993,
     'L1_attn_init_state': 8.0,
     'L1_attn_u': 8.0,
     'L1_ffn_wg': 8.0,
     'L1_ffn_w1': 8.0,
     'L1_ffn_w3': 8.0,
     'L1_ffn_w2': 8.0}
    for name, (base, spread) in spreads.items():
        noise = np.random.default_rng([zlib.crc32(name.encode()), seed]).standard_normal(out[name].shape)
        drawn = base * np.exp(spread * noise) if base else spread * noise
        out[name] = jnp.asarray(drawn.astype(out[name].dtype))
    for name, factor in factors.items():
        out[name] = (out[name] * factor).astype(out[name].dtype)
    return out
```

```python
from contextlib import ExitStack

import concourse.bass as bass
from concourse import mybir

F32 = mybir.dt.float32
F32R = mybir.dt.float32r
ALU = mybir.AluOpType
ACT = mybir.ActivationFunctionType

P = 128
D = 128
NB, SEQ = 4, 1024
TOK = NB * SEQ
TILE = 512
SUB = TILE // P
NT = TOK // TILE
PAIRS = NT // 2
E = 8
FF = 512
FI = 256
HEADS, HD = 16, 8
LORA = 64
EPS = 1e-5
TEMP = 0.9
DT_MAX = 10.0
RATE_EPS = 1e-4
BIG = 3.0e38

VECTORS = ["L0_attn_b_dt", "L0_attn_A_log", "L0_attn_D", "L1_attn_xw", "L1_attn_r_ll", "L1_attn_k_ll",
           "L1_attn_v_ll", "L1_attn_g_ll", "L1_attn_d_ll", "L1_attn_u"]
COL = {n: i for i, n in enumerate(VECTORS)}
COL_B2 = len(VECTORS)
COL_WG = COL_B2 + E
COL_B1 = COL_WG + E
COL_LNW = COL_B1 + E * FF // P
COL_LNB = COL_LNW + 1
COLS = COL_LNB + 1

SQUARES = ["Wu", "Wgate", "Wstate", "Wdt", "WC", "Wout", "rW", "kW", "vW", "gW", "oW"]
LORAS = "rkvgd"
SQ = {n: i for i, n in enumerate(SQUARES)}
LA = {"r": (0, 0), "k": (0, 1), "v": (1, 0), "g": (1, 1), "d": (2, 0)}


class Steps:

    def __init__(self, eng, sem, before, held=None):
        self.eng, self.sem, self.before, self.held, self.n = eng, sem, before, held, 0

    def step(self, ins):
        ins.then_inc(self.sem, 1)
        self.n += 1

    def settle(self):
        self.eng.wait_ge(self.sem, self.before + self.n)

    def settle_apart(self):
        self.settle()
        self.eng.sem_inc(self.held, 1)


class Layer:

    def __init__(self, nc, ctx, name):
        self.nc, self.ctx, self.name, self.sems = nc, ctx, name, []
        ctx.callback(self.clear)

    def sb(self, name, shape, dt=F32):
        return self.ctx.enter_context(self.nc.sbuf_tensor(f"{self.name}_{name}", shape, dt))

    def bank(self, name):
        return self.ctx.enter_context(self.nc.psum_tensor(f"{self.name}_{name}", [P, TILE], F32))

    def sem(self, name):
        self.sems.append(self.nc.alloc_semaphore(name=f"{self.name}_{name}"))
        return self.sems[-1]

    def clear(self):
        self.nc.clear_and_free_semaphores(self.sems)
        self.nc.all_engine_barrier()


def row(ap):
    return ap.rearrange("(a n) -> a n", a=1)


def of_tile(x, t):
    return x[:, bass.ds(t * SUB, SUB), :]


def of_group(x, t, s):
    return x[:, bass.ds(t * SUB + s, 1), :].rearrange("p a d -> p (a d)")


def setup(nc, ins, x, res, ident, block_diag):
    with ExitStack() as ctx:
        L = Layer(nc, ctx, "setup")
        raw1 = L.sb("raw1", [P, E, FF])
        raw2 = raw1[:, :, :].rearrange("p e f -> p (e f)").rearrange("p (c d) -> p c d", d=D)
        raw_s1 = L.sb("raw_s1", [P, E * FI // P, D])
        raw_s3 = L.sb("raw_s3", [P, E * FI // P, D])
        raw_s2 = L.sb("raw_s2", [P, E, FI])
        raw_sq = L.sb("raw_sq", [P, len(SQUARES), P])
        raw_la = L.sb("raw_la", [P, 3, P])
        raw_lb = L.sb("raw_lb", [P, 3, P])
        raw_cols = L.sb("raw_cols", [COLS, P])
        raw_gate = L.sb("raw_gate", [P, E])
        banks = [L.bank(f"bank{k}") for k in range(8)]
        small_in = L.sem("small_in")
        x_in = L.sem("x_in")
        gelu_in = L.sem("gelu_in")
        swiglu_in = L.sem("swiglu_in")
        zeroed = L.sem("zeroed")
        turned = L.sem("turned")
        emptied = L.sem("emptied")
        high = L.sem("high")
        low = L.sem("low")
        misc = L.sem("misc")
        block = ctx.enter_context(nc.Block())

        jobs = []
        squares = [(raw_sq[:, k, :], P, P) for k in range(len(SQUARES))]
        squares += [(raw_la[:, k, :] if k < 2 else raw_la[0:LORA, k, :], P if k < 2 else LORA, P) for k in range(3)]
        squares += [(raw_lb[:, k, :] if k < 2 else raw_lb[:, k, 0:LORA], P, P if k < 2 else LORA) for k in range(3)]
        outs = [res["sqT"][:, k, :] for k in range(len(SQUARES))]
        outs += [res["laT"][:, k, :] if k < 2 else res["laT"][:, k, 0:LORA] for k in range(3)]
        outs += [res["lbT"][:, k, :] if k < 2 else res["lbT"][0:LORA, k, :] for k in range(3)]
        squares.append((raw_cols[:, :], COLS, P))
        outs.append(res["cols"][:, 0:COLS])
        n_small = len(squares)
        swiglu_turns = []
        for raw, hi, lo in ((raw_s1, "s1h", "s1l"), (raw_s3, "s3h", "s3l")):
            for k in range(0, E * FI // P, 4):
                swiglu_turns.append(([raw[:, k + j, :] for j in range(4)],
                                     res[hi][:, k * P:(k + 4) * P], res[lo][:, k * P:(k + 4) * P]))
        for k in range(0, E * FI // P, 4):
            swiglu_turns.append(([raw_s2[:, (k + j) // 2, ((k + j) % 2) * P:((k + j) % 2 + 1) * P] for j in range(4)],
                                 res["s2h"][:, k * P:(k + 4) * P], res["s2l"][:, k * P:(k + 4) * P]))
        gelu_parts = [(raw1[:, :, :], res["w1h"][:, :, :], res["w1l"][:, :, :]),
                      (raw2, res["w2h"][:, :, :], res["w2l"][:, :, :])]

        total_small = (3 + len(VECTORS) + 3 + 2 + 3) + (len(SQUARES) - 1 + 2 * len(LORAS) + 1)

        @block.sync
        def _(sp):
            def small(dst, src):
                sp.dma_start(dst, src).then_inc(small_in, 16)

            sp.dma_start(x[:, :, :], ins["L0_attn_x"].rearrange("b (g p) d -> p (b g) d", p=P)).then_inc(x_in, 16)
            small(ident[:, :], ins["const_ident"])
            small(block_diag[:, :], ins["const_block"])
            small(raw_gate[:, :], ins["L0_ffn_gate_w"])
            sp.wait_ge(zeroed, 1)
            for n in VECTORS:
                small(raw_cols[COL[n]:COL[n] + 1, :], row(ins[n]))
            small(raw_cols[COL_B2:COL_B2 + E, :], ins["L0_ffn_b2"])
            small(raw_cols[COL_WG:COL_WG + E, :], ins["L1_ffn_wg"])
            small(raw_cols[COL_B1:COL_LNW, :], ins["L0_ffn_b1"].rearrange("e (c p) -> (e c) p", p=P))
            for c, n in ((COL_LNW, "L1_attn_ln_w"), (COL_LNB, "L1_attn_ln_b")):
                small(raw_cols[c:c + 1, :].rearrange("a (h j) -> a h j", j=HD),
                      ins[n].rearrange("(a b j) -> a b j", a=1, b=1).broadcast_to([1, HEADS, HD]))
            small(res["gate_bias"][:, :], row(ins["L0_ffn_gate_b"]).broadcast_to([P, E]))
            small(res["post_g"][:, :], row(ins["L0_ffn_ln_g"]).broadcast_to([P, D]))
            small(res["post_b"][:, :], row(ins["L0_ffn_ln_b"]).broadcast_to([P, D]))
            sp.dma_start(raw1[:, :, :], ins["L0_ffn_w1"].rearrange("e d f -> d e f")).then_inc(gelu_in, 16)
            sp.wait_ge(low, 3)
            sp.dma_start(raw2, ins["L0_ffn_w2"].rearrange("e (c p) d -> p (e c) d", p=P)).then_inc(gelu_in, 16)

        @block.gpsimd
        def _(pool):
            pool.memset(raw_cols[:, :], 0.0).then_inc(zeroed, 1)
            pool.memset(res["replace"][:, :, :], BIG)
            pool.memset(res["neg_half"][:, :], -0.5)
            pool.memset(res["e_temp"][:, :], float(2.718281828459045 ** (1.0 / TEMP)))
            pool.memset(res["eps"][:, :], EPS)
            pool.memset(res["e_one"][:, :], 2.718281828459045)
            pool.memset(res["sel"][:, :, :], 0.0).then_inc(misc, 1)
            pool.wait_ge(small_in, 16 * total_small)
            pool.wait_ge(misc, 1)
            for n in ("post_g", "post_b"):
                pool.tensor_scalar_mul(res[n][:, :], res[n][:, :], 0.5).then_inc(misc, 1)
            for j in range(HD):
                pool.tensor_copy(res["sel"][:, j, :].rearrange("p (h j) -> p h j", j=HD)[:, :, j],
                                 block_diag[:, :].rearrange("p (h j) -> p h j", j=HD)[:, :, j]).then_inc(misc, 1)
            pool.tensor_scalar_mul(res["head_mean"][:, :], block_diag[:, :], 1.0 / HD).then_inc(misc, 1)
            pool.wait_ge(misc, 4 + HD)
            pool.tensor_tensor(res["head_centre"][:, :], ident[:, :], res["head_mean"][:, :], ALU.subtract).then_inc(misc, 1)

        @block.scalar
        def _(act):
            def extra(dst, src):
                act.dma_start(dst, src).then_inc(small_in, 16)

            extra(raw_sq[:, 0:2, :], ins["L0_attn_W_in"].rearrange("(a p) d -> p a d", p=P))
            for k, n in enumerate(("L0_attn_W_state", "L0_attn_W_dt", "L0_attn_W_C", "L0_attn_W_out", "L1_attn_rW",
                                   "L1_attn_kW", "L1_attn_vW", "L1_attn_gW", "L1_attn_oW")):
                extra(raw_sq[:, 2 + k, :], ins[n])
            for q in LORAS:
                pair, half = LA[q]
                extra(raw_la[half * LORA:(half + 1) * LORA, pair, :], ins[f"L1_attn_{q}_la"])
                extra(raw_lb[:, pair, half * LORA:(half + 1) * LORA], ins[f"L1_attn_{q}_lb"])
            extra(res["state0"][:, :], ins["L1_attn_init_state"].rearrange("h i j -> (h i) j"))
            act.dma_start(raw_s1[:, :, :], ins["L1_ffn_w1"].rearrange("e (c p) h -> p (e c) h", p=P)).then_inc(swiglu_in, 16)
            act.dma_start(raw_s3[:, :, :], ins["L1_ffn_w3"].rearrange("e (c p) h -> p (e c) h", p=P)).then_inc(swiglu_in, 16)
            act.dma_start(raw_s2[:, :, :], ins["L1_ffn_w2"].rearrange("e h i -> h e i")).then_inc(swiglu_in, 16)
            for k, (src, hi, _lo) in enumerate(gelu_parts):
                act.wait_ge(gelu_in, 16 * (k + 1))
                act.copy(hi, src).then_inc(high, 1)
            for k, (_src, hi, _lo) in enumerate(swiglu_turns):
                act.wait_ge(turned, n_small + k + 1)
                act.copy(hi, banks[(n_small + k) % 8][:, :]).then_inc(high, 1)

        @block.tensor
        def _(pe):
            pe.wait_ge(small_in, 16 * total_small)
            for k, (src, rows, cols) in enumerate(squares):
                if k >= 8:
                    pe.wait_ge(emptied, k - 7)
                pe.transpose(banks[k % 8][0:cols, 0:rows], src, ident[0:rows, 0:rows]).then_inc(turned, 1)
            pe.wait_ge(swiglu_in, 48)
            for k, (srcs, _hi, _lo) in enumerate(swiglu_turns):
                pe.wait_ge(emptied, n_small + k - 7)
                for j, src in enumerate(srcs):
                    last = pe.transpose(banks[(n_small + k) % 8][:, j * P:(j + 1) * P], src, ident[:, :])
                last.then_inc(turned, 1)

        @block.vector
        def _(dve):
            for k, (dst, (src, rows, cols)) in enumerate(zip(outs, squares)):
                dve.wait_ge(turned, k + 1)
                dve.tensor_copy(dst, banks[k % 8][0:cols, 0:rows]).then_inc(emptied, 1)
            dve.wait_ge(emptied, n_small)
            wg = res["cols"][:, COL_WG:COL_WG + E]
            dve.tensor_copy(res["gate0h"][:, :], raw_gate[:, :]).then_inc(low, 1)
            dve.tensor_copy(res["gate1h"][:, :], wg).then_inc(low, 1)
            dve.wait_ge(low, 2)
            dve.tensor_tensor(res["gate0l"][:, :], raw_gate[:, :], res["gate0h"][:, :].bitcast(F32), ALU.subtract)
            dve.tensor_tensor(res["gate1l"][:, :], wg, res["gate1h"][:, :].bitcast(F32), ALU.subtract)
            for j in range(HD):
                dve.tensor_copy(res["v_each"][:, j, :].rearrange("p (h i) -> p h i", i=HD),
                                res["sqT"][:, SQ["vW"], :].rearrange("p (h j) -> p h j", j=HD)[:, :, j:j + 1]
                                .broadcast_to([P, HEADS, HD]))
            for k, (src, hi, lo) in enumerate(gelu_parts):
                dve.wait_ge(high, k + 1)
                dve.tensor_tensor(lo, src, hi.bitcast(F32), ALU.subtract).then_inc(low, 1)
            for k, (_src, hi, lo) in enumerate(swiglu_turns):
                dve.wait_ge(high, len(gelu_parts) + k + 1)
                dve.tensor_tensor(lo, banks[(n_small + k) % 8][:, :], hi.bitcast(F32), ALU.subtract).then_inc(emptied, 1)


def rates(nc, res):
    with ExitStack() as ctx:
        L = Layer(nc, ctx, "rates")
        t1 = L.sb("t1", [P, 1])
        t2 = L.sb("t2", [P, 1])
        t3 = L.sb("t3", [P, 1])
        acted = L.sem("acted")
        summed = L.sem("summed")
        a_log = res["cols"][:, COL["L0_attn_A_log"]:COL["L0_attn_A_log"] + 1]
        block = ctx.enter_context(nc.Block())

        @block.scalar
        def _(act):
            act.activation(t1[:, :], a_log, ACT.Abs).then_inc(acted, 1)
            act.wait_ge(acted, 1)
            act.activation(t2[:, :], t1[:, :], ACT.Exp, scale=-1.0).then_inc(acted, 1)
            act.wait_ge(acted, 2)
            act.activation(t3[:, :], t2[:, :], ACT.Ln, bias=1.0).then_inc(acted, 1)
            act.wait_ge(summed, 2)
            act.activation(res["floor"][:, :], res["neg_rate"][:, :], ACT.Exp, scale=DT_MAX).then_inc(acted, 1)

        @block.vector
        def _(dve):
            dve.wait_ge(acted, 3)
            dve.scalar_tensor_tensor(t1[:, :], a_log, 0.0, t3[:, :], ALU.max, ALU.add).then_inc(summed, 1)
            dve.wait_ge(summed, 1)
            dve.tensor_scalar(res["neg_rate"][:, :], t1[:, :], RATE_EPS, -1.0, ALU.add, ALU.mult).then_inc(summed, 1)


def mixture(nc, name, kind, x, res, ident):
    gelu = kind == "gelu"
    CH = (FF if gelu else FI) // P
    NC = E * CH
    LAG = 3 if gelu else 2
    RING = 4
    H_BUFS = 4 if gelu else 2
    PB_RING = 4
    SCALE_LAG = 4 if gelu else 3
    EPI = LAG + 5 if gelu else LAG + 4
    STATS, NORM = SCALE_LAG, SCALE_LAG + 2
    TURN, GATE = (14, 18) if gelu else (9, 11)
    GATE_E = (GATE + 1 - SCALE_LAG) // CH
    if gelu:
        w1h, w1l = res["w1h"][:, :, :].rearrange("p e f -> p (e f)"), res["w1l"][:, :, :].rearrange("p e f -> p (e f)")
        w2h, w2l = res["w2h"][:, :, :].rearrange("p c d -> p (c d)"), res["w2l"][:, :, :].rearrange("p c d -> p (c d)")
        gate_h, gate_l, base = res["gate0h"], res["gate0l"], res["e_temp"]
    else:
        w1h, w1l, w3h, w3l = (res[n][:, :] for n in ("s1h", "s1l", "s3h", "s3l"))
        w2h, w2l = res["s2h"][:, :], res["s2l"][:, :]
        gate_h, gate_l, base = res["gate1h"], res["gate1l"], res["e_one"]

    def chunk(w, n):
        return w[:, n * P:(n + 1) * P]

    with ExitStack() as ctx:
        L = Layer(nc, ctx, name)
        xn = L.sb("xn", [P, SUB, D])
        xTh = [L.sb(f"xTh{q}", [P, TILE], F32R) for q in range(2)]
        xTl = [L.sb(f"xTl{q}", [P, TILE], F32R) for q in range(2)]
        gate = [L.sb(f"gate{q}", [P, SUB, E]) for q in range(2)]
        sil = None if gelu else L.sb("sil", [P, RING, TILE])
        hid = L.sb("hid", [P, RING, TILE])
        hidh = L.sb("hidh", [P, RING, TILE], F32R)
        hidl = L.sb("hidl", [P, RING, TILE], F32R)
        gate_b = L.sb("gate_b", [P, PB_RING, TILE])
        part = L.sb("part", [P, 2, TILE])
        acc = L.sb("acc", [P, TILE])
        yn = L.sb("yn", [P, SUB, D]) if gelu else None
        st = L.sb("st", [P, SUB, 6])
        mv = L.sb("mv", [P, SUB, 2])
        ve = L.sb("ve", [P, SUB])
        rstd = L.sb("rstd", [P, SUB])
        st2 = L.sb("st2", [P, SUB, 6])
        mv2 = L.sb("mv2", [P, SUB, 2])
        ve2 = L.sb("ve2", [P, SUB])
        rstd2 = L.sb("rstd2", [P, SUB])
        lg = L.sb("lg", [P, SUB, E])
        top = L.sb("top", [P, SUB, 8])
        cut = L.sb("cut", [P, SUB, E])
        diff = L.sb("diff", [P, SUB])
        e2 = L.sb("e2", [P, SUB])
        den = L.sb("den", [P, SUB])
        mask = L.sb("mask", [P, SUB, E])
        first = L.sb("first", [P, SUB, E])
        weight = L.sb("weight", [P, SUB, E])
        replace = res["replace"]

        hb = [L.bank(f"hb{k}") for k in range(4)]
        ob = [L.bank(f"ob{k}") for k in range(2)]
        pb = L.bank("pb")
        tp = L.bank("tp")
        tp_s = tp[:, :].rearrange("p (s d) -> p s d", s=SUB)
        lg_ps = tp[:, 0:SUB * E].rearrange("p (s e) -> p s e", s=SUB)

        chain, held = L.sem("dve_chain"), L.sem("held")
        pvar, prstd = L.sem("pvar"), L.sem("prstd")
        evar, erstd = L.sem("evar"), L.sem("erstd")
        xn_ready, xt_ready, split_done = L.sem("xn_ready"), L.sem("xt_ready"), L.sem("split_done")
        lg_ready, lg_read = L.sem("lg_ready"), L.sem("lg_read")
        diff_ready, e2_ready, gate_ready = L.sem("diff_ready"), L.sem("e2_ready"), L.sem("gate_ready")
        h_ready = L.sem("h_ready")
        act_done = L.sem("act_done")
        mul_done = L.sem("mul_done")
        hh_ready, hl_ready = L.sem("hh_ready"), L.sem("hl_ready")
        second_done = L.sem("second_done")
        scaled = L.sem("scaled")
        acc_done = L.sem("acc_done")
        pb_ready, pb_copied = L.sem("pb_ready"), L.sem("pb_copied")
        out_ready, out_read = L.sem("out_ready"), L.sem("out_read")
        yn_ready = L.sem("yn_ready")
        x_done = L.sem("x_done")
        block = ctx.enter_context(nc.Block())

        ADDS = E - 1

        @block.tensor
        def _(pe):
            def turn_tokens(t):
                pe.wait_ge(xn_ready, t + 1)
                if not isinstance(t, int) or t:
                    pe.wait_ge(out_read, t)
                for s in range(SUB):
                    last = pe.transpose(tp[:, s * P:(s + 1) * P], xn[:, s, :], ident[:, :])
                last.then_inc(xt_ready, 1)

            def logits(t, q):
                pe.wait_ge(split_done, t + 1)
                for s in range(SUB):
                    xh, xl = xTh[q][:, s * P:(s + 1) * P], xTl[q][:, s * P:(s + 1) * P]
                    pe.matmul(lg_ps[:, s, :], xh, gate_h[:, :], start=True, stop=False)
                    pe.matmul(lg_ps[:, s, :], xh, gate_l[:, :], start=False, stop=False)
                    last = pe.matmul(lg_ps[:, s, :], xl, gate_h[:, :], start=False, stop=True)
                last.then_inc(lg_ready, 1)

            def spread_gate(t, q, e):
                if e == 0:
                    pe.wait_ge(gate_ready, t + 1)
                pe.wait_ge(pb_copied, t * E + e + 1)
                for s in range(SUB):
                    last = pe.transpose(pb[:, s * P:(s + 1) * P], gate[q][:, s, e:e + 1].broadcast_to([P, P]), ident[:, :])
                last.then_inc(pb_ready, 1)

            def first_products(N, T0, q, n):
                if gelu:
                    pe.wait_ge(act_done, T0 + N + 1)
                    for w, xx in ((w1h, xTh), (w1l, xTh), (w1h, xTl)):
                        last = pe.matmul(hb[N % 4][:, :], chunk(w, n), xx[q][:, :], start=w is w1h and xx is xTh, stop=xx is xTl)
                else:
                    pe.wait_ge(mul_done, T0 + N + 1)
                    for b, wh, wl in ((N % 2, w1h, w1l), (2 + N % 2, w3h, w3l)):
                        pe.matmul(hb[b][:, :], chunk(wh, n), xTh[q][:, :], start=True, stop=False)
                        pe.matmul(hb[b][:, :], chunk(wl, n), xTh[q][:, :], start=False, stop=False)
                        last = pe.matmul(hb[b][:, :], chunk(wh, n), xTl[q][:, :], start=False, stop=True)
                last.then_inc(h_ready, 1)

            def second_products(N, T0, G0, n):
                e, c = n // CH, n % CH
                if c == 0:
                    pe.wait_ge(scaled, G0 + N // CH + PB_RING - 1)
                pe.wait_ge(hl_ready, T0 + N + RING + 1)
                r = N % RING
                o = ob[e % 2][:, :]
                pe.matmul(o, chunk(w2h, n), hidh[:, r, :], start=c == 0, stop=False)
                pe.matmul(o, chunk(w2l, n), hidh[:, r, :], start=False, stop=False)
                last = pe.matmul(o, chunk(w2h, n), hidl[:, r, :], start=False, stop=c == CH - 1)
                last.then_inc(second_done, 1)

            def turn_back(t, routed):
                pe.wait_ge(acc_done, (t + 1) * ADDS + 1)
                pe.wait_ge(lg_read, routed)
                for s in range(SUB):
                    last = pe.transpose(tp[:, s * P:(s + 1) * P], acc[:, s * P:(s + 1) * P], ident[:, :])
                last.then_inc(out_ready, 1)

            def body(i, last):
                T0 = i * (2 * NC)
                for N in range(2 * NC + LAG):
                    q, n = N // NC, N % NC
                    if N < 2 * NC:
                        if q == 1 and n == EPI:
                            turn_back(i * 2, i * 2 + 2)
                        if not (last and q == 1):
                            if n == TURN:
                                turn_tokens(i * 2 + (q + 1))
                            if n == GATE:
                                logits(i * 2 + (q + 1), 1 - q)
                        if n % CH == 0:
                            spread_gate(i * 2 + q, q, n // CH)
                        first_products(N, T0, q, n)
                    if N >= LAG:
                        second_products(N - LAG, T0, i * (2 * E), (N - LAG) % NC)
                turn_back(i * 2 + 1, i * 2 + (2 if last else 3))

            pe.sem_inc(second_done, RING)
            pe.sem_inc(out_ready, 1)
            turn_tokens(0)
            logits(0, 0)
            with pe.Fori(0, PAIRS - 1) as i:
                body(i, False)
            body(PAIRS - 1, True)

        @block.scalar
        def _(act):
            act.sem_inc(act_done, 4)
            act.sem_inc(pb_copied, 1)

            def nonlinear(N, T0, n):
                act.wait_ge(h_ready, T0 + N + 1)
                if gelu:
                    act.wait_ge(hl_ready, T0 + N + 1)
                    act.activation(hid[:, N % RING, :], hb[N % 4][:, :], ACT.Gelu,
                                   bias=res["cols"][:, COL_B1 + n:COL_B1 + n + 1]).then_inc(act_done, 1)
                else:
                    act.activation(sil[:, N % RING, :], hb[N % 2][:, :], ACT.Silu).then_inc(act_done, 1)

            def high_half(N, T0):
                if gelu:
                    act.wait_ge(act_done, T0 + N + 1 + 4)
                else:
                    act.wait_ge(mul_done, T0 + N + 1 + 2)
                act.wait_ge(second_done, T0 + N + 1)
                act.copy(hidh[:, N % RING, :], hid[:, N % RING, :]).then_inc(hh_ready, 1)

            def copy_gate(t, e):
                act.wait_ge(pb_ready, t * E + e + 1)
                act.wait_ge(scaled, t * E + e + 1)
                act.copy(gate_b[:, e % PB_RING, :], pb[:, :]).then_inc(pb_copied, 1)

            def body(i):
                T0 = i * (2 * NC)
                for N in range(2 * NC):
                    q, n = N // NC, N % NC
                    nonlinear(N, T0, n)
                    if N >= 1:
                        high_half(N - 1, T0)
                    if n % CH == 0:
                        copy_gate(i * 2 + q, n // CH)
                high_half(2 * NC - 1, T0)

            with act.Fori(0, PAIRS) as i:
                body(i)

        @block.vector
        def _(dve):
            dve.sem_inc(hl_ready, RING)
            dve.sem_inc(scaled, PB_RING)
            dve.sem_inc(out_read, 1)
            if not gelu:
                dve.sem_inc(mul_done, 2)

            def stats(ch, t):
                for s in range(SUB):
                    last = dve.bn_stats(st[:, s, :], of_group(x, t, s))
                ch.step(last)
                ch.settle_apart()
                for s in range(SUB):
                    last = dve.bn_aggr(mv[:, s, :], st[:, s, :])
                ch.step(last)
                ch.settle()
                dve.tensor_scalar(ve[:, :], mv[:, :, 1], EPS, None, ALU.add).then_inc(pvar, 1)

            def normalise(t):
                dve.wait_ge(prstd, t + 1)
                for s in range(SUB):
                    last = dve.tensor_scalar(xn[:, s, :], of_group(x, t, s), mv[:, s, 0:1], rstd[:, s:s + 1],
                                             ALU.subtract, ALU.mult)
                last.then_inc(xn_ready, 1)

            def split_tokens(ch, t, q):
                dve.wait_ge(xt_ready, t + 1)
                ch.step(dve.tensor_copy(xTh[q][:, :], tp[:, :]))
                ch.settle()
                dve.tensor_tensor(xTl[q][:, :], tp[:, :], xTh[q][:, :].bitcast(F32), ALU.subtract).then_inc(split_done, 1)

            def route(ch, t):
                dve.wait_ge(lg_ready, t + 1)
                if gelu:
                    ins = dve.tensor_tensor(lg[:, :, :], lg_ps, res["gate_bias"][:, :].rearrange("p (a e) -> p a e", a=1)
                                            .broadcast_to([P, SUB, E]), ALU.add)
                else:
                    ins = dve.tensor_copy(lg[:, :, :], lg_ps)
                ins.then_inc(lg_read, 1)
                dve.wait_ge(lg_read, t + 1)
                dve.sem_inc(held, 1)
                for s in range(SUB):
                    last = dve.max(top[:, s, :], lg[:, s, :])
                ch.step(last)
                ch.settle()
                dve.tensor_tensor(diff[:, :], top[:, :, 1], top[:, :, 0], ALU.subtract).then_inc(diff_ready, 1)
                ch.step(dve.tensor_copy(replace[:, :, 0:2], top[:, :, 0:2]))
                ch.settle_apart()
                for s in range(SUB):
                    last = dve.match_replace(cut[:, s, :], replace[:, s, :], lg[:, s, :], -BIG)
                ch.step(last)
                ch.step(dve.tensor_tensor(first[:, :, :], lg[:, :, :], top[:, :, 0:1].broadcast_to([P, SUB, E]), ALU.is_equal))
                ch.settle()
                dve.tensor_tensor(mask[:, :, :], cut[:, :, :], lg[:, :, :], ALU.not_equal)

            def gates(ch, t, q):
                dve.wait_ge(e2_ready, t + 1)
                ch.step(dve.tensor_tensor(weight[:, :, :], first[:, :, :],
                                          e2[:, :].rearrange("p (s a) -> p s a", a=1).broadcast_to([P, SUB, E]), ALU.max))
                ch.step(dve.tensor_scalar(diff[:, :], e2[:, :], 1.0, None, ALU.add))
                ch.settle()
                dve.tensor_tensor(first[:, :, :], weight[:, :, :], mask[:, :, :], ALU.mult)
                ch.step(dve.reciprocal(den[:, :], diff[:, :]))
                ch.settle()
                dve.tensor_tensor(gate[q][:, :, :], first[:, :, :],
                                  den[:, :].rearrange("p (s a) -> p s a", a=1).broadcast_to([P, SUB, E]), ALU.mult)\
                   .then_inc(gate_ready, 1)

            def multiply(N, T0):
                dve.wait_ge(act_done, T0 + N + 1 + 4)
                dve.tensor_tensor(hid[:, N % RING, :], sil[:, N % RING, :], hb[2 + N % 2][:, :], ALU.mult).then_inc(mul_done, 1)

            def low_half(N, T0):
                dve.wait_ge(hh_ready, T0 + N + 1)
                dve.tensor_tensor(hidl[:, N % RING, :], hid[:, N % RING, :], hidh[:, N % RING, :].bitcast(F32), ALU.subtract)\
                   .then_inc(hl_ready, 1)

            def gated(t, e, T0, N):
                dve.wait_ge(second_done, T0 + N + 1 + RING)
                dve.wait_ge(pb_copied, t * E + e + 2)
                dve.wait_ge(acc_done, t * ADDS + (max(1, e - 2) if e >= 2 else 0) + 1)
                o = ob[e % 2][:, :]
                if gelu:
                    ins = dve.scalar_tensor_tensor(part[:, e % 2, :], o, res["cols"][:, COL_B2 + e:COL_B2 + e + 1],
                                                   gate_b[:, e % PB_RING, :], ALU.add, ALU.mult)
                else:
                    ins = dve.tensor_tensor(part[:, e % 2, :], o, gate_b[:, e % PB_RING, :], ALU.mult)
                ins.then_inc(scaled, 1)

            def finish_a(ch, t):
                dve.wait_ge(out_ready, t + 2)
                if not gelu:
                    xt = of_tile(x, t)
                    dve.scalar_tensor_tensor(xt, tp_s, 0.5, xt, ALU.mult, ALU.add).then_inc(out_read, 1)
                    return
                for s in range(SUB):
                    last = dve.bn_stats(st2[:, s, :], tp_s[:, s, :])
                ch.step(last)
                ch.settle_apart()
                for s in range(SUB):
                    last = dve.bn_aggr(mv2[:, s, :], st2[:, s, :])
                ch.step(last)
                ch.settle()
                dve.tensor_scalar(ve2[:, :], mv2[:, :, 1], EPS, None, ALU.add).then_inc(evar, 1)

            def finish_b(t):
                if not gelu:
                    return
                dve.wait_ge(erstd, t + 1)
                dve.wait_ge(x_done, t + 1)
                for s in range(SUB):
                    last = dve.tensor_scalar(yn[:, s, :], tp_s[:, s, :], mv2[:, s, 0:1], rstd2[:, s:s + 1],
                                             ALU.subtract, ALU.mult)
                last.then_inc(out_read, 1)

            def body(i, ch, last):
                T0 = i * (2 * NC)
                for N in range(2 * NC + SCALE_LAG):
                    q, n = N // NC, N % NC
                    if N < 2 * NC:
                        t = i * 2 + q
                        if gelu:
                            low_half(N, T0)
                        else:
                            multiply(N, T0)
                            if N >= 1:
                                low_half(N - 1, T0)
                            if N == 2 * NC - 1:
                                low_half(N, T0)
                        if not (last and q == 1):
                            if n == STATS:
                                stats(ch, t + 1)
                            if n == NORM:
                                normalise(t + 1)
                            if n == TURN:
                                split_tokens(ch, t + 1, 1 - q)
                            if n == GATE:
                                route(ch, t + 1)
                            if n == GATE + 1:
                                gates(ch, t + 1, 1 - q)
                        if q == 1 and n == EPI:
                            finish_a(ch, i * 2)
                        if q == 1 and n == EPI + 1:
                            finish_b(i * 2)
                    M = N - SCALE_LAG
                    if M >= 0 and M % CH == CH - 1:
                        gated(i * 2 + M // NC, (M % NC) // CH, T0, M)
                finish_a(ch, i * 2 + 1)
                finish_b(i * 2 + 1)

            ch = Steps(dve, chain, 0, held)
            stats(ch, 0)
            normalise(0)
            split_tokens(ch, 0, 0)
            route(ch, 0)
            gates(ch, 0, 0)
            before = ch.n
            per_body = 2 * before + (4 if gelu else 0)
            with dve.Fori(0, PAIRS - 1) as i:
                ch = Steps(dve, chain, i * per_body + before, held)
                body(i, ch, False)
                assert ch.n == per_body
            body(PAIRS - 1, Steps(dve, chain, (PAIRS - 1) * per_body + before, held), True)

        @block.gpsimd
        def _(pool):
            pool.sem_inc(acc_done, 1)
            pool.sem_inc(x_done, 1)

            def prologue_power(t):
                pool.wait_ge(pvar, t + 1)
                pool.tensor_tensor(rstd[:, :], ve[:, :], res["neg_half"][:, :], ALU.pow).then_inc(prstd, 1)

            def gate_power(t):
                pool.wait_ge(diff_ready, t + 1)
                pool.tensor_tensor(e2[:, :], base[:, :], diff[:, :], ALU.pow).then_inc(e2_ready, 1)

            def sums(t, e):
                pool.wait_ge(scaled, t * E + e + 1 + PB_RING)
                if e == 1:
                    pool.wait_ge(out_ready, t + 1)
                else:
                    pool.wait_ge(acc_done, t * ADDS + e)
                pool.tensor_tensor(acc[:, :], part[:, 0, :] if e == 1 else acc[:, :], part[:, e % 2, :], ALU.add)\
                    .then_inc(acc_done, 1)

            def finish(t):
                if not gelu:
                    return
                pool.wait_ge(evar, t + 1)
                pool.tensor_tensor(rstd2[:, :], ve2[:, :], res["neg_half"][:, :], ALU.pow).then_inc(erstd, 1)
                pool.wait_ge(out_read, t + 2)
                wide = lambda n: res[n][:, :].rearrange("p (a d) -> p a d", a=1).broadcast_to([P, SUB, D])
                pool.tensor_tensor(yn[:, :, :], yn[:, :, :], wide("post_g"), ALU.mult).then_inc(yn_ready, 1)
                pool.wait_ge(yn_ready, t * 2 + 1)
                pool.tensor_tensor(yn[:, :, :], yn[:, :, :], wide("post_b"), ALU.add).then_inc(yn_ready, 1)
                pool.wait_ge(yn_ready, t * 2 + 2)
                xt = of_tile(x, t)
                pool.tensor_tensor(xt, xt, yn[:, :, :], ALU.add).then_inc(x_done, 1)

            def body(i, last):
                for q in range(2):
                    t = i * 2 + q
                    if not (last and q == 1):
                        prologue_power(t + 1)
                    if q == 1:
                        finish(i * 2)
                    for e in range(1, E):
                        if e == GATE_E and not (last and q == 1):
                            gate_power(t + 1)
                        sums(t, e)
                finish(i * 2 + 1)

            prologue_power(0)
            gate_power(0)
            with pool.Fori(0, PAIRS - 1) as i:
                body(i, False)
            body(PAIRS - 1, True)


def state_space(nc, x, res, ident):
    STEPS_OF_TIME = SEQ // TILE
    col = lambda n: res["cols"][:, COL[n]:COL[n] + 1]
    w = lambda n: res["sqT"][:, SQ[n], :]
    with ExitStack() as ctx:
        L = Layer(nc, ctx, "ssm")
        per_batch = lambda n, shape=(P, TILE): [L.sb(f"{n}{b}", list(shape)) for b in range(NB)]
        xn = per_batch("xn", (P, SUB, D))
        xT, u, sg, ab, dt, nbt = (per_batch(n) for n in ("xT", "u", "sg", "ab", "dt", "nbt"))
        h = ab
        carry = per_batch("carry", (P, 1))
        st, mv, ve, rstd = per_batch("st", (P, SUB, 6)), per_batch("mv", (P, SUB, 2)), per_batch("ve", (P, SUB)), per_batch("rstd", (P, SUB))
        bank_a = [L.bank(f"bank_a{b}") for b in range(NB)]
        bank_b = [L.bank(f"bank_b{b}") for b in range(NB)]
        names = ("var_ready", "rstd_ready", "xn_ready", "xt_ps", "xt_ready", "ug_ready", "u_ready", "tanh_done", "sg_done",
                 "dt_ready", "bt_ready", "abs_done", "exp_done", "ln_done", "max_done", "dt_done", "decay_done",
                 "scan_done", "y_ready", "gated", "z_ready", "out_ready", "chain", "held")
        (var_ready, rstd_ready, xn_ready, xt_ps, xt_ready, ug_ready, u_ready, tanh_done, sg_done, dt_ready, bt_ready,
         abs_done, exp_done, ln_done, max_done, dt_done, decay_done, scan_done, y_ready, gated, z_ready, out_ready,
         chain, held) = (L.sem(n) for n in names)
        block = ctx.enter_context(nc.Block())

        @block.tensor
        def _(pe):
            with pe.Fori(0, STEPS_OF_TIME) as k:
                c = k * NB
                for b in range(NB):
                    pe.wait_ge(xn_ready, c + b + 1)
                    for s in range(SUB):
                        last = pe.transpose(bank_a[b][:, s * P:(s + 1) * P], xn[b][:, s, :], ident[:, :])
                    last.then_inc(xt_ps, 1)
                for b in range(NB):
                    pe.wait_ge(xt_ready, c + b + 1)
                    pe.matmul(bank_a[b][:, :], w("Wu"), xT[b][:, :], start=True, stop=True)
                    pe.matmul(bank_b[b][:, :], w("Wgate"), xT[b][:, :], start=True, stop=True).then_inc(ug_ready, 1)
                for b in range(NB):
                    pe.wait_ge(u_ready, c + b + 1)
                    pe.matmul(bank_a[b][:, :], w("Wdt"), u[b][:, :], start=True, stop=True).then_inc(dt_ready, 1)
                    pe.wait_ge(sg_done, c + b + 1)
                    pe.matmul(bank_b[b][:, :], w("Wstate"), u[b][:, :], start=True, stop=True).then_inc(bt_ready, 1)
                for b in range(NB):
                    pe.wait_ge(scan_done, c + b + 1)
                    pe.matmul(bank_a[b][:, :], w("WC"), h[b][:, :], start=True, stop=True).then_inc(y_ready, 1)
                for b in range(NB):
                    pe.wait_ge(z_ready, c + b + 1)
                    for s in range(SUB):
                        last = pe.matmul(bank_b[b][:, s * P:(s + 1) * P], sg[b][:, s * P:(s + 1) * P], w("Wout"), start=True, stop=True)
                    last.then_inc(out_ready, 1)

        @block.scalar
        def _(act):
            with act.Fori(0, STEPS_OF_TIME) as k:
                c = k * NB
                for b in range(NB):
                    act.wait_ge(xt_ps, c + b + 1)
                    act.copy(xT[b][:, :], bank_a[b][:, :]).then_inc(xt_ready, 1)
                for b in range(NB):
                    act.wait_ge(ug_ready, c + b + 1)
                    act.copy(u[b][:, :], bank_a[b][:, :]).then_inc(u_ready, 1)
                    act.activation(sg[b][:, :], bank_b[b][:, :], ACT.Tanh, scale=0.5).then_inc(tanh_done, 1)
                for b in range(NB):
                    act.wait_ge(dt_ready, c + b + 1)
                    act.activation(ab[b][:, :], bank_a[b][:, :], ACT.Abs, bias=col("L0_attn_b_dt")).then_inc(abs_done, 1)
                for b in range(NB):
                    act.wait_ge(abs_done, c + b + 1)
                    act.activation(ab[b][:, :], ab[b][:, :], ACT.Exp, scale=-1.0).then_inc(exp_done, 1)
                for b in range(NB):
                    act.wait_ge(exp_done, c + b + 1)
                    act.activation(ab[b][:, :], ab[b][:, :], ACT.Ln, bias=1.0).then_inc(ln_done, 1)
                for b in range(NB):
                    act.wait_ge(dt_done, c + b + 1)
                    act.activation(dt[b][:, :], dt[b][:, :], ACT.Exp, scale=res["neg_rate"][:, 0:1]).then_inc(decay_done, 1)

        @block.vector
        def _(dve):
            for b in range(NB):
                last = dve.memset(carry[b][:, :], 0.0)
            last.then_inc(chain, 1)
            CHAIN = 5 * NB
            with dve.Fori(0, STEPS_OF_TIME) as k:
                c = k * NB
                ch = Steps(dve, chain, k * CHAIN + 1, held)
                for b in range(NB):
                    for s in range(SUB):
                        last = dve.bn_stats(st[b][:, s, :], of_group(x, k + b * STEPS_OF_TIME, s))
                    ch.step(last)
                ch.settle_apart()
                for b in range(NB):
                    for s in range(SUB):
                        last = dve.bn_aggr(mv[b][:, s, :], st[b][:, s, :])
                    ch.step(last)
                ch.settle()
                for b in range(NB):
                    dve.tensor_scalar(ve[b][:, :], mv[b][:, :, 1], EPS, None, ALU.add).then_inc(var_ready, 1)
                for b in range(NB):
                    dve.wait_ge(rstd_ready, c + b + 1)
                    for s in range(SUB):
                        last = dve.tensor_scalar(xn[b][:, s, :], of_group(x, k + b * STEPS_OF_TIME, s), mv[b][:, s, 0:1],
                                                 rstd[b][:, s:s + 1], ALU.subtract, ALU.mult)
                    last.then_inc(xn_ready, 1)
                for b in range(NB):
                    dve.wait_ge(tanh_done, c + b + 1)
                    dve.scalar_tensor_tensor(sg[b][:, :], sg[b][:, :], 1.0, bank_b[b][:, :], ALU.add, ALU.mult).then_inc(sg_done, 1)
                for b in range(NB):
                    dve.wait_ge(dt_ready, c + b + 1)
                    dve.wait_ge(abs_done, c + b + 1)
                    dve.tensor_scalar(dt[b][:, :], bank_a[b][:, :], col("L0_attn_b_dt"), 0.0, ALU.add, ALU.max).then_inc(max_done, 1)
                for b in range(NB):
                    dve.wait_ge(ln_done, c + b + 1)
                    dve.wait_ge(max_done, c + b + 1)
                    dve.tensor_tensor(dt[b][:, :], dt[b][:, :], ab[b][:, :], ALU.add).then_inc(dt_done, 1)
                for b in range(NB):
                    dve.wait_ge(decay_done, c + b + 1)
                    ch.step(dve.tensor_scalar(dt[b][:, :], dt[b][:, :], res["floor"][:, 0:1], 1.0, ALU.max, ALU.min))
                for b in range(NB):
                    dve.wait_ge(bt_ready, c + b + 1)
                    ch.settle()
                    ch.step(dve.scalar_tensor_tensor(nbt[b][:, :], dt[b][:, :], 1.0, bank_b[b][:, :], ALU.subtract, ALU.mult))
                for b in range(NB):
                    ch.settle()
                    dve.tensor_tensor_scan(h[b][:, :], dt[b][:, :], nbt[b][:, :], carry[b][:, 0:1], ALU.mult, ALU.subtract)\
                        .then_inc(scan_done, 1)
                for b in range(NB):
                    dve.wait_ge(scan_done, c + b + 1)
                    ch.step(dve.tensor_copy(carry[b][:, :], h[b][:, TILE - 1:TILE]))
                for b in range(NB):
                    dve.wait_ge(y_ready, c + b + 1)
                    dve.scalar_tensor_tensor(sg[b][:, :], bank_a[b][:, :], 0.5, sg[b][:, :], ALU.mult, ALU.mult).then_inc(gated, 1)
                for b in range(NB):
                    dve.wait_ge(gated, c + b + 1)
                    dve.scalar_tensor_tensor(sg[b][:, :], xT[b][:, :], col("L0_attn_D"), sg[b][:, :], ALU.mult, ALU.add)\
                        .then_inc(z_ready, 1)
                for b in range(NB):
                    dve.wait_ge(out_ready, c + b + 1)
                    xt = of_tile(x, k + b * STEPS_OF_TIME)
                    dve.tensor_tensor(xt, xt, bank_b[b][:, :].rearrange("p (s d) -> p s d", s=SUB), ALU.add)
                assert ch.n == CHAIN

        @block.gpsimd
        def _(pool):
            with pool.Fori(0, STEPS_OF_TIME) as k:
                for b in range(NB):
                    pool.wait_ge(var_ready, k * NB + b + 1)
                    pool.tensor_tensor(rstd[b][:, :], ve[b][:, :], res["neg_half"][:, :], ALU.pow).then_inc(rstd_ready, 1)


def receptance(nc, x, res, ident, block_diag):
    STEPS_OF_TIME = SEQ // TILE
    col = lambda n: res["cols"][:, COL[n]:COL[n] + 1]
    w = lambda n: res["sqT"][:, SQ[n], :]
    with ExitStack() as ctx:
        L = Layer(nc, ctx, "rwkv")
        per_batch = lambda n, shape=(P, TILE): [L.sb(f"{n}{b}", list(shape)) for b in range(NB)]
        xn = per_batch("xn", (P, SUB, D))
        xT = per_batch("xT", (P, TILE + 1))
        dx, lx = per_batch("dx"), per_batch("lx")
        tw = per_batch("tw", (P, 3, TILE + 1))
        q = {p: per_batch("q" + p) for p in LORAS}
        v = per_batch("v")
        carry = per_batch("carry", (P, HD))
        st, mv, ve, rstd = per_batch("st", (P, SUB, 6)), per_batch("mv", (P, SUB, 2)), per_batch("ve", (P, SUB)), per_batch("rstd", (P, SUB))
        bank_a = [L.bank(f"bank_a{b}") for b in range(NB)]
        bank_b = [L.bank(f"bank_b{b}") for b in range(NB)]
        S = {}
        for n in ("var_ready", "rstd_ready", "xn_ready", "xt_ps", "xt_ready", "dx_ready", "lx_ready", "la_rk", "la_vg", "la_d",
                  "tanh_rk", "tanh_vg", "tanh_d", "lb_ready", "scaled", "xin_ready", "proj_ready", "copied", "tanh_g", "sg_done",
                  "la_d2", "tanh_d2", "lb_d2", "exp1", "w_ready", "ruk_done", "bonus_ps", "bonus_done",
                  "ve_ready", "kv_done", "scan_done", "carried", "m_done", "sum_done", "y_done", "centred", "squared", "var_ps",
                  "ln_done", "rs_done", "normed", "shifted", "o_ready", "out_ready", "chain", "held", "acts"):
            S[n] = L.sem(n)
        block = ctx.enter_context(nc.Block())
        NP = len(LORAS)
        mid = lambda b: xT[b][:, 1:TILE + 1]
        y = [xn[b][:, :, :].rearrange("p s d -> p (s d)") for b in range(NB)]
        T = lambda b, k: tw[b][:, k, 0:TILE]

        @block.tensor
        def _(pe):
            with pe.Fori(0, STEPS_OF_TIME) as k:
                c = k * NB
                for b in range(NB):
                    pe.wait_ge(S["xn_ready"], c + b + 1)
                    for s in range(SUB):
                        last = pe.transpose(bank_a[b][:, s * P:(s + 1) * P], xn[b][:, s, :], ident[:, :])
                    last.then_inc(S["xt_ps"], 1)
                for b in range(NB):
                    pe.wait_ge(S["lx_ready"], c + b + 1)
                    pe.matmul(bank_a[b][:, :], res["laT"][:, 0, :], lx[b][:, :], start=True, stop=True).then_inc(S["la_rk"], 1)
                    pe.matmul(bank_b[b][:, :], res["laT"][:, 1, :], lx[b][:, :], start=True, stop=True).then_inc(S["la_vg"], 1)
                for b in range(NB):
                    pe.wait_ge(S["tanh_rk"], c + b + 1)
                    pe.matmul(bank_a[b][0:LORA, :], res["laT"][:, 2, 0:LORA], lx[b][:, :], start=True, stop=True).then_inc(S["la_d"], 1)

                def expand(n, p):
                    pair, half = LA[p]
                    rows = slice(half * LORA, (half + 1) * LORA)
                    for b in range(NB):
                        if n == 0:
                            pe.wait_ge(S["tanh_d"], c + b + 1)
                        else:
                            pe.wait_ge(S["scaled"], k * (NP * NB) + (n - 1) * NB + b + 1)
                        pe.matmul(bank_a[b][:, :], res["lbT"][rows, pair, :], tw[b][rows, pair, 0:TILE], start=True, stop=True)\
                            .then_inc(S["lb_ready"], 1)

                def project(n, p):
                    for b in range(NB):
                        pe.wait_ge(S["xin_ready"], k * (NP * NB) + n * NB + b + 1)
                        if n == 0:
                            pe.wait_ge(S["tanh_vg"], c + b + 1)
                        else:
                            pe.wait_ge(S["copied"], k * (3 * NB) + (n - 1) * NB + b + 1)
                        pe.matmul(bank_b[b][:, :], w(p + "W"), q[p][b][:, :], start=True, stop=True).then_inc(S["proj_ready"], 1)

                for n, p in enumerate(LORAS):
                    expand(n, p)
                    if n >= 1:
                        project(n - 1, LORAS[n - 1])
                for b in range(NB):
                    pe.wait_ge(S["xin_ready"], k * (NP * NB) + 4 * NB + b + 1)
                    pe.matmul(bank_a[b][0:LORA, :], res["laT"][:, 2, 0:LORA], q["d"][b][:, :], start=True, stop=True).then_inc(S["la_d2"], 1)
                for b in range(NB):
                    pe.wait_ge(S["tanh_d2"], c + b + 1)
                    pe.wait_ge(S["sg_done"], c + b + 1)
                    pe.matmul(bank_b[b][:, :], res["lbT"][0:LORA, 2, :], tw[b][0:LORA, 2, 0:TILE], start=True, stop=True).then_inc(S["lb_d2"], 1)
                for b in range(NB):
                    pe.wait_ge(S["ruk_done"], c + b + 1)
                    pe.matmul(bank_a[b][:, :], block_diag[:, :], lx[b][:, :], start=True, stop=True).then_inc(S["bonus_ps"], 1)

                def values(j):
                    for b in range(NB):
                        if j == 0:
                            pe.wait_ge(S["bonus_done"], c + b + 1)
                        else:
                            pe.wait_ge(S["kv_done"], k * (HD * NB) + (j - 1) * NB + b + 1)
                        pe.matmul(bank_a[b][:, :], res["v_each"][:, j, :], q["v"][b][:, :], start=True, stop=True).then_inc(S["ve_ready"], 1)

                def head_sums(j):
                    for b in range(NB):
                        pe.wait_ge(S["m_done"], k * (HD * NB) + j * NB + b + 1)
                        pe.matmul(bank_b[b][:, :], res["sel"][:, j, :], T(b, 2), start=j == 0, stop=j == HD - 1).then_inc(S["sum_done"], 1)

                for j in range(HD):
                    values(j)
                    if j >= 1:
                        head_sums(j - 1)
                head_sums(HD - 1)
                for b in range(NB):
                    pe.wait_ge(S["y_done"], c + b + 1)
                    pe.matmul(bank_a[b][:, :], res["head_centre"][:, :], y[b], start=True, stop=True).then_inc(S["centred"], 1)
                for b in range(NB):
                    pe.wait_ge(S["squared"], c + b + 1)
                    pe.matmul(bank_b[b][:, :], res["head_mean"][:, :], lx[b][:, :], start=True, stop=True).then_inc(S["var_ps"], 1)
                for b in range(NB):
                    pe.wait_ge(S["o_ready"], c + b + 1)
                    for s in range(SUB):
                        last = pe.matmul(bank_b[b][:, s * P:(s + 1) * P], y[b][:, s * P:(s + 1) * P], w("oW"), start=True, stop=True)
                    last.then_inc(S["out_ready"], 1)

        @block.scalar
        def _(act):
            for b in range(NB):
                last = act.activation(xT[b][:, TILE:TILE + 1], ident[:, 0:1], ACT.Copy, scale=0.0)
            last.then_inc(S["acts"], 1)
            act.wait_ge(S["acts"], 1)
            with act.Fori(0, STEPS_OF_TIME) as k:
                c = k * NB
                for b in range(NB):
                    act.wait_ge(S["xt_ps"], c + b + 1)
                    act.copy(xT[b][:, 0:1], xT[b][:, TILE:TILE + 1]).then_inc(S["acts"], 1)
                for b in range(NB):
                    act.wait_ge(S["acts"], c + b + 2)
                    act.copy(mid(b), bank_a[b][:, :]).then_inc(S["xt_ready"], 1)
                for b in range(NB):
                    act.wait_ge(S["la_rk"], c + b + 1)
                    act.activation(T(b, 0), bank_a[b][:, :], ACT.Tanh).then_inc(S["tanh_rk"], 1)
                    act.wait_ge(S["la_vg"], c + b + 1)
                    act.activation(T(b, 1), bank_b[b][:, :], ACT.Tanh).then_inc(S["tanh_vg"], 1)
                for b in range(NB):
                    act.wait_ge(S["la_d"], c + b + 1)
                    act.activation(tw[b][0:LORA, 2, 0:TILE], bank_a[b][0:LORA, :], ACT.Tanh).then_inc(S["tanh_d"], 1)
                for n, p in enumerate("rkv"):
                    for b in range(NB):
                        act.wait_ge(S["proj_ready"], k * (4 * NB) + n * NB + b + 1)
                        act.copy({"r": q["r"], "k": q["k"], "v": v}[p][b][:, :], bank_b[b][:, :]).then_inc(S["copied"], 1)
                for b in range(NB):
                    act.wait_ge(S["proj_ready"], k * (4 * NB) + 3 * NB + b + 1)
                    act.activation(q["g"][b][:, :], bank_b[b][:, :], ACT.Tanh, scale=0.5).then_inc(S["tanh_g"], 1)
                for b in range(NB):
                    act.wait_ge(S["la_d2"], c + b + 1)
                    act.activation(tw[b][0:LORA, 2, 0:TILE], bank_a[b][0:LORA, :], ACT.Tanh).then_inc(S["tanh_d2"], 1)
                for b in range(NB):
                    act.wait_ge(S["lb_d2"], c + b + 1)
                    act.activation(q["d"][b][:, :], bank_b[b][:, :], ACT.Exp, bias=col("L1_attn_d_ll")).then_inc(S["exp1"], 1)
                for b in range(NB):
                    act.wait_ge(S["exp1"], c + b + 1)
                    act.activation(q["d"][b][:, :], q["d"][b][:, :], ACT.Exp, scale=-1.0).then_inc(S["w_ready"], 1)
                for b in range(NB):
                    act.wait_ge(S["centred"], c + b + 1)
                    act.activation(lx[b][:, :], bank_a[b][:, :], ACT.Square).then_inc(S["squared"], 1)
                for b in range(NB):
                    act.wait_ge(S["var_ps"], c + b + 1)
                    act.activation(lx[b][:, :], bank_b[b][:, :], ACT.Ln, bias=res["eps"][:, 0:1]).then_inc(S["ln_done"], 1)
                for b in range(NB):
                    act.wait_ge(S["ln_done"], c + b + 1)
                    act.activation(lx[b][:, :], lx[b][:, :], ACT.Exp, scale=-0.5).then_inc(S["rs_done"], 1)

        @block.vector
        def _(dve):
            for b in range(NB):
                last = dve.tensor_copy(carry[b][:, :], res["state0"][:, :])
            last.then_inc(S["chain"], 1)
            CHAIN = (2 + HD) * NB
            with dve.Fori(0, STEPS_OF_TIME) as k:
                c = k * NB
                ch = Steps(dve, S["chain"], k * CHAIN + 1, S["held"])
                for b in range(NB):
                    for s in range(SUB):
                        last = dve.bn_stats(st[b][:, s, :], of_group(x, k + b * STEPS_OF_TIME, s))
                    ch.step(last)
                ch.settle_apart()
                for b in range(NB):
                    for s in range(SUB):
                        last = dve.bn_aggr(mv[b][:, s, :], st[b][:, s, :])
                    ch.step(last)
                ch.settle()
                for b in range(NB):
                    dve.tensor_scalar(ve[b][:, :], mv[b][:, :, 1], EPS, None, ALU.add).then_inc(S["var_ready"], 1)
                for b in range(NB):
                    dve.wait_ge(S["rstd_ready"], c + b + 1)
                    for s in range(SUB):
                        last = dve.tensor_scalar(xn[b][:, s, :], of_group(x, k + b * STEPS_OF_TIME, s), mv[b][:, s, 0:1],
                                                 rstd[b][:, s:s + 1], ALU.subtract, ALU.mult)
                    last.then_inc(S["xn_ready"], 1)
                for b in range(NB):
                    dve.wait_ge(S["xt_ready"], c + b + 1)
                    dve.tensor_tensor(dx[b][:, :], xT[b][:, 0:TILE], mid(b), ALU.subtract).then_inc(S["dx_ready"], 1)
                for b in range(NB):
                    dve.wait_ge(S["dx_ready"], c + b + 1)
                    dve.scalar_tensor_tensor(lx[b][:, :], dx[b][:, :], col("L1_attn_xw"), mid(b), ALU.mult, ALU.add).then_inc(S["lx_ready"], 1)

                def mix(n, p):
                    for b in range(NB):
                        dve.wait_ge(S["lb_ready"], k * (NP * NB) + n * NB + b + 1)
                        dve.scalar_tensor_tensor(q[p][b][:, :], bank_a[b][:, :], col(f"L1_attn_{p}_ll"), dx[b][:, :], ALU.add, ALU.mult)\
                            .then_inc(S["scaled"], 1)

                for n, p in enumerate(LORAS):
                    mix(n, p)
                    if n == 4:
                        for b in range(NB):
                            dve.wait_ge(S["copied"], k * (3 * NB) + 2 * NB + b + 1)
                            dve.scalar_tensor_tensor(lx[b][:, :], q["r"][b][:, :], col("L1_attn_u"), q["k"][b][:, :], ALU.mult, ALU.mult)\
                                .then_inc(S["ruk_done"], 1)
                for b in range(NB):
                    dve.wait_ge(S["tanh_g"], c + b + 1)
                    dve.scalar_tensor_tensor(q["g"][b][:, :], q["g"][b][:, :], 1.0, bank_b[b][:, :], ALU.add, ALU.mult).then_inc(S["sg_done"], 1)
                for b in range(NB):
                    dve.wait_ge(S["bonus_ps"], c + b + 1)
                    dve.tensor_tensor(v[b][:, :], v[b][:, :], bank_a[b][:, :], ALU.mult).then_inc(S["bonus_done"], 1)
                for j in range(HD):
                    n = k * (HD * NB) + j * NB
                    for b in range(NB):
                        dve.wait_ge(S["ve_ready"], n + b + 1)
                        dve.tensor_tensor(dx[b][:, :], q["k"][b][:, :], bank_a[b][:, :], ALU.mult).then_inc(S["kv_done"], 1)
                        if j >= 2:
                            dve.wait_ge(S["m_done"], k * (HD * NB) + (j - 2) * NB + b + 1)
                        ch.step(dve.tensor_copy(tw[b][:, j % 2, 0:1], carry[b][:, j:j + 1]))
                    for b in range(NB):
                        if j == 0:
                            dve.wait_ge(S["w_ready"], c + b + 1)
                        dve.wait_ge(S["kv_done"], n + b + 1)
                        dve.tensor_tensor_scan(tw[b][:, j % 2, 1:TILE + 1], q["d"][b][:, :], dx[b][:, :], carry[b][:, j:j + 1],
                                               ALU.mult, ALU.add).then_inc(S["scan_done"], 1)
                    for b in range(NB):
                        dve.wait_ge(S["scan_done"], n + b + 1)
                        dve.tensor_copy(carry[b][:, j:j + 1], tw[b][:, j % 2, TILE:TILE + 1]).then_inc(S["carried"], 1)
                for b in range(NB):
                    dve.wait_ge(S["sum_done"], k * (HD * NB) + (HD - 1) * NB + b + 1)
                    dve.tensor_tensor(y[b], bank_b[b][:, :], v[b][:, :], ALU.add).then_inc(S["y_done"], 1)
                for b in range(NB):
                    dve.wait_ge(S["rs_done"], c + b + 1)
                    dve.tensor_tensor(y[b], bank_a[b][:, :], lx[b][:, :], ALU.mult).then_inc(S["normed"], 1)
                for b in range(NB):
                    dve.wait_ge(S["normed"], c + b + 1)
                    dve.tensor_scalar(y[b], y[b], res["cols"][:, COL_LNW:COL_LNW + 1], res["cols"][:, COL_LNB:COL_LNB + 1],
                                      ALU.mult, ALU.add).then_inc(S["shifted"], 1)
                for b in range(NB):
                    dve.wait_ge(S["shifted"], c + b + 1)
                    dve.scalar_tensor_tensor(y[b], q["g"][b][:, :], 0.5, y[b], ALU.mult, ALU.mult).then_inc(S["o_ready"], 1)
                for b in range(NB):
                    dve.wait_ge(S["out_ready"], c + b + 1)
                    xt = of_tile(x, k + b * STEPS_OF_TIME)
                    dve.tensor_tensor(xt, xt, bank_b[b][:, :].rearrange("p (s d) -> p s d", s=SUB), ALU.add)
                assert ch.n == CHAIN

        @block.gpsimd
        def _(pool):
            with pool.Fori(0, STEPS_OF_TIME) as k:
                for b in range(NB):
                    pool.wait_ge(S["var_ready"], k * NB + b + 1)
                    pool.tensor_tensor(rstd[b][:, :], ve[b][:, :], res["neg_half"][:, :], ALU.pow).then_inc(S["rstd_ready"], 1)
                for n, p in enumerate(LORAS):
                    for b in range(NB):
                        pool.wait_ge(S["scaled"], k * (NP * NB) + n * NB + b + 1)
                        pool.tensor_tensor(q[p][b][:, :], q[p][b][:, :], mid(b), ALU.add).then_inc(S["xin_ready"], 1)
                for j in range(HD):
                    n = k * (HD * NB) + j * NB
                    for b in range(NB):
                        pool.wait_ge(S["scan_done"], n + b + 1)
                        if j >= 1:
                            pool.wait_ge(S["sum_done"], k * (HD * NB) + (j - 1) * NB + b + 1)
                        pool.tensor_tensor(T(b, 2), tw[b][:, j % 2, 0:TILE], q["r"][b][:, :], ALU.mult).then_inc(S["m_done"], 1)


def store(nc, x, out):
    with ExitStack() as ctx:
        stored = Layer(nc, ctx, "store").sem("stored")
        block = ctx.enter_context(nc.Block())

        @block.sync
        def _(sp):
            sp.dma_start(out.rearrange("b (g p) d -> p (b g) d", p=P), x[:, :, :]).then_inc(stored, 16)
            sp.wait_ge(stored, 16)


def build(nc, ins, out, layers=6):
    with ExitStack() as ctx:
        def sb(name, shape, dt=F32):
            return ctx.enter_context(nc.sbuf_tensor(name, shape, dt))

        x = sb("x", [P, NT * SUB, D])
        ident = sb("ident", [P, P])
        block_diag = sb("block_diag", [P, P])
        res = {}
        for n, shape in (("cols", [P, COLS]), ("sqT", [P, len(SQUARES), P]), ("laT", [P, 3, P]), ("lbT", [P, 3, P]),
                         ("v_each", [P, HD, P]), ("sel", [P, HD, P]), ("head_mean", [P, P]), ("head_centre", [P, P]),
                         ("state0", [P, HD]), ("neg_rate", [P, 1]), ("floor", [P, 1]), ("eps", [P, 1]), ("neg_half", [P, SUB]),
                         ("e_temp", [P, SUB]), ("e_one", [P, SUB]), ("replace", [P, SUB, 8]), ("gate_bias", [P, E]),
                         ("post_g", [P, D]), ("post_b", [P, D])):
            res[n] = sb(n, shape)
        for n in ("gate0h", "gate0l", "gate1h", "gate1l"):
            res[n] = sb(n, [P, E], F32R)
        for n in ("s1h", "s1l", "s3h", "s3l", "s2h", "s2l"):
            res[n] = sb(n, [P, E * FI], F32R)
        with ExitStack() as first:
            for n in ("w1h", "w1l"):
                res[n] = first.enter_context(nc.sbuf_tensor(n, [P, E, FF], F32R))
            for n in ("w2h", "w2l"):
                res[n] = first.enter_context(nc.sbuf_tensor(n, [P, E * FF // P, D], F32R))
            setup(nc, ins, x, res, ident, block_diag)
            rates(nc, res)
            if layers > 0:
                mixture(nc, "gelu0", "gelu", x, res, ident)
            if layers > 1:
                state_space(nc, x, res, ident)
            if layers > 2:
                mixture(nc, "gelu1", "gelu", x, res, ident)
        if layers > 3:
            mixture(nc, "swiglu0", "swiglu", x, res, ident)
        if layers > 4:
            receptance(nc, x, res, ident, block_diag)
        if layers > 5:
            mixture(nc, "swiglu1", "swiglu", x, res, ident)
        store(nc, x, out)


_INS = ["L0_attn_x", "L0_attn_W_in", "L0_attn_W_state", "L0_attn_W_dt", "L0_attn_b_dt", "L0_attn_A_log", "L0_attn_W_C",
        "L0_attn_D", "L0_attn_W_out", "L0_ffn_gate_w", "L0_ffn_gate_b", "L0_ffn_w1", "L0_ffn_b1", "L0_ffn_w2", "L0_ffn_b2",
        "L0_ffn_ln_g", "L0_ffn_ln_b", "L1_attn_xw", "L1_attn_rW", "L1_attn_kW", "L1_attn_vW", "L1_attn_gW",
        "L1_attn_r_la", "L1_attn_r_lb", "L1_attn_r_ll", "L1_attn_k_la", "L1_attn_k_lb", "L1_attn_k_ll",
        "L1_attn_v_la", "L1_attn_v_lb", "L1_attn_v_ll", "L1_attn_g_la", "L1_attn_g_lb", "L1_attn_g_ll",
        "L1_attn_d_la", "L1_attn_d_lb", "L1_attn_d_ll", "L1_attn_ln_w", "L1_attn_ln_b", "L1_attn_oW",
        "L1_attn_init_state", "L1_attn_u", "L1_ffn_wg", "L1_ffn_w1", "L1_ffn_w3", "L1_ffn_w2"]


def kernel(**inputs):
    import numpy as _np
    import concourse.bacc as _bacc
    from concourse import mybir as _mybir
    from concourse.bass_utils import run_bass_kernel_spmd as _run

    nc = _bacc.Bacc("TRN2", target_bir_lowering=False, num_devices=1)
    arrays, aps = {}, {}
    given = {n: _np.ascontiguousarray(inputs[n]) for n in _INS}
    given["const_ident"] = _np.eye(P, dtype=_np.float32)
    given["const_block"] = _np.kron(_np.eye(HEADS, dtype=_np.float32), _np.ones((HD, HD), _np.float32))
    for n, a in given.items():
        arrays[f"in_{n}"] = a
        aps[n] = nc.dram_tensor(f"in_{n}", a.shape, _mybir.dt.from_np(a.dtype), kind="ExternalInput").ap()
    out = nc.dram_tensor("out_x", (NB, SEQ, D), F32, kind="ExternalOutput").ap()
    build(nc, aps, out)
    r = _run(nc, [arrays], core_ids=[0])
    return r.results[0]["out_x"]
```

```python
from contextlib import ExitStack

import concourse.bass as bass
from concourse import mybir

F32 = mybir.dt.float32
F32R = mybir.dt.float32r
I32 = mybir.dt.int32
AX = mybir.AxisListType
ALU = mybir.AluOpType
ACT = mybir.ActivationFunctionType

P = 128
D = 128
NB, SEQ = 4, 1024
TOK = NB * SEQ
TILE = 512
SUB = TILE // P
NT = TOK // TILE
PAIRS = NT // 2
E = 8
FF = 512
FI = 256
WIDE = FF + FF // P
assert 2 * FI == FF
HEADS, HD = 16, 8
LORA = 64
EPS = 1e-5
TEMP = 0.9
DT_MAX = 10.0
RATE_EPS = 1e-4
BIG = 3.0e38
TOP = 2
GROUPS = TOK // P
PARTS_OF = {"gelu": (4, 12, 12, 4), "swiglu": (8, 12, 8, 4)}
PARTS = 4
EARLY = 2
MOST = max(max(groups) for groups in PARTS_OF.values())
BODY = 4
UNROLL = 2


def tiles_of(groups):
    tiles = [(g * P * TOP + E * (P - 1)) // P for g in groups]
    tiles[-1] += -sum(tiles) % BODY
    return tiles


PLACES = P * max(sum(tiles_of(groups)) for groups in PARTS_OF.values())
MOST_TILES = max(max(tiles_of(groups)) for groups in PARTS_OF.values())
LO_ROW = 32

VECTORS = ["L0_attn_b_dt", "L0_attn_A_log", "L0_attn_D", "L1_attn_xw", "L1_attn_r_ll", "L1_attn_k_ll",
           "L1_attn_v_ll", "L1_attn_g_ll", "L1_attn_d_ll", "L1_attn_u"]
COL = {n: i for i, n in enumerate(VECTORS)}
COL_WG = len(VECTORS)
COL_LNW = COL_WG + E
COL_LNB = COL_LNW + 1
COLS = COL_LNB + 1

SQUARES = ["Wu", "Wgate", "Wstate", "Wdt", "WC", "Wout", "rW", "kW", "vW", "gW", "oW"]
LORAS = "rkvgd"
SQ = {n: i for i, n in enumerate(SQUARES)}
LA = {"r": (0, 0), "k": (0, 1), "v": (1, 0), "g": (1, 1), "d": (2, 0)}


class Steps:

    def __init__(self, eng, sem, before, held=None):
        self.eng, self.sem, self.before, self.held, self.n = eng, sem, before, held, 0

    def step(self, ins):
        ins.then_inc(self.sem, 1)
        self.n += 1

    def settle(self):
        self.eng.wait_ge(self.sem, self.before + self.n)

    def settle_apart(self):
        self.settle()
        self.eng.sem_inc(self.held, 1)


class Layer:

    def __init__(self, nc, ctx, name):
        self.nc, self.ctx, self.name, self.sems = nc, ctx, name, []
        ctx.callback(self.clear)

    def sb(self, name, shape, dt=F32):
        return self.ctx.enter_context(self.nc.sbuf_tensor(f"{self.name}_{name}", shape, dt))

    def bank(self, name):
        return self.ctx.enter_context(self.nc.psum_tensor(f"{self.name}_{name}", [P, TILE], F32))

    def sem(self, name):
        self.sems.append(self.nc.alloc_semaphore(name=f"{self.name}_{name}"))
        return self.sems[-1]

    def clear(self):
        self.nc.clear_and_free_semaphores(self.sems)
        self.nc.all_engine_barrier()


def row(ap):
    return ap.rearrange("(a n) -> a n", a=1)


def of_tile(x, t):
    return x[:, bass.ds(t * SUB, SUB), :]


def of_group(x, t, s):
    return x[:, bass.ds(t * SUB + s, 1), :].rearrange("p a d -> p (a d)")


def setup(nc, ins, x, res, ident, block_diag, slots_x, later):
    with ExitStack() as ctx:
        L = Layer(nc, ctx, "setup")
        raw_bias = L.sb("raw_bias", [LO_ROW + 1, E * D])
        raw_sq = L.sb("raw_sq", [P, len(SQUARES), P])
        raw_la = L.sb("raw_la", [P, 3, P])
        raw_lb = L.sb("raw_lb", [P, 3, P])
        raw_cols = raw_la[LORA:LORA + COLS, 2, :]
        banks = [L.bank(f"bank{k}") for k in range(8)]
        small_in = L.sem("small_in")
        vectors_in = L.sem("vectors_in")
        x_in = L.sem("x_in")
        bias_in = L.sem("bias_in")
        cleared = L.sem("cleared")
        ready = L.sem("ready")
        turned = L.sem("turned")
        emptied = L.sem("emptied")
        split = L.sem("split")
        misc = L.sem("misc")
        block = ctx.enter_context(nc.Block())

        squares = [(raw_sq[:, k, :], P, P) for k in range(len(SQUARES))]
        squares += [(raw_la[:, k, :] if k < 2 else raw_la[0:LORA + COLS, k, :], P if k < 2 else LORA + COLS, P) for k in range(3)]
        squares += [(raw_lb[:, k, :] if k < 2 else raw_lb[:, k, 0:LORA], P, P if k < 2 else LORA) for k in range(3)]
        outs = [res["sqT"][:, k, :] for k in range(len(SQUARES))]
        outs += [res["laT"][:, k, :] if k < 2 else res["laT"][:, k, 0:LORA + COLS] for k in range(3)]
        outs += [res["lbT"][:, k, :] if k < 2 else res["lbT"][0:LORA, k, :] for k in range(3)]
        n_small = len(squares)

        total_small = 8 + 2 + (len(SQUARES) - 1 + 2 * len(LORAS) + 1)

        @block.sync
        def _(sp):
            def small(dst, src):
                sp.dma_start(dst, src).then_inc(small_in, 16)

            sp.dma_start(x[:, :, :], ins["L0_attn_x"].rearrange("b (g p) d -> p (b g) d", p=P)).then_inc(x_in, 16)
            sp.wait_ge(cleared, 1)
            for r in (0, LO_ROW):
                sp.dma_start(raw_bias[r:r + 1, :], ins["L0_ffn_b2"].rearrange("(a e) f -> a (e f)", a=1)).then_inc(bias_in, 16)
            small(ident[:, :], ins["const_ident"])
            small(block_diag[:, :], ins["const_block"])
            small(res["gate0"][:, :], ins["L0_ffn_gate_w"])
            small(res["before"][:, :], ins["const_before"])
            small(res["tile_start"][:, :], ins["const_tile_start"])
            small(res["gate_bias"][:, :], row(ins["L0_ffn_gate_b"]).broadcast_to([P, E]))
            small(res["post_g"][:, :], row(ins["L0_ffn_ln_g"]).broadcast_to([P, D]))
            small(res["post_b"][:, :], row(ins["L0_ffn_ln_b"]).broadcast_to([P, D]))
            for c, n in ((COL_LNW, "L1_attn_ln_w"), (COL_LNB, "L1_attn_ln_b")):
                small(raw_cols[c:c + 1, :].rearrange("a (h j) -> a h j", j=HD),
                      ins[n].rearrange("(a b j) -> a b j", a=1, b=1).broadcast_to([1, HEADS, HD]))
            sp.wait_ge(ready, 1)
            sp.dma_start(slots_x.rearrange("(t p) d -> p t d", p=P), res["zeros"][:, :, :].broadcast_to([P, PLACES // P, D]))\
              .then_inc(later["slots_zeroed"], 16)
            for n, w in (("raw_s1", "L1_ffn_w1"), ("raw_s3", "L1_ffn_w3")):
                sp.dma_start(res[n][:, :, :], ins[w].rearrange("e (c p) h -> p (e c) h", p=P)).then_inc(later["swiglu_in"], 16)
            sp.dma_start(res["raw_s2"][:, :, :], ins["L1_ffn_w2"].rearrange("e h i -> h e i")).then_inc(later["swiglu_in"], 16)
            sp.wait_ge(x_in, 16)

        @block.gpsimd
        def _(pool):
            pool.memset(res["zeros"][:, :, :], 0.0)
            pool.memset(res["ones"][:, :], 1.0).then_inc(ready, 1)
            for n in VECTORS:
                pool.dma_start(raw_cols[COL[n]:COL[n] + 1, :], row(ins[n])).then_inc(vectors_in, 16)
            pool.dma_start(raw_cols[COL_WG:COL_WG + E, :], ins["L1_ffn_wg"]).then_inc(vectors_in, 16)
            pool.memset(res["replace"][:, :, :], BIG)
            pool.memset(res["neg_half"][:, :], -0.5)
            pool.memset(res["e_temp"][:, :], float(2.718281828459045 ** (1.0 / TEMP)))
            pool.memset(res["eps"][:, :], EPS)
            pool.memset(res["e_one"][:, :], 2.718281828459045)
            pool.memset(res["sel"][:, :, :], 0.0).then_inc(misc, 1)
            pool.wait_ge(small_in, 16 * total_small)
            pool.wait_ge(misc, 1)
            for n in ("post_g", "post_b"):
                pool.tensor_scalar_mul(res[n][:, :], res[n][:, :], 0.5).then_inc(misc, 1)
            for j in range(HD):
                pool.tensor_copy(res["sel"][:, j, :].rearrange("p (h j) -> p h j", j=HD)[:, :, j],
                                 block_diag[:, :].rearrange("p (h j) -> p h j", j=HD)[:, :, j]).then_inc(misc, 1)
            pool.tensor_scalar_mul(res["head_mean"][:, :], block_diag[:, :], 1.0 / HD).then_inc(misc, 1)
            pool.wait_ge(misc, 4 + HD)
            pool.tensor_tensor(res["head_centre"][:, :], ident[:, :], res["head_mean"][:, :], ALU.subtract).then_inc(misc, 1)

        @block.scalar
        def _(act):
            def extra(dst, src):
                act.dma_start(dst, src).then_inc(small_in, 16)

            extra(raw_sq[:, 0:2, :], ins["L0_attn_W_in"].rearrange("(a p) d -> p a d", p=P))
            for k, n in enumerate(("L0_attn_W_state", "L0_attn_W_dt", "L0_attn_W_C", "L0_attn_W_out", "L1_attn_rW",
                                   "L1_attn_kW", "L1_attn_vW", "L1_attn_gW", "L1_attn_oW")):
                extra(raw_sq[:, 2 + k, :], ins[n])
            for q in LORAS:
                pair, half = LA[q]
                extra(raw_la[half * LORA:(half + 1) * LORA, pair, :], ins[f"L1_attn_{q}_la"])
                extra(raw_lb[:, pair, half * LORA:(half + 1) * LORA], ins[f"L1_attn_{q}_lb"])
            extra(res["state0"][:, :], ins["L1_attn_init_state"].rearrange("h i j -> (h i) j"))
            act.dma_start(res["w1"][:, :, 0:FF], ins["L0_ffn_w1"].rearrange("e d f -> d e f")).then_inc(later["gelu_in"], 16)
            act.dma_start(res["w1"][:, :, FF:WIDE], ins["b1_columns"]).then_inc(later["gelu_in"], 16)
            act.dma_start(res["w2"][:, :, :], ins["L0_ffn_w2"].rearrange("e (c p) d -> p (e c) d", p=P)).then_inc(later["gelu_in"], 16)
            for k, (dst, (src, rows, cols)) in enumerate(zip(outs, squares)):
                act.wait_ge(turned, k + 1)
                act.copy(dst, banks[k % 8][0:cols, 0:rows]).then_inc(emptied, 1)

        @block.tensor
        def _(pe):
            pe.wait_ge(small_in, 16 * total_small)
            pe.wait_ge(vectors_in, 16 * (len(VECTORS) + 1))
            for k, (src, rows, cols) in enumerate(squares):
                if k >= 8:
                    pe.wait_ge(emptied, k - 7)
                pe.transpose(banks[k % 8][0:cols, 0:rows], src, ident[0:rows, 0:rows]).then_inc(turned, 1)

        @block.vector
        def _(dve):
            dve.memset(raw_bias[:, :], 0.0).then_inc(cleared, 1)
            dve.wait_ge(ready, 1)
            dve.tensor_copy(res["bias_ones"][:, :], res["ones"][0:LO_ROW + 1, :])
            dve.wait_ge(bias_in, 32)
            lo = slice(LO_ROW, LO_ROW + 1)
            dve.tensor_copy(res["bias"][:, :], raw_bias[:, :]).then_inc(split, 1)
            dve.wait_ge(split, 1)
            dve.tensor_tensor(raw_bias[lo, :], raw_bias[lo, :], res["bias"][lo, :].bitcast(F32), ALU.subtract).then_inc(split, 1)
            dve.wait_ge(split, 2)
            dve.tensor_copy(res["bias"][lo, :], raw_bias[lo, :])
            dve.wait_ge(emptied, n_small)
            for j in range(HD):
                dve.tensor_copy(res["v_each"][:, j, :].rearrange("p (h i) -> p h i", i=HD),
                                res["sqT"][:, SQ["vW"], :].rearrange("p (h j) -> p h j", j=HD)[:, :, j:j + 1]
                                .broadcast_to([P, HEADS, HD]))


def swiglu_weights(nc, res, ident, swiglu_in):
    with ExitStack() as ctx:
        L = Layer(nc, ctx, "swiglu_weights")
        banks = [L.bank(f"bank{k}") for k in range(8)]
        turned = L.sem("turned")
        emptied = [L.sem("emptied_even"), L.sem("emptied_odd")]
        jobs = []
        for half, raw in enumerate(("raw_s1", "raw_s3")):
            for k in range(0, E * FI // P, 4):
                e = slice(k * P // FI, (k + 4) * P // FI)
                jobs.append(([res[raw][:, k + j, :] for j in range(4)], res["s13"][:, e, half * FI:(half + 1) * FI]))
        for k in range(0, E * FI // P, 4):
            jobs.append(([res["raw_s2"][:, (k + j) // 2, ((k + j) % 2) * P:((k + j) % 2 + 1) * P] for j in range(4)],
                         res["s2"][:, k:k + 4, :]))
        block = ctx.enter_context(nc.Block())

        def bank_as(k, like):
            return banks[k % 8][:, :].rearrange("p (c d) -> p c d", d=like.shape[-1])

        @block.tensor
        def _(pe):
            pe.wait_ge(swiglu_in, 48)
            for k, (srcs, _dst) in enumerate(jobs):
                if k >= 8:
                    pe.wait_ge(emptied[k % 2], (k - 8) // 2 + 1)
                for j, src in enumerate(srcs):
                    last = pe.transpose(banks[k % 8][:, j * P:(j + 1) * P], src, ident[:, :])
                last.then_inc(turned, 1)

        @block.scalar
        def _(act):
            for k in range(0, len(jobs), 2):
                dst = jobs[k][1]
                act.wait_ge(turned, k + 1)
                act.copy(dst, bank_as(k, dst)).then_inc(emptied[0], 1)

        @block.vector
        def _(dve):
            for k in range(1, len(jobs), 2):
                dst = jobs[k][1]
                dve.wait_ge(turned, k + 1)
                dve.tensor_copy(dst, bank_as(k, dst)).then_inc(emptied[1], 1)


def rates(nc, res):
    with ExitStack() as ctx:
        L = Layer(nc, ctx, "rates")
        t1 = L.sb("t1", [P, 1])
        t2 = L.sb("t2", [P, 1])
        t3 = L.sb("t3", [P, 1])
        acted = L.sem("acted")
        summed = L.sem("summed")
        a_log = res["cols"][:, COL["L0_attn_A_log"]:COL["L0_attn_A_log"] + 1]
        block = ctx.enter_context(nc.Block())

        @block.scalar
        def _(act):
            act.activation(t1[:, :], a_log, ACT.Abs).then_inc(acted, 1)
            act.wait_ge(acted, 1)
            act.activation(t2[:, :], t1[:, :], ACT.Exp, scale=-1.0).then_inc(acted, 1)
            act.wait_ge(acted, 2)
            act.activation(t3[:, :], t2[:, :], ACT.Ln, bias=1.0).then_inc(acted, 1)
            act.wait_ge(summed, 2)
            act.activation(res["floor"][:, :], res["neg_rate"][:, :], ACT.Exp, scale=DT_MAX).then_inc(acted, 1)

        @block.vector
        def _(dve):
            dve.wait_ge(acted, 3)
            dve.scalar_tensor_tensor(t1[:, :], a_log, 0.0, t3[:, :], ALU.max, ALU.add).then_inc(summed, 1)
            dve.wait_ge(summed, 1)
            dve.tensor_scalar(res["neg_rate"][:, :], t1[:, :], RATE_EPS, -1.0, ALU.add, ALU.mult).then_inc(summed, 1)


def mixture(nc, name, kind, x, res, ident, slots_x, slots_y, slots_zeroed=None, weights_in=None):
    gelu = kind == "gelu"
    PART_GROUPS, PART_TILES = PARTS_OF[kind], tiles_of(PARTS_OF[kind])
    GROUP0 = [sum(PART_GROUPS[:p]) for p in range(PARTS + 1)]
    TILE0 = [sum(PART_TILES[:p]) for p in range(PARTS + 1)]
    NTILES = TILE0[PARTS]
    F = FF if gelu else FI
    CH = F // P
    XT = 3
    QUADS = [g // SUB for g in PART_GROUPS]
    QUAD0 = [g // SUB for g in GROUP0]
    SET = BODY // 2
    ITERS = NTILES // BODY
    LAG, RING = (1, 2) if gelu else (2, 4)
    BANKS = BODY
    DIGITS = UNROLL * BODY
    assert ITERS * BODY == NTILES and E ** DIGITS <= 2 ** 24 and 2 * SET == BODY and LAG <= SET and LAG + BODY <= DIGITS
    upto = lambda p: TILE0[p] // BODY
    ROUND = 1.5 * 2 ** 23
    gate_w = res["gate0"][:, :] if gelu else res["cols"][:, COL_WG:COL_WG + E]
    base = res["e_temp"] if gelu else res["e_one"]

    with ExitStack() as ctx:
        L = Layer(nc, ctx, name)
        xn = L.sb("xn", [P, GROUPS, D])
        st, mv = L.sb("st", [P, GROUPS, 6]), L.sb("mv", [P, GROUPS, 2])
        ve, rstd = L.sb("ve", [P, GROUPS]), L.sb("rstd", [P, GROUPS])
        each = lambda n, *shape: [L.sb(f"{n}{p}", [P] + [PART_GROUPS[p] if d is G else d for d in shape]) for p in range(PARTS)]
        G = object()
        lg, cut, first, mask, weight, gate = (each(n, G, E) for n in ("lg", "cut", "first", "mask", "weight", "gate"))
        top = each("top", G, 8)
        diff, e2, den = (each(n, G) for n in ("diff", "e2", "den"))
        count = each("count", 4, E)
        steps = [L.sb(f"steps{p}", [P, E, PART_GROUPS[p] + 1]) for p in range(PARTS)]
        ends = [L.sb(f"ends{p}", [P, E, PART_GROUPS[p] + 1]) for p in range(PARTS)]
        pos, taken, free = (each(n, G, E) for n in ("pos", "taken", "free"))
        place = each("place", TOP, G)
        own = each("own", TOP, G)
        picked = each("picked", TOP, G, E)
        index = [L.sb(f"index{p}", [P, TOP, PART_GROUPS[p]], I32) for p in range(PARTS)]
        xT = L.sb("xT", [P, XT, TILE])
        ended = L.sb("ended", [1, MOST_TILES, E])
        expert = L.sb("expert", [1, LAG + NTILES + BODY])
        packed = L.sb("packed", [1, 2, ITERS])
        words = L.sb("words", [1, ITERS], I32)

        xs = L.sb("xs", [P, 2 * BODY, D])
        xsT = [L.sb(f"xsT{k}", [P, SET, P]) for k in range(2)]
        weights = L.sb("weights", [P, BODY, WIDE if gelu else FF])
        hid = L.sb("hid", [P, RING, F])
        sil = None if gelu else L.sb("sil", [P, BANKS, F])
        ys = [L.sb(f"ys{k}", [P, SET, D]) for k in range(2)]
        st2, mv2, ve2, rstd2 = each("st2", G, 6), each("mv2", G, 2), each("ve2", G), each("rstd2", G)
        small, large = (L.sb(n, [P, TOP * g, D]) for n, g in (("back_small", PART_GROUPS[0]), ("back_large", PART_GROUPS[1])))
        back = [[t[:, k * g:(k + 1) * g, :] for k in range(TOP)] for t, g in zip((small, large, xn, small), PART_GROUPS)]

        turn = L.bank("turn")
        hb = [L.bank(f"hb{k}") for k in range(BANKS)]
        ob = [L.bank(f"ob{k}") for k in range(2)]
        side = L.bank("side")
        unused = hb + [turn]
        early = [unused[0:QUADS[0]], unused[QUADS[0]:], [side] * QUADS[2], [side] * QUADS[3]]
        counts = [ob[0], ob[1], side, side]
        CW = [g * E for g in PART_GROUPS]

        chain, held = L.sem("dve_chain"), L.sem("held")
        var_ready, rstd_ready = L.sem("var_ready"), L.sem("rstd_ready")
        xn_ready = L.sem("xn_ready")
        xt_ps, xt_copied, xt_used = L.sem("xt_ps"), L.sem("xt_copied"), L.sem("xt_used")
        diff_ready, e2_ready = L.sem("diff_ready"), L.sem("e2_ready")
        mask_ready, counted = L.sem("mask_ready"), L.sem("counted")
        index_ready, table_ready = L.sem("index_ready"), L.sem("table_ready")
        sent = [L.sem(f"sent{p}") for p in range(PARTS)]
        loaded = L.sem("loaded")
        weights_ready = [L.sem(f"weights_ready{j}") for j in range(BODY)]
        turned = L.sem("turned")
        set_ready = L.sem("set_ready")
        h_ready = L.sem("h_ready")
        sil_ready = L.sem("sil_ready")
        hid_ready = L.sem("hid_ready")
        out_ready, y_done = L.sem("out_ready"), L.sem("y_done")
        stored = [L.sem(f"stored{k}") for k in range(2)]
        came = [[[L.sem(f"came{p}_{q}_{k}") for k in range(TOP)] for q in range(QUADS[p])] for p in range(PARTS)]
        gates_ready = L.sem("gates_ready")
        lower_scaled = L.sem("lower_scaled")
        combined = L.sem("combined")
        shifted = L.sem("shifted")
        var2, rstd2_ready = L.sem("var2"), L.sem("rstd2_ready")
        block = ctx.enter_context(nc.Block())

        SENT = [16 * g * TOP for g in PART_GROUPS]
        group = lambda t, p: t[:, GROUP0[p]:GROUP0[p + 1]]

        def run(eng, body, beside, breaks=(), prepare=lambda i: None):
            i = 0
            while i < ITERS:
                n = i
                while n < ITERS - 1 and n > 0 and n not in beside and (n == i or n not in breaks):
                    n += 1
                if i in breaks:
                    breaks[i]()
                turns = (n - i) // UNROLL
                if turns > 1:
                    with eng.Fori(0, turns) as k:
                        ready = prepare(k * UNROLL + i)
                        for u in range(UNROLL):
                            body(k * UNROLL + (i + u), False, False, {}, (ready, u, (i + u) % 2))
                    i += turns * UNROLL
                else:
                    body(i, i == 0, i == ITERS - 1, beside.get(i, {}), (prepare(i), 0, i % 2))
                    i += 1

        @block.sync
        def _(sp):
            w1 = res["w1" if gelu else "s13"]
            used = hid_ready if gelu else h_ready

            def load(i):
                sp.dma_start(xs[:, bass.ds((i & 1) * BODY, BODY), :],
                             slots_x[bass.ds(i * (BODY * P), BODY * P), :].rearrange("(j p) d -> p j d", p=P)).then_inc(loaded, 16)

            def experts_of(i):
                word = sp.value_load(words[0:1, bass.ds(i, 1)], min_val=0, max_val=E ** DIGITS - 1)
                return [sp.snap((word >> (3 * (LAG + j))) & (E - 1), min_val=0, max_val=E - 1) for j in range(BODY)]

            def fill(j, e):
                sp.dma_start(weights[:, j, :], w1[:, bass.ds(e, 1), :].rearrange("p a f -> p (a f)")).then_inc(weights_ready[j], 16)

            def body(i, needs=None, loads=True):
                experts = experts_of(i + 1)
                for j in range(BODY):
                    sp.wait_ge(used, i * BODY + (j + 1 + BANKS))
                    sp.sem_inc(held, 1)
                    fill(j, experts[j])
                if needs:
                    sp.wait_ge(sent[needs], SENT[needs])
                    sp.wait_ge(table_ready, needs + 1)
                if loads:
                    sp.wait_ge(turned, i * 2 + 2)
                    sp.wait_ge(loaded, i * 16 + 32)
                    sp.sem_inc(held, 1)
                    load(i + 2)

            sp.wait_ge(sent[0], SENT[0])
            load(0)
            if weights_in:
                sp.wait_ge(weights_in, 48)
            sp.wait_ge(table_ready, 1)
            experts = experts_of(0)
            for j in range(BODY):
                fill(j, experts[j])
            sp.wait_ge(loaded, 16)
            load(1)
            i = 0
            for p in range(1, PARTS + 1):
                to = -(-(TILE0[p] - 3 * BODY + 1) // BODY) if p < PARTS else ITERS - 2
                if to > i:
                    with sp.Fori(0, to - i) as k:
                        body(k + i)
                if p < PARTS:
                    body(to, needs=p)
                i = to + 1
            body(ITERS - 2, loads=False)

        @block.tensor
        def _(pe):
            def turn_tokens(p, q):
                n = QUAD0[p] + q
                pe.wait_ge(xn_ready, n + 1)
                if p >= EARLY:
                    pe.wait_ge(xt_copied, n)
                if p > EARLY and q == 0:
                    pe.wait_ge(index_ready, p)
                for s in range(SUB):
                    last = pe.transpose(early[p][q][:, s * P:(s + 1) * P], xn[:, n * SUB + s, :], ident[:, :])
                last.then_inc(xt_ps, 1)

            def logits(p, q):
                n = QUAD0[p] + q
                pe.wait_ge(xt_copied, QUAD0[p + 1] if counts[p] is side else n + 1)
                for s in range(SUB):
                    g = q * SUB + s
                    last = pe.matmul(counts[p][:, g * E:(g + 1) * E], xT[:, n % XT, s * P:(s + 1) * P], gate_w, start=True, stop=True)
                last.then_inc(xt_used, 1)

            def count_tokens(p):
                pe.wait_ge(mask_ready, p + 1)
                chosen = mask[p][:, :, :].rearrange("p g e -> p (g e)")
                w = CW[p]
                pe.matmul(counts[p][:, w:2 * w], res["before"][:, :], chosen, start=True, stop=True)
                pe.matmul(counts[p][:, 2 * w:3 * w], res["ones"][:, :], chosen, start=True, stop=True).then_inc(counted, 1)

            def turn_set(k, half, i, odd):
                pe.wait_ge(loaded, i * 16 + 16)
                pe.wait_ge(set_ready, k + 1)
                for j in range(SET):
                    last = pe.transpose(turn[:, j * P:(j + 1) * P], xs[:, odd * BODY + half * SET + j, :], ident[:, :])
                last.then_inc(turned, 1)

            def first_products(s, j, i):
                if j % SET == 0:
                    pe.wait_ge(set_ready, i * 2 + (j // SET + 2))
                pe.wait_ge(weights_ready[j], i * 16 + 16)
                pe.wait_ge(hid_ready, s + 1)
                for c in range(FF // P):
                    last = pe.matmul(hb[j][:, c * P:(c + 1) * P], weights[:, j, c * P:(c + 1) * P], xsT[j // SET][:, j % SET, :],
                                     start=True, stop=True)
                last.then_inc(h_ready, 1)

            def second_products(s, j, e):
                pe.wait_ge(hid_ready, s + (1 + BANKS))
                pe.wait_ge(y_done, s + 1)
                r, o = j % RING, ob[j % 2]
                w2 = res["w2" if gelu else "s2"][:, :, :].rearrange("p (e c) d -> p e c d", e=E)
                if gelu:
                    pe.matmul(o[:, 0:D], res["bias_ones"][:, :], res["bias"][:, bass.ds(e * D, D)], start=True, stop=False)
                for c in range(CH):
                    last = pe.matmul(o[:, 0:D], hid[:, r, c * P:(c + 1) * P], w2[:, bass.ds(e, 1), c, :].rearrange("p a d -> p (a d)"),
                                     start=not gelu and c == 0, stop=c == CH - 1)
                last.then_inc(out_ready, 1)

            def word_of(i):
                return pe.value_load(words[0:1, bass.ds(i, 1)], min_val=0, max_val=E ** DIGITS - 1)

            def body(i, first, last, beside, ready):
                word, u, odd = ready
                expert_of = lambda d: pe.snap((word >> (3 * (u * BODY + d))) & (E - 1), min_val=0, max_val=E - 1)
                for j in range(BODY):
                    s = i * BODY + j
                    if j == 0:
                        turn_set(i * 2 + 1, 1, i, odd)
                    first_products(s, j, i)
                    if first and j == LAG + 1:
                        pe.wait_ge(table_ready, 2)
                    if not (first and j < LAG):
                        second_products(s - LAG, j - LAG, expert_of(j))
                    if j == 2 and not last:
                        turn_set(i * 2 + 2, 0, i + 1, 1 - odd)
                    for part in beside.get(j, []):
                        part()
                if last:
                    for d in range(LAG):
                        second_products(NTILES - LAG + d, BODY - LAG + d, expert_of(BODY + d))

            pe.sem_inc(xt_used, XT)
            pe.sem_inc(h_ready, 2 * SET)
            pe.sem_inc(out_ready, RING)
            for p in range(EARLY):
                for q in range(QUADS[p]):
                    turn_tokens(p, q)
                    if q:
                        logits(p, q - 1)
                logits(p, QUADS[p] - 1)
                count_tokens(p)
            pe.wait_ge(table_ready, 1)
            if weights_in:
                pe.wait_ge(weights_in, 48)
            turn_set(0, 0, 0, 0)
            at = lambda f, *a: [lambda: f(*a)]
            beside = {0: {2: at(turn_tokens, 2, 0), 3: at(turn_tokens, 2, 1)},
                      1: {0: at(turn_tokens, 2, 2), 2: at(logits, 2, 0) + at(logits, 2, 1) + at(logits, 2, 2)},
                      2: {2: at(count_tokens, 2)},
                      6: {0: at(turn_tokens, 3, 0), 2: at(logits, 3, 0)},
                      7: {2: at(count_tokens, 3)}} if gelu else \
                     {1: {2: at(turn_tokens, 2, 0), 3: at(turn_tokens, 2, 1)},
                      2: {2: at(logits, 2, 0) + at(logits, 2, 1)},
                      3: {2: at(count_tokens, 2)},
                      9: {0: at(turn_tokens, 3, 0), 2: at(logits, 3, 0)},
                      10: {2: at(count_tokens, 3)}}
            run(pe, body, beside,
                {upto(p): (lambda p=p: pe.wait_ge(table_ready, p + 1)) for p in range(1, PARTS)}, word_of)

        @block.scalar
        def _(act):
            def copy_set(k, half):
                act.wait_ge(turned, k + 1)
                act.wait_ge(h_ready, k * SET + SET)
                act.copy(xsT[half][:, :, :], turn[:, 0:SET * P].rearrange("p (j d) -> p j d", j=SET)).then_inc(set_ready, 1)

            def nonlinear(s, j):
                act.wait_ge(h_ready, s + 1 + 2 * SET)
                if gelu:
                    act.wait_ge(out_ready, s + 1)
                    for c in range(CH):
                        last = act.activation(hid[:, j % RING, c * P:(c + 1) * P], hb[j][:, c * P:(c + 1) * P], ACT.Gelu,
                                              bias=weights[:, j, FF + c:FF + c + 1])
                    last.then_inc(hid_ready, 1)
                else:
                    act.activation(sil[:, j, :], hb[j][:, 0:FI], ACT.Silu).then_inc(sil_ready, 1)

            def store(k, odd):
                act.wait_ge(y_done, k * SET + SET + 2)
                act.dma_start(slots_y[bass.ds(k * (SET * P), SET * P), :].rearrange("(j p) d -> p j d", p=P), ys[odd][:, :, :])\
                   .then_inc(stored[odd], 16)

            def scale_lower(p, q):
                act.wait_ge(gates_ready, p + 1)
                act.wait_ge(came[p][q][0], 16 * SUB)
                for g in range(q * SUB, (q + 1) * SUB):
                    last = act.activation(back[p][0][:, g, :], back[p][0][:, g, :], ACT.Copy, scale=own[p][:, 0, g:g + 1])
                last.then_inc(lower_scaled, 1)

            def copy_tokens(p, q):
                n = QUAD0[p] + q
                act.wait_ge(xt_ps, n + 1)
                act.wait_ge(xt_used, n + 1)
                act.copy(xT[:, n % XT, :], early[p][q][:, :]).then_inc(xt_copied, 1)

            def body(i, first, last, beside, _ready):
                for j in range(BODY):
                    s = i * BODY + j
                    if j == 0:
                        copy_set(i * 2 + 1, 1)
                    nonlinear(s, j)
                    if j == 2 and not last:
                        copy_set(i * 2 + 2, 0)
                    if (j - LAG) % SET == 0:
                        k = (j - LAG) // SET - 1
                        if not (first and k < 0):
                            store(i * 2 + k, k % 2)
                    for part in beside.get(j, []):
                        part()

            act.sem_inc(set_ready, 1)
            if gelu:
                act.sem_inc(hid_ready, BANKS)
            for p in range(EARLY):
                for q in range(QUADS[p]):
                    copy_tokens(p, q)
            nc.scalar.preload_act_table(ACT.Gelu if gelu else ACT.Silu)
            copy_set(0, 0)
            at = lambda f, *a: [lambda: f(*a)]
            beside = {0: {2: at(copy_tokens, 2, 0), 3: at(copy_tokens, 2, 1)},
                      1: {0: at(copy_tokens, 2, 2)},
                      6: {0: at(copy_tokens, 3, 0)},
                      12: {1: at(scale_lower, 0, 0)},
                      16: {1: at(scale_lower, 1, 0)},
                      17: {1: at(scale_lower, 1, 1)},
                      18: {1: at(scale_lower, 1, 2)},
                      22: {1: at(scale_lower, 2, 0)}} if gelu else \
                     {1: {2: at(copy_tokens, 2, 0), 3: at(copy_tokens, 2, 1)},
                      9: {0: at(copy_tokens, 3, 0)},
                      13: {0: at(scale_lower, 0, 0), 1: at(scale_lower, 0, 1)},
                      18: {3: at(scale_lower, 1, 0)},
                      19: {1: at(scale_lower, 1, 1), 3: at(scale_lower, 1, 2)}}
            run(act, body, beside)
            for k in range(NTILES // SET - LAG, NTILES // SET):
                store(k, k % 2)
            for p, q in ((2, 1), (2, 2), (3, 0)) if gelu else ((2, 0), (2, 1), (3, 0)):
                scale_lower(p, q)

        @block.vector
        def _(dve):
            ch = Steps(dve, chain, 0, held)

            def stats(p):
                for g in range(GROUP0[p], GROUP0[p + 1]):
                    last = dve.bn_stats(st[:, g, :], x[:, g, :])
                ch.step(last)
                ch.settle()
                for g in range(GROUP0[p], GROUP0[p + 1]):
                    last = dve.bn_aggr(mv[:, g, :], st[:, g, :])
                ch.step(last)
                ch.settle()
                dve.tensor_scalar(group(ve, p), mv[:, GROUP0[p]:GROUP0[p + 1], 1], EPS, None, ALU.add).then_inc(var_ready, 1)

            def normalise(p):
                dve.wait_ge(rstd_ready, p + 1)
                for n in range(QUAD0[p], QUAD0[p + 1]):
                    for g in range(n * SUB, (n + 1) * SUB):
                        last = dve.tensor_scalar(xn[:, g, :], x[:, g, :], mv[:, g, 0:1], rstd[:, g:g + 1], ALU.subtract, ALU.mult)
                    last.then_inc(xn_ready, 1)

            def route(p):
                dve.wait_ge(xt_used, QUAD0[p + 1] + XT)
                lg_ps = counts[p][:, 0:CW[p]].rearrange("p (g e) -> p g e", e=E)
                if gelu:
                    ch.step(dve.tensor_tensor(lg[p][:, :, :], lg_ps, res["gate_bias"][:, :].rearrange("p (a e) -> p a e", a=1)
                                              .broadcast_to([P, PART_GROUPS[p], E]), ALU.add))
                else:
                    ch.step(dve.tensor_copy(lg[p][:, :, :], lg_ps))
                ch.settle()
                for g in range(PART_GROUPS[p]):
                    last = dve.max(top[p][:, g, :], lg[p][:, g, :])
                ch.step(last)
                ch.settle()
                dve.tensor_tensor(diff[p][:, :], top[p][:, :, 1], top[p][:, :, 0], ALU.subtract).then_inc(diff_ready, 1)
                ch.step(dve.tensor_copy(res["replace"][:, GROUP0[p]:GROUP0[p + 1], 0:TOP], top[p][:, :, 0:TOP]))
                ch.settle()
                for g in range(PART_GROUPS[p]):
                    last = dve.match_replace(cut[p][:, g, :], res["replace"][:, GROUP0[p] + g, :], lg[p][:, g, :], -BIG)
                ch.step(last)
                ch.settle()
                dve.tensor_tensor(mask[p][:, :, :], cut[p][:, :, :], lg[p][:, :, :], ALU.not_equal).then_inc(mask_ready, 1)
                ch.step(dve.tensor_tensor(first[p][:, :, :], lg[p][:, :, :], top[p][:, :, 0:1].broadcast_to([P, PART_GROUPS[p], E]), ALU.is_equal))

            def gates(p):
                dve.wait_ge(e2_ready, p + 1)
                ch.settle()
                ch.step(dve.tensor_tensor(weight[p][:, :, :], first[p][:, :, :],
                                          e2[p][:, :].rearrange("p (s a) -> p s a", a=1).broadcast_to([P, PART_GROUPS[p], E]), ALU.max))
                ch.step(dve.tensor_scalar(diff[p][:, :], e2[p][:, :], 1.0, None, ALU.add))
                ch.settle()
                ch.step(dve.tensor_tensor(first[p][:, :, :], weight[p][:, :, :], mask[p][:, :, :], ALU.mult))
                ch.step(dve.reciprocal(den[p][:, :], diff[p][:, :]))
                ch.settle()
                ch.step(dve.tensor_tensor(gate[p][:, :, :], first[p][:, :, :],
                                          den[p][:, :].rearrange("p (s a) -> p s a", a=1).broadcast_to([P, PART_GROUPS[p], E]), ALU.mult))
                ch.settle()
                for k in range(TOP):
                    ch.step(dve.tensor_tensor(picked[p][:, k, :, :], pos[p][:, :, :],
                                              place[p][:, k, :].rearrange("p (g a) -> p g a", a=1).broadcast_to([P, PART_GROUPS[p], E]), ALU.is_equal))
                ch.settle()
                for k in range(TOP):
                    ch.step(dve.tensor_tensor(picked[p][:, k, :, :], picked[p][:, k, :, :], gate[p][:, :, :], ALU.mult))
                ch.settle()
                dve.tensor_reduce(own[p][:, :, :], picked[p][:, :, :, :], AX.X, ALU.add).then_inc(gates_ready, 1)

            def places(p):
                dve.wait_ge(counted, p + 1)
                by_expert = lambda ap: ap.rearrange("p g e -> p e g")
                total = counts[p][:, 2 * CW[p]:3 * CW[p]].rearrange("p (g e) -> p g e", e=E)
                rank = counts[p][:, CW[p]:2 * CW[p]].rearrange("p (g e) -> p g e", e=E)
                n, t1, t2, tiles = (count[p][:, k, :] for k in range(4))
                ch.step(dve.tensor_copy(steps[p][:, :, 0:PART_GROUPS[p]], by_expert(total)))
                ch.settle()
                ch.step(dve.tensor_reduce(n, steps[p][:, :, 0:PART_GROUPS[p]], AX.X, ALU.add))
                ch.settle()
                ch.step(dve.tensor_scalar(t1, n, 1.0 / P, 0.5 - 0.5 / P, ALU.mult, ALU.add))
                ch.settle()
                ch.step(dve.tensor_scalar(t2, t1, ROUND, None, ALU.add))
                ch.settle()
                ch.step(dve.tensor_scalar(tiles, t2, -ROUND, None, ALU.add))
                ch.settle()
                ch.step(dve.scalar_tensor_tensor(steps[p][:, :, PART_GROUPS[p]], tiles, float(P), n, ALU.mult, ALU.subtract))
                ch.settle()
                ch.step(dve.tensor_tensor_scan(ends[p][:, :, :].rearrange("p e g -> p (e g)"),
                                               res["ones"][:, 0:1].broadcast_to([P, E * (PART_GROUPS[p] + 1)]),
                                               steps[p][:, :, :].rearrange("p e g -> p (e g)"), 0.0, ALU.mult, ALU.add))
                ch.settle()
                ch.step(dve.tensor_tensor(by_expert(pos[p][:, :, :]), ends[p][:, :, 0:PART_GROUPS[p]], steps[p][:, :, 0:PART_GROUPS[p]], ALU.subtract))
                ch.settle()
                ch.step(dve.scalar_tensor_tensor(taken[p][:, :, :], rank, float(TILE0[p] * P + 1), pos[p][:, :, :], ALU.add, ALU.add))
                ch.step(dve.tensor_scalar(free[p][:, :, :], mask[p][:, :, :], -float(2 ** 20), float(2 ** 20), ALU.mult, ALU.add))
                ch.settle()
                ch.step(dve.tensor_tensor(pos[p][:, :, :], taken[p][:, :, :], mask[p][:, :, :], ALU.mult))
                ch.settle()
                ch.step(dve.tensor_reduce(place[p][:, 1, :], pos[p][:, :, :], AX.X, ALU.max))
                ch.step(dve.tensor_tensor(free[p][:, :, :], free[p][:, :, :], pos[p][:, :, :], ALU.add))
                ch.settle()
                ch.step(dve.tensor_reduce(place[p][:, 0, :], free[p][:, :, :], AX.X, ALU.min))
                ch.settle()
                dve.tensor_scalar(index[p][:, :, :], place[p][:, :, :], -1.0, None, ALU.add).then_inc(index_ready, 1)

            def table(p):
                tiles = PART_TILES[p]
                ch.step(dve.tensor_tensor(ended[:, 0:tiles, :], res["tile_start"][:, 0:tiles].rearrange("p (t a) -> p t a", a=1)
                                          .broadcast_to([1, tiles, E]), ends[p][0:1, :, PART_GROUPS[p]:].rearrange("p e a -> p a e")
                                          .broadcast_to([1, tiles, E]), ALU.is_ge))
                ch.settle()
                tile_expert = expert[:, LAG + TILE0[p]:LAG + TILE0[p + 1]]
                ch.step(dve.tensor_reduce(tile_expert, ended[:, 0:tiles, :], AX.X, ALU.add))
                ch.settle()
                ch.step(dve.tensor_scalar(tile_expert, tile_expert, float(E - 1), None, ALU.min))
                ch.settle()
                lo, hi = upto(p), upto(p + 1)
                digit = lambda d: expert[:, lo * BODY + d:(hi - 1) * BODY + d + 1:BODY]
                so_far = digit(DIGITS - 1)
                for d in reversed(range(DIGITS - 1)):
                    to = packed[:, d % 2, lo:hi] if d else words[:, lo:hi]
                    ins = dve.scalar_tensor_tensor(to, so_far, float(E), digit(d), ALU.mult, ALU.add)
                    if d:
                        ch.step(ins)
                        ch.settle()
                    else:
                        ins.then_inc(table_ready, 1)
                    so_far = to

            def multiply(s, j):
                dve.wait_ge(sil_ready, s + 1)
                dve.wait_ge(out_ready, s + 1)
                dve.tensor_tensor(hid[:, j % RING, :], sil[:, j, :], hb[j][:, FI:2 * FI], ALU.mult).then_inc(hid_ready, 1)

            def output(s, j, kk):
                dve.wait_ge(out_ready, s + 1 + RING)
                if j % SET == 0:
                    dve.wait_ge(stored[j // SET], kk * 16 + 16)
                dve.tensor_copy(ys[j // SET][:, j % SET, :], ob[j % 2][:, 0:D]).then_inc(y_done, 1)

            def body(i, first, last, beside, _ready):
                for j in range(BODY):
                    s = i * BODY + j
                    if not gelu:
                        multiply(s, j)
                    if not (first and j < LAG):
                        output(s - LAG, (j - LAG) % BODY, i if j >= LAG else i - 1)
                    for part in beside.get(j, []):
                        part()

            def combine(p, q):
                gs = range(q * SUB, (q + 1) * SUB)
                y = back[p]
                dve.wait_ge(came[p][q][1], 16 * SUB)
                dve.wait_ge(lower_scaled, QUAD0[p] + q + 1)
                for g in gs:
                    last = dve.scalar_tensor_tensor(y[0][:, g, :], y[1][:, g, :], own[p][:, 1, g:g + 1], y[0][:, g, :], ALU.mult, ALU.add)
                ch.step(last)
                ch.settle()
                wide = slice(q * SUB, (q + 1) * SUB)
                if not gelu:
                    xt = x[:, GROUP0[p] + q * SUB:GROUP0[p] + (q + 1) * SUB, :]
                    dve.scalar_tensor_tensor(xt, y[0][:, wide, :], 0.5, xt, ALU.mult, ALU.add).then_inc(combined, 1)

            def norm(p, q):
                if not gelu:
                    return
                gs = range(q * SUB, (q + 1) * SUB)
                wide = slice(q * SUB, (q + 1) * SUB)
                y = back[p]
                for g in gs:
                    last = dve.bn_stats(st2[p][:, g, :], y[0][:, g, :])
                ch.step(last)
                ch.settle()
                for g in gs:
                    last = dve.bn_aggr(mv2[p][:, g, :], st2[p][:, g, :])
                ch.step(last)
                ch.settle()
                dve.tensor_scalar(ve2[p][:, wide], mv2[p][:, wide, 1], EPS, None, ALU.add).then_inc(var2, 1)

            def finish(p, q):
                if not gelu:
                    return
                gs = range(q * SUB, (q + 1) * SUB)
                y = back[p]
                dve.wait_ge(rstd2_ready, QUAD0[p] + q + 1)
                for g in gs:
                    last = dve.tensor_scalar(y[1][:, g, :], y[0][:, g, :], mv2[p][:, g, 0:1], rstd2[p][:, g:g + 1], ALU.subtract, ALU.mult)
                ch.step(last)
                ch.settle()
                wide = slice(q * SUB, (q + 1) * SUB)
                ch.step(dve.tensor_tensor(y[0][:, wide, :], y[1][:, wide, :], res["post_g"][:, :].rearrange("p (a d) -> p a d", a=1)
                                          .broadcast_to([P, SUB, D]), ALU.mult))
                ch.settle()
                if q == 0:
                    dve.wait_ge(shifted, p + 1)
                xt = x[:, GROUP0[p] + q * SUB:GROUP0[p] + (q + 1) * SUB, :]
                dve.tensor_tensor(xt, xt, y[0][:, wide, :], ALU.add).then_inc(combined, 1)

            dve.sem_inc(y_done, 2)
            for k in range(2):
                dve.sem_inc(stored[k], 16)
            if not gelu:
                dve.sem_inc(hid_ready, BANKS)
            dve.memset(expert[:, :], 0.0)
            stats(0)
            normalise(0)
            stats(1)
            route(0)
            places(0)
            normalise(1)
            table(0)
            stats(2)
            route(1)
            places(1)
            table(1)
            if gelu:
                normalise(2)
                stats(3)
            at = lambda f, *a: [lambda: f(*a)]
            beside = {2: {0: at(route, 2)},
                      3: {0: at(places, 2), 2: at(table, 2)},
                      5: {0: at(normalise, 3), 2: at(gates, 0)},
                      7: {0: at(route, 3)},
                      8: {0: at(places, 3), 2: at(table, 3)},
                      9: {0: at(gates, 1)},
                      11: {0: at(gates, 2)},
                      12: {2: at(combine, 0, 0), 3: at(norm, 0, 0)},
                      14: {0: at(gates, 3)},
                      16: {0: at(finish, 0, 0), 2: at(combine, 1, 0), 3: at(norm, 1, 0)},
                      17: {0: at(finish, 1, 0), 2: at(combine, 1, 1), 3: at(norm, 1, 1)},
                      18: {0: at(finish, 1, 1), 2: at(combine, 1, 2), 3: at(norm, 1, 2)},
                      19: {0: at(finish, 1, 2)},
                      22: {2: at(combine, 2, 0), 3: at(norm, 2, 0)}} if gelu else \
                     {1: {0: at(normalise, 2)},
                      3: {0: at(route, 2)},
                      4: {0: at(places, 2), 2: at(table, 2)},
                      5: {2: at(gates, 0)},
                      6: {0: at(stats, 3)},
                      7: {0: at(gates, 1)},
                      8: {0: at(normalise, 3)},
                      10: {0: at(route, 3)},
                      11: {0: at(places, 3), 2: at(table, 3)},
                      12: {0: at(gates, 2)},
                      13: {1: at(combine, 0, 0), 2: at(combine, 0, 1)},
                      15: {0: at(gates, 3)},
                      19: {0: at(combine, 1, 0), 2: at(combine, 1, 1)},
                      20: {0: at(combine, 1, 2)}}
            run(dve, body, beside)
            for d in range(LAG):
                output(NTILES - LAG + d, BODY - LAG + d, ITERS - 1)
            if gelu:
                combine(2, 1)
                norm(2, 1)
                combine(2, 2)
                norm(2, 2)
                finish(2, 0)
                combine(3, 0)
                norm(3, 0)
                finish(2, 1)
                finish(2, 2)
                finish(3, 0)
            else:
                for p, q in ((2, 0), (2, 1), (3, 0)):
                    combine(p, q)

        @block.gpsimd
        def _(pool):
            def power(p):
                pool.wait_ge(var_ready, p + 1)
                pool.tensor_tensor(group(rstd, p), group(ve, p), res["neg_half"][:, 0:PART_GROUPS[p]], ALU.pow).then_inc(rstd_ready, 1)

            def gate_power(p):
                pool.wait_ge(diff_ready, p + 1)
                pool.tensor_tensor(e2[p][:, :], base[:, 0:PART_GROUPS[p]], diff[p][:, :], ALU.pow).then_inc(e2_ready, 1)

            def send(p):
                pool.wait_ge(index_ready, p + 1)
                for g in range(PART_GROUPS[p]):
                    for k in range(TOP):
                        pool.indirect_dma_start(slots_x[:, :], bass.IndirectOffsetOnAxis(index[p][:, k, g:g + 1], 0),
                                                xn[:, GROUP0[p] + g, :], None).then_inc(sent[p], 16)

            def shift(p):
                xt = x[:, GROUP0[p]:GROUP0[p + 1], :]
                pool.tensor_tensor(xt, xt, res["post_b"][:, :].rearrange("p (a d) -> p a d", a=1).broadcast_to([P, PART_GROUPS[p], D]), ALU.add)\
                    .then_inc(shifted, 1)

            def fetch(p, q):
                for k in range(TOP):
                    for g in range(q * SUB, (q + 1) * SUB):
                        pool.indirect_dma_start(back[p][k][:, g, :], None, slots_y[0:TILE0[p + 1] * P, :],
                                                bass.IndirectOffsetOnAxis(index[p][:, k, g:g + 1], 0)).then_inc(came[p][q][k], 16)

            def final_power(p, q):
                if gelu:
                    pool.wait_ge(var2, QUAD0[p] + q + 1)
                    wide = slice(q * SUB, (q + 1) * SUB)
                    pool.tensor_tensor(rstd2[p][:, wide], ve2[p][:, wide], res["neg_half"][:, wide], ALU.pow).then_inc(rstd2_ready, 1)

            def await_sets(sets):
                pool.wait_ge(stored[0], (sets + 1) // 2 * 16 + 16)
                pool.wait_ge(stored[1], sets // 2 * 16 + 16)

            power(0)
            power(1)
            if slots_zeroed:
                pool.wait_ge(slots_zeroed, 16)
            send(0)
            power(2)
            send(1)
            gate_power(0)
            gate_power(1)
            if gelu:
                power(3)
            send(2)
            gate_power(2)
            if not gelu:
                power(3)
            await_sets(-(-TILE0[1] // SET))
            for q in range(QUADS[0]):
                fetch(0, q)
            send(3)
            gate_power(3)
            if gelu:
                for p in range(PARTS):
                    shift(p)
            await_sets(-(-TILE0[2] // SET))
            for q in range(QUADS[1]):
                fetch(1, q)
            for p in range(2):
                for q in range(QUADS[p]):
                    final_power(p, q)
            for p in range(PARTS):
                pool.wait_ge(sent[p], SENT[p])
            await_sets(-(-TILE0[3] // SET))
            for q in range(QUADS[2]):
                fetch(2, q)
            final_power(2, 0)
            pool.wait_ge(combined, QUAD0[1])
            await_sets(NTILES // SET)
            fetch(3, 0)
            for q in range(1, QUADS[2]):
                final_power(2, q)
            final_power(3, 0)


def state_space(nc, x, res, ident):
    STEPS_OF_TIME = SEQ // TILE
    col = lambda n: res["cols"][:, COL[n]:COL[n] + 1]
    w = lambda n: res["sqT"][:, SQ[n], :]
    with ExitStack() as ctx:
        L = Layer(nc, ctx, "ssm")
        per_batch = lambda n, shape=(P, TILE): [L.sb(f"{n}{b}", list(shape)) for b in range(NB)]
        xn = per_batch("xn", (P, SUB, D))
        xT, u, sg, ab, dt, nbt = (per_batch(n) for n in ("xT", "u", "sg", "ab", "dt", "nbt"))
        h = ab
        carry = per_batch("carry", (P, 1))
        st, mv, ve, rstd = per_batch("st", (P, SUB, 6)), per_batch("mv", (P, SUB, 2)), per_batch("ve", (P, SUB)), per_batch("rstd", (P, SUB))
        bank_a = [L.bank(f"bank_a{b}") for b in range(NB)]
        bank_b = [L.bank(f"bank_b{b}") for b in range(NB)]
        names = ("var_ready", "rstd_ready", "xn_ready", "xt_ps", "xt_ready", "ug_ready", "u_ready", "tanh_done", "sg_done",
                 "dt_ready", "bt_ready", "abs_done", "exp_done", "ln_done", "max_done", "dt_done", "decay_done",
                 "scan_done", "y_ready", "gated", "z_ready", "out_ready", "chain", "held")
        (var_ready, rstd_ready, xn_ready, xt_ps, xt_ready, ug_ready, u_ready, tanh_done, sg_done, dt_ready, bt_ready,
         abs_done, exp_done, ln_done, max_done, dt_done, decay_done, scan_done, y_ready, gated, z_ready, out_ready,
         chain, held) = (L.sem(n) for n in names)
        block = ctx.enter_context(nc.Block())

        @block.tensor
        def _(pe):
            with pe.Fori(0, STEPS_OF_TIME) as k:
                c = k * NB
                for b in range(NB):
                    pe.wait_ge(xn_ready, c + b + 1)
                    for s in range(SUB):
                        last = pe.transpose(bank_a[b][:, s * P:(s + 1) * P], xn[b][:, s, :], ident[:, :])
                    last.then_inc(xt_ps, 1)
                for b in range(NB):
                    pe.wait_ge(xt_ready, c + b + 1)
                    pe.matmul(bank_a[b][:, :], w("Wu"), xT[b][:, :], start=True, stop=True)
                    pe.matmul(bank_b[b][:, :], w("Wgate"), xT[b][:, :], start=True, stop=True).then_inc(ug_ready, 1)
                for b in range(NB):
                    pe.wait_ge(u_ready, c + b + 1)
                    pe.matmul(bank_a[b][:, :], w("Wdt"), u[b][:, :], start=True, stop=True).then_inc(dt_ready, 1)
                    pe.wait_ge(sg_done, c + b + 1)
                    pe.matmul(bank_b[b][:, :], w("Wstate"), u[b][:, :], start=True, stop=True).then_inc(bt_ready, 1)
                for b in range(NB):
                    pe.wait_ge(scan_done, c + b + 1)
                    pe.matmul(bank_a[b][:, :], w("WC"), h[b][:, :], start=True, stop=True).then_inc(y_ready, 1)
                for b in range(NB):
                    pe.wait_ge(z_ready, c + b + 1)
                    for s in range(SUB):
                        last = pe.matmul(bank_b[b][:, s * P:(s + 1) * P], sg[b][:, s * P:(s + 1) * P], w("Wout"), start=True, stop=True)
                    last.then_inc(out_ready, 1)

        @block.scalar
        def _(act):
            with act.Fori(0, STEPS_OF_TIME) as k:
                c = k * NB
                for b in range(NB):
                    act.wait_ge(xt_ps, c + b + 1)
                    act.copy(xT[b][:, :], bank_a[b][:, :]).then_inc(xt_ready, 1)
                for b in range(NB):
                    act.wait_ge(ug_ready, c + b + 1)
                    act.copy(u[b][:, :], bank_a[b][:, :]).then_inc(u_ready, 1)
                    act.activation(sg[b][:, :], bank_b[b][:, :], ACT.Tanh, scale=0.5).then_inc(tanh_done, 1)
                for b in range(NB):
                    act.wait_ge(dt_ready, c + b + 1)
                    act.activation(ab[b][:, :], bank_a[b][:, :], ACT.Abs, bias=col("L0_attn_b_dt")).then_inc(abs_done, 1)
                for b in range(NB):
                    act.wait_ge(abs_done, c + b + 1)
                    act.activation(ab[b][:, :], ab[b][:, :], ACT.Exp, scale=-1.0).then_inc(exp_done, 1)
                for b in range(NB):
                    act.wait_ge(exp_done, c + b + 1)
                    act.activation(ab[b][:, :], ab[b][:, :], ACT.Ln, bias=1.0).then_inc(ln_done, 1)
                for b in range(NB):
                    act.wait_ge(dt_done, c + b + 1)
                    act.activation(dt[b][:, :], dt[b][:, :], ACT.Exp, scale=res["neg_rate"][:, 0:1]).then_inc(decay_done, 1)

        @block.vector
        def _(dve):
            for b in range(NB):
                last = dve.memset(carry[b][:, :], 0.0)
            last.then_inc(chain, 1)
            CHAIN = 5 * NB
            with dve.Fori(0, STEPS_OF_TIME) as k:
                c = k * NB
                ch = Steps(dve, chain, k * CHAIN + 1, held)
                for b in range(NB):
                    for s in range(SUB):
                        last = dve.bn_stats(st[b][:, s, :], of_group(x, k + b * STEPS_OF_TIME, s))
                    ch.step(last)
                ch.settle_apart()
                for b in range(NB):
                    for s in range(SUB):
                        last = dve.bn_aggr(mv[b][:, s, :], st[b][:, s, :])
                    ch.step(last)
                ch.settle()
                for b in range(NB):
                    dve.tensor_scalar(ve[b][:, :], mv[b][:, :, 1], EPS, None, ALU.add).then_inc(var_ready, 1)
                for b in range(NB):
                    dve.wait_ge(rstd_ready, c + b + 1)
                    for s in range(SUB):
                        last = dve.tensor_scalar(xn[b][:, s, :], of_group(x, k + b * STEPS_OF_TIME, s), mv[b][:, s, 0:1],
                                                 rstd[b][:, s:s + 1], ALU.subtract, ALU.mult)
                    last.then_inc(xn_ready, 1)
                for b in range(NB):
                    dve.wait_ge(tanh_done, c + b + 1)
                    dve.scalar_tensor_tensor(sg[b][:, :], sg[b][:, :], 1.0, bank_b[b][:, :], ALU.add, ALU.mult).then_inc(sg_done, 1)
                for b in range(NB):
                    dve.wait_ge(dt_ready, c + b + 1)
                    dve.wait_ge(abs_done, c + b + 1)
                    dve.tensor_scalar(dt[b][:, :], bank_a[b][:, :], col("L0_attn_b_dt"), 0.0, ALU.add, ALU.max).then_inc(max_done, 1)
                for b in range(NB):
                    dve.wait_ge(ln_done, c + b + 1)
                    dve.wait_ge(max_done, c + b + 1)
                    dve.tensor_tensor(dt[b][:, :], dt[b][:, :], ab[b][:, :], ALU.add).then_inc(dt_done, 1)
                for b in range(NB):
                    dve.wait_ge(decay_done, c + b + 1)
                    ch.step(dve.tensor_scalar(dt[b][:, :], dt[b][:, :], res["floor"][:, 0:1], 1.0, ALU.max, ALU.min))
                for b in range(NB):
                    dve.wait_ge(bt_ready, c + b + 1)
                    ch.settle()
                    ch.step(dve.scalar_tensor_tensor(nbt[b][:, :], dt[b][:, :], 1.0, bank_b[b][:, :], ALU.subtract, ALU.mult))
                for b in range(NB):
                    ch.settle()
                    dve.tensor_tensor_scan(h[b][:, :], dt[b][:, :], nbt[b][:, :], carry[b][:, 0:1], ALU.mult, ALU.subtract)\
                        .then_inc(scan_done, 1)
                for b in range(NB):
                    dve.wait_ge(scan_done, c + b + 1)
                    ch.step(dve.tensor_copy(carry[b][:, :], h[b][:, TILE - 1:TILE]))
                for b in range(NB):
                    dve.wait_ge(y_ready, c + b + 1)
                    dve.scalar_tensor_tensor(sg[b][:, :], bank_a[b][:, :], 0.5, sg[b][:, :], ALU.mult, ALU.mult).then_inc(gated, 1)
                for b in range(NB):
                    dve.wait_ge(gated, c + b + 1)
                    dve.scalar_tensor_tensor(sg[b][:, :], xT[b][:, :], col("L0_attn_D"), sg[b][:, :], ALU.mult, ALU.add)\
                        .then_inc(z_ready, 1)
                for b in range(NB):
                    dve.wait_ge(out_ready, c + b + 1)
                    xt = of_tile(x, k + b * STEPS_OF_TIME)
                    dve.tensor_tensor(xt, xt, bank_b[b][:, :].rearrange("p (s d) -> p s d", s=SUB), ALU.add)
                assert ch.n == CHAIN

        @block.gpsimd
        def _(pool):
            with pool.Fori(0, STEPS_OF_TIME) as k:
                for b in range(NB):
                    pool.wait_ge(var_ready, k * NB + b + 1)
                    pool.tensor_tensor(rstd[b][:, :], ve[b][:, :], res["neg_half"][:, 0:SUB], ALU.pow).then_inc(rstd_ready, 1)


def receptance(nc, x, res, ident, block_diag):
    STEPS_OF_TIME = SEQ // TILE
    col = lambda n: res["cols"][:, COL[n]:COL[n] + 1]
    w = lambda n: res["sqT"][:, SQ[n], :]
    with ExitStack() as ctx:
        L = Layer(nc, ctx, "rwkv")
        per_batch = lambda n, shape=(P, TILE): [L.sb(f"{n}{b}", list(shape)) for b in range(NB)]
        xn = per_batch("xn", (P, SUB, D))
        xT = per_batch("xT", (P, TILE + 1))
        spare = lambda n: [res[n][:, :, :].rearrange("p a b -> p (a b)")[:, b * TILE:(b + 1) * TILE] for b in range(NB)]
        dx, lx = spare("raw_s1"), spare("raw_s3")
        tw = per_batch("tw", (P, 3, TILE + 1))
        q = {p: per_batch("q" + p) for p in LORAS}
        v = spare("raw_s2")
        carry = per_batch("carry", (P, HD))
        st, mv, ve, rstd = per_batch("st", (P, SUB, 6)), per_batch("mv", (P, SUB, 2)), per_batch("ve", (P, SUB)), per_batch("rstd", (P, SUB))
        bank_a = [L.bank(f"bank_a{b}") for b in range(NB)]
        bank_b = [L.bank(f"bank_b{b}") for b in range(NB)]
        S = {}
        for n in ("var_ready", "rstd_ready", "xn_ready", "xt_ps", "xt_ready", "dx_ready", "lx_ready", "la_rk", "la_vg", "la_d",
                  "tanh_rk", "tanh_vg", "tanh_d", "lb_ready", "scaled", "xin_ready", "proj_ready", "copied", "tanh_g", "sg_done",
                  "la_d2", "tanh_d2", "lb_d2", "exp1", "w_ready", "ruk_done", "bonus_ps", "bonus_done",
                  "ve_ready", "kv_done", "scan_done", "carried", "m_done", "sum_done", "y_done", "centred", "squared", "var_ps",
                  "ln_done", "rs_done", "normed", "shifted", "o_ready", "out_ready", "chain", "held", "acts"):
            S[n] = L.sem(n)
        block = ctx.enter_context(nc.Block())
        NP = len(LORAS)
        mid = lambda b: xT[b][:, 1:TILE + 1]
        y = [xn[b][:, :, :].rearrange("p s d -> p (s d)") for b in range(NB)]
        T = lambda b, k: tw[b][:, k, 0:TILE]

        @block.tensor
        def _(pe):
            with pe.Fori(0, STEPS_OF_TIME) as k:
                c = k * NB
                for b in range(NB):
                    pe.wait_ge(S["xn_ready"], c + b + 1)
                    for s in range(SUB):
                        last = pe.transpose(bank_a[b][:, s * P:(s + 1) * P], xn[b][:, s, :], ident[:, :])
                    last.then_inc(S["xt_ps"], 1)
                for b in range(NB):
                    pe.wait_ge(S["lx_ready"], c + b + 1)
                    pe.matmul(bank_a[b][:, :], res["laT"][:, 0, :], lx[b][:, :], start=True, stop=True).then_inc(S["la_rk"], 1)
                    pe.matmul(bank_b[b][:, :], res["laT"][:, 1, :], lx[b][:, :], start=True, stop=True).then_inc(S["la_vg"], 1)
                for b in range(NB):
                    pe.wait_ge(S["tanh_rk"], c + b + 1)
                    pe.matmul(bank_a[b][0:LORA, :], res["laT"][:, 2, 0:LORA], lx[b][:, :], start=True, stop=True).then_inc(S["la_d"], 1)

                def expand(n, p):
                    pair, half = LA[p]
                    rows = slice(half * LORA, (half + 1) * LORA)
                    for b in range(NB):
                        if n == 0:
                            pe.wait_ge(S["tanh_d"], c + b + 1)
                        else:
                            pe.wait_ge(S["scaled"], k * (NP * NB) + (n - 1) * NB + b + 1)
                        pe.matmul(bank_a[b][:, :], res["lbT"][rows, pair, :], tw[b][rows, pair, 0:TILE], start=True, stop=True)\
                            .then_inc(S["lb_ready"], 1)

                def project(n, p):
                    for b in range(NB):
                        pe.wait_ge(S["xin_ready"], k * (NP * NB) + n * NB + b + 1)
                        if n == 0:
                            pe.wait_ge(S["tanh_vg"], c + b + 1)
                        else:
                            pe.wait_ge(S["copied"], k * (3 * NB) + (n - 1) * NB + b + 1)
                        pe.matmul(bank_b[b][:, :], w(p + "W"), q[p][b][:, :], start=True, stop=True).then_inc(S["proj_ready"], 1)

                for n, p in enumerate(LORAS):
                    expand(n, p)
                    if n >= 1:
                        project(n - 1, LORAS[n - 1])
                for b in range(NB):
                    pe.wait_ge(S["xin_ready"], k * (NP * NB) + 4 * NB + b + 1)
                    pe.matmul(bank_a[b][0:LORA, :], res["laT"][:, 2, 0:LORA], q["d"][b][:, :], start=True, stop=True).then_inc(S["la_d2"], 1)
                for b in range(NB):
                    pe.wait_ge(S["tanh_d2"], c + b + 1)
                    pe.wait_ge(S["sg_done"], c + b + 1)
                    pe.matmul(bank_b[b][:, :], res["lbT"][0:LORA, 2, :], tw[b][0:LORA, 2, 0:TILE], start=True, stop=True).then_inc(S["lb_d2"], 1)
                for b in range(NB):
                    pe.wait_ge(S["ruk_done"], c + b + 1)
                    pe.matmul(bank_a[b][:, :], block_diag[:, :], lx[b][:, :], start=True, stop=True).then_inc(S["bonus_ps"], 1)

                def values(j):
                    for b in range(NB):
                        if j == 0:
                            pe.wait_ge(S["bonus_done"], c + b + 1)
                        else:
                            pe.wait_ge(S["kv_done"], k * (HD * NB) + (j - 1) * NB + b + 1)
                        pe.matmul(bank_a[b][:, :], res["v_each"][:, j, :], q["v"][b][:, :], start=True, stop=True).then_inc(S["ve_ready"], 1)

                def head_sums(j):
                    for b in range(NB):
                        pe.wait_ge(S["m_done"], k * (HD * NB) + j * NB + b + 1)
                        pe.matmul(bank_b[b][:, :], res["sel"][:, j, :], T(b, 2), start=j == 0, stop=j == HD - 1).then_inc(S["sum_done"], 1)

                for j in range(HD):
                    values(j)
                    if j >= 1:
                        head_sums(j - 1)
                head_sums(HD - 1)
                for b in range(NB):
                    pe.wait_ge(S["y_done"], c + b + 1)
                    pe.matmul(bank_a[b][:, :], res["head_centre"][:, :], y[b], start=True, stop=True).then_inc(S["centred"], 1)
                for b in range(NB):
                    pe.wait_ge(S["squared"], c + b + 1)
                    pe.matmul(bank_b[b][:, :], res["head_mean"][:, :], lx[b][:, :], start=True, stop=True).then_inc(S["var_ps"], 1)
                for b in range(NB):
                    pe.wait_ge(S["o_ready"], c + b + 1)
                    for s in range(SUB):
                        last = pe.matmul(bank_b[b][:, s * P:(s + 1) * P], y[b][:, s * P:(s + 1) * P], w("oW"), start=True, stop=True)
                    last.then_inc(S["out_ready"], 1)

        @block.scalar
        def _(act):
            for b in range(NB):
                last = act.activation(xT[b][:, TILE:TILE + 1], ident[:, 0:1], ACT.Copy, scale=0.0)
            last.then_inc(S["acts"], 1)
            act.wait_ge(S["acts"], 1)
            with act.Fori(0, STEPS_OF_TIME) as k:
                c = k * NB
                for b in range(NB):
                    act.wait_ge(S["xt_ps"], c + b + 1)
                    act.copy(xT[b][:, 0:1], xT[b][:, TILE:TILE + 1]).then_inc(S["acts"], 1)
                for b in range(NB):
                    act.wait_ge(S["acts"], c + b + 2)
                    act.copy(mid(b), bank_a[b][:, :]).then_inc(S["xt_ready"], 1)
                for b in range(NB):
                    act.wait_ge(S["la_rk"], c + b + 1)
                    act.activation(T(b, 0), bank_a[b][:, :], ACT.Tanh).then_inc(S["tanh_rk"], 1)
                    act.wait_ge(S["la_vg"], c + b + 1)
                    act.activation(T(b, 1), bank_b[b][:, :], ACT.Tanh).then_inc(S["tanh_vg"], 1)
                for b in range(NB):
                    act.wait_ge(S["la_d"], c + b + 1)
                    act.activation(tw[b][0:LORA, 2, 0:TILE], bank_a[b][0:LORA, :], ACT.Tanh).then_inc(S["tanh_d"], 1)
                for n, p in enumerate("rkv"):
                    for b in range(NB):
                        act.wait_ge(S["proj_ready"], k * (4 * NB) + n * NB + b + 1)
                        act.copy({"r": q["r"], "k": q["k"], "v": v}[p][b][:, :], bank_b[b][:, :]).then_inc(S["copied"], 1)
                for b in range(NB):
                    act.wait_ge(S["proj_ready"], k * (4 * NB) + 3 * NB + b + 1)
                    act.activation(q["g"][b][:, :], bank_b[b][:, :], ACT.Tanh, scale=0.5).then_inc(S["tanh_g"], 1)
                for b in range(NB):
                    act.wait_ge(S["la_d2"], c + b + 1)
                    act.activation(tw[b][0:LORA, 2, 0:TILE], bank_a[b][0:LORA, :], ACT.Tanh).then_inc(S["tanh_d2"], 1)
                for b in range(NB):
                    act.wait_ge(S["lb_d2"], c + b + 1)
                    act.activation(q["d"][b][:, :], bank_b[b][:, :], ACT.Exp, bias=col("L1_attn_d_ll")).then_inc(S["exp1"], 1)
                for b in range(NB):
                    act.wait_ge(S["exp1"], c + b + 1)
                    act.activation(q["d"][b][:, :], q["d"][b][:, :], ACT.Exp, scale=-1.0).then_inc(S["w_ready"], 1)
                for b in range(NB):
                    act.wait_ge(S["centred"], c + b + 1)
                    act.activation(lx[b][:, :], bank_a[b][:, :], ACT.Square).then_inc(S["squared"], 1)
                for b in range(NB):
                    act.wait_ge(S["var_ps"], c + b + 1)
                    act.activation(lx[b][:, :], bank_b[b][:, :], ACT.Ln, bias=res["eps"][:, 0:1]).then_inc(S["ln_done"], 1)
                for b in range(NB):
                    act.wait_ge(S["ln_done"], c + b + 1)
                    act.activation(lx[b][:, :], lx[b][:, :], ACT.Exp, scale=-0.5).then_inc(S["rs_done"], 1)

        @block.vector
        def _(dve):
            for b in range(NB):
                last = dve.tensor_copy(carry[b][:, :], res["state0"][:, :])
            last.then_inc(S["chain"], 1)
            CHAIN = (2 + HD) * NB
            with dve.Fori(0, STEPS_OF_TIME) as k:
                c = k * NB
                ch = Steps(dve, S["chain"], k * CHAIN + 1, S["held"])
                for b in range(NB):
                    for s in range(SUB):
                        last = dve.bn_stats(st[b][:, s, :], of_group(x, k + b * STEPS_OF_TIME, s))
                    ch.step(last)
                ch.settle_apart()
                for b in range(NB):
                    for s in range(SUB):
                        last = dve.bn_aggr(mv[b][:, s, :], st[b][:, s, :])
                    ch.step(last)
                ch.settle()
                for b in range(NB):
                    dve.tensor_scalar(ve[b][:, :], mv[b][:, :, 1], EPS, None, ALU.add).then_inc(S["var_ready"], 1)
                for b in range(NB):
                    dve.wait_ge(S["rstd_ready"], c + b + 1)
                    for s in range(SUB):
                        last = dve.tensor_scalar(xn[b][:, s, :], of_group(x, k + b * STEPS_OF_TIME, s), mv[b][:, s, 0:1],
                                                 rstd[b][:, s:s + 1], ALU.subtract, ALU.mult)
                    last.then_inc(S["xn_ready"], 1)
                for b in range(NB):
                    dve.wait_ge(S["xt_ready"], c + b + 1)
                    dve.tensor_tensor(dx[b][:, :], xT[b][:, 0:TILE], mid(b), ALU.subtract).then_inc(S["dx_ready"], 1)
                for b in range(NB):
                    dve.wait_ge(S["dx_ready"], c + b + 1)
                    dve.scalar_tensor_tensor(lx[b][:, :], dx[b][:, :], col("L1_attn_xw"), mid(b), ALU.mult, ALU.add).then_inc(S["lx_ready"], 1)

                def mix(n, p):
                    for b in range(NB):
                        dve.wait_ge(S["lb_ready"], k * (NP * NB) + n * NB + b + 1)
                        dve.scalar_tensor_tensor(q[p][b][:, :], bank_a[b][:, :], col(f"L1_attn_{p}_ll"), dx[b][:, :], ALU.add, ALU.mult)\
                            .then_inc(S["scaled"], 1)

                for n, p in enumerate(LORAS):
                    mix(n, p)
                    if n == 4:
                        for b in range(NB):
                            dve.wait_ge(S["copied"], k * (3 * NB) + 2 * NB + b + 1)
                            dve.scalar_tensor_tensor(lx[b][:, :], q["r"][b][:, :], col("L1_attn_u"), q["k"][b][:, :], ALU.mult, ALU.mult)\
                                .then_inc(S["ruk_done"], 1)
                for b in range(NB):
                    dve.wait_ge(S["tanh_g"], c + b + 1)
                    dve.scalar_tensor_tensor(q["g"][b][:, :], q["g"][b][:, :], 1.0, bank_b[b][:, :], ALU.add, ALU.mult).then_inc(S["sg_done"], 1)
                for b in range(NB):
                    dve.wait_ge(S["bonus_ps"], c + b + 1)
                    dve.tensor_tensor(v[b][:, :], v[b][:, :], bank_a[b][:, :], ALU.mult).then_inc(S["bonus_done"], 1)
                for j in range(HD):
                    n = k * (HD * NB) + j * NB
                    for b in range(NB):
                        dve.wait_ge(S["ve_ready"], n + b + 1)
                        dve.tensor_tensor(dx[b][:, :], q["k"][b][:, :], bank_a[b][:, :], ALU.mult).then_inc(S["kv_done"], 1)
                        if j >= 2:
                            dve.wait_ge(S["m_done"], k * (HD * NB) + (j - 2) * NB + b + 1)
                        ch.step(dve.tensor_copy(tw[b][:, j % 2, 0:1], carry[b][:, j:j + 1]))
                    for b in range(NB):
                        if j == 0:
                            dve.wait_ge(S["w_ready"], c + b + 1)
                        dve.wait_ge(S["kv_done"], n + b + 1)
                        dve.tensor_tensor_scan(tw[b][:, j % 2, 1:TILE + 1], q["d"][b][:, :], dx[b][:, :], carry[b][:, j:j + 1],
                                               ALU.mult, ALU.add).then_inc(S["scan_done"], 1)
                    for b in range(NB):
                        dve.wait_ge(S["scan_done"], n + b + 1)
                        dve.tensor_copy(carry[b][:, j:j + 1], tw[b][:, j % 2, TILE:TILE + 1]).then_inc(S["carried"], 1)
                for b in range(NB):
                    dve.wait_ge(S["sum_done"], k * (HD * NB) + (HD - 1) * NB + b + 1)
                    dve.tensor_tensor(y[b], bank_b[b][:, :], v[b][:, :], ALU.add).then_inc(S["y_done"], 1)
                for b in range(NB):
                    dve.wait_ge(S["rs_done"], c + b + 1)
                    dve.tensor_tensor(y[b], bank_a[b][:, :], lx[b][:, :], ALU.mult).then_inc(S["normed"], 1)
                for b in range(NB):
                    dve.wait_ge(S["normed"], c + b + 1)
                    dve.tensor_scalar(y[b], y[b], res["cols"][:, COL_LNW:COL_LNW + 1], res["cols"][:, COL_LNB:COL_LNB + 1],
                                      ALU.mult, ALU.add).then_inc(S["shifted"], 1)
                for b in range(NB):
                    dve.wait_ge(S["shifted"], c + b + 1)
                    dve.scalar_tensor_tensor(y[b], q["g"][b][:, :], 0.5, y[b], ALU.mult, ALU.mult).then_inc(S["o_ready"], 1)
                for b in range(NB):
                    dve.wait_ge(S["out_ready"], c + b + 1)
                    xt = of_tile(x, k + b * STEPS_OF_TIME)
                    dve.tensor_tensor(xt, xt, bank_b[b][:, :].rearrange("p (s d) -> p s d", s=SUB), ALU.add)
                assert ch.n == CHAIN

        @block.gpsimd
        def _(pool):
            with pool.Fori(0, STEPS_OF_TIME) as k:
                for b in range(NB):
                    pool.wait_ge(S["var_ready"], k * NB + b + 1)
                    pool.tensor_tensor(rstd[b][:, :], ve[b][:, :], res["neg_half"][:, 0:SUB], ALU.pow).then_inc(S["rstd_ready"], 1)
                for n, p in enumerate(LORAS):
                    for b in range(NB):
                        pool.wait_ge(S["scaled"], k * (NP * NB) + n * NB + b + 1)
                        pool.tensor_tensor(q[p][b][:, :], q[p][b][:, :], mid(b), ALU.add).then_inc(S["xin_ready"], 1)
                for j in range(HD):
                    n = k * (HD * NB) + j * NB
                    for b in range(NB):
                        pool.wait_ge(S["scan_done"], n + b + 1)
                        if j >= 1:
                            pool.wait_ge(S["sum_done"], k * (HD * NB) + (j - 1) * NB + b + 1)
                        pool.tensor_tensor(T(b, 2), tw[b][:, j % 2, 0:TILE], q["r"][b][:, :], ALU.mult).then_inc(S["m_done"], 1)


def store(nc, x, out):
    with ExitStack() as ctx:
        stored = Layer(nc, ctx, "store").sem("stored")
        block = ctx.enter_context(nc.Block())

        @block.sync
        def _(sp):
            sp.dma_start(out.rearrange("b (g p) d -> p (b g) d", p=P), x[:, :, :]).then_inc(stored, 16)
            sp.wait_ge(stored, 16)


def build(nc, ins, out, layers=6):
    with ExitStack() as ctx:
        def sb(name, shape, dt=F32):
            return ctx.enter_context(nc.sbuf_tensor(name, shape, dt))

        x = sb("x", [P, NT * SUB, D])
        ident = sb("ident", [P, P])
        block_diag = sb("block_diag", [P, P])
        res = {}
        for n, shape in (("sqT", [P, len(SQUARES), P]), ("laT", [P, 3, P]), ("lbT", [P, 3, P]),
                         ("v_each", [P, HD, P]), ("sel", [P, HD, P]), ("head_mean", [P, P]), ("head_centre", [P, P]),
                         ("state0", [P, HD]), ("neg_rate", [P, 1]), ("floor", [P, 1]), ("eps", [P, 1]), ("neg_half", [P, MOST]),
                         ("e_temp", [P, MOST]), ("e_one", [P, MOST]), ("replace", [P, GROUPS, 8]), ("gate_bias", [P, E]),
                         ("gate0", [P, E]), ("before", [P, P]), ("ones", [P, P]), ("tile_start", [1, MOST_TILES]), ("zeros", [P, 1, D]),
                         ("post_g", [P, D]), ("post_b", [P, D])):
            res[n] = sb(n, shape)
        res["cols"] = res["laT"][:, 2, LORA:LORA + COLS]
        later = {n: nc.alloc_semaphore(name=n) for n in ("slots_zeroed", "swiglu_in", "gelu_in")}
        slots_x = nc.dram_tensor("slots_x", (PLACES, D), F32).ap()
        slots_y = nc.dram_tensor("slots_y", (PLACES, D), F32).ap()
        with ExitStack() as raw:
            for n, shape in (("raw_s1", [P, E * FI // P, D]), ("raw_s3", [P, E * FI // P, D]), ("raw_s2", [P, E, FI])):
                res[n] = raw.enter_context(nc.sbuf_tensor(n, shape, F32))
            with ExitStack() as first:
                for n, shape, dt in (("w1", [P, E, WIDE], F32), ("w2", [P, E * FF // P, D], F32),
                                     ("bias", [LO_ROW + 1, E * D], F32R), ("bias_ones", [LO_ROW + 1, P], F32R)):
                    res[n] = first.enter_context(nc.sbuf_tensor(n, shape, dt))
                setup(nc, ins, x, res, ident, block_diag, slots_x, later)
                rates(nc, res)
                if layers > 0:
                    mixture(nc, "gelu0", "gelu", x, res, ident, slots_x, slots_y, later["slots_zeroed"], later["gelu_in"])
                if layers > 1:
                    state_space(nc, x, res, ident)
                if layers > 2:
                    mixture(nc, "gelu1", "gelu", x, res, ident, slots_x, slots_y)
            for n, shape in (("s13", [P, E, FF]), ("s2", [P, E * FI // P, D])):
                res[n] = raw.enter_context(nc.sbuf_tensor(n, shape, F32))
            if layers > 3:
                swiglu_weights(nc, res, ident, later["swiglu_in"])
                mixture(nc, "swiglu0", "swiglu", x, res, ident, slots_x, slots_y)
            if layers > 4:
                receptance(nc, x, res, ident, block_diag)
            if layers > 5:
                mixture(nc, "swiglu1", "swiglu", x, res, ident, slots_x, slots_y)
        store(nc, x, out)


_INS = ["L0_attn_x", "L0_attn_W_in", "L0_attn_W_state", "L0_attn_W_dt", "L0_attn_b_dt", "L0_attn_A_log", "L0_attn_W_C",
        "L0_attn_D", "L0_attn_W_out", "L0_ffn_gate_w", "L0_ffn_gate_b", "L0_ffn_w1", "L0_ffn_b1", "L0_ffn_w2", "L0_ffn_b2",
        "L0_ffn_ln_g", "L0_ffn_ln_b", "L1_attn_xw", "L1_attn_rW", "L1_attn_kW", "L1_attn_vW", "L1_attn_gW",
        "L1_attn_r_la", "L1_attn_r_lb", "L1_attn_r_ll", "L1_attn_k_la", "L1_attn_k_lb", "L1_attn_k_ll",
        "L1_attn_v_la", "L1_attn_v_lb", "L1_attn_v_ll", "L1_attn_g_la", "L1_attn_g_lb", "L1_attn_g_ll",
        "L1_attn_d_la", "L1_attn_d_lb", "L1_attn_d_ll", "L1_attn_ln_w", "L1_attn_ln_b", "L1_attn_oW",
        "L1_attn_init_state", "L1_attn_u", "L1_ffn_wg", "L1_ffn_w1", "L1_ffn_w3", "L1_ffn_w2"]


def kernel(**inputs):
    import numpy as _np
    import concourse.bacc as _bacc
    from concourse import mybir as _mybir
    from concourse.bass_utils import run_bass_kernel_spmd as _run

    nc = _bacc.Bacc("TRN2", target_bir_lowering=False, num_devices=1)
    arrays, aps = {}, {}
    given = {n: _np.ascontiguousarray(inputs[n]) for n in _INS}
    given["const_ident"] = _np.eye(P, dtype=_np.float32)
    given["const_block"] = _np.kron(_np.eye(HEADS, dtype=_np.float32), _np.ones((HD, HD), _np.float32))
    given["const_before"] = _np.triu(_np.ones((P, P), _np.float32), 1)
    given["const_tile_start"] = (P * _np.arange(MOST_TILES, dtype=_np.float32)).reshape(1, -1)
    given["b1_columns"] = _np.ascontiguousarray(given.pop("L0_ffn_b1").reshape(E, FF // P, P).transpose(2, 0, 1))
    for n, a in given.items():
        arrays[f"in_{n}"] = a
        aps[n] = nc.dram_tensor(f"in_{n}", a.shape, _mybir.dt.from_np(a.dtype), kind="ExternalInput").ap()
    out = nc.dram_tensor("out_x", (NB, SEQ, D), F32, kind="ExternalOutput").ap()
    build(nc, aps, out)
    r = _run(nc, [arrays], core_ids=[0])
    return r.results[0]["out_x"]
```

```python
from contextlib import ExitStack

import concourse.bass as bass
from concourse import mybir

F32 = mybir.dt.float32
F32R = mybir.dt.float32r
I32 = mybir.dt.int32
AX = mybir.AxisListType
ALU = mybir.AluOpType
ACT = mybir.ActivationFunctionType

P = 128
D = 128
NB, SEQ = 4, 1024
TOK = NB * SEQ
TILE = 512
SUB = TILE // P
NT = TOK // TILE
PAIRS = NT // 2
E = 8
FF = 512
FI = 256
WIDE = FF + FF // P
assert 2 * FI == FF
HEADS, HD = 16, 8
LORA = 64
EPS = 1e-5
TEMP = 0.9
DT_MAX = 10.0
RATE_EPS = 1e-4
BIG = 3.0e38
TOP = 2
GROUPS = TOK // P
PARTS_OF = {"gelu": (4, 12, 12, 4), "swiglu": (8, 12, 8, 4)}
PARTS = 4
EARLY = 2
MOST = max(max(groups) for groups in PARTS_OF.values())
BODY = 4
UNROLL = 2


def tiles_of(groups):
    tiles = [(g * P * TOP + E * (P - 1)) // P for g in groups]
    tiles[-1] += -sum(tiles) % BODY
    return tiles


PLACES = P * max(sum(tiles_of(groups)) for groups in PARTS_OF.values())
MOST_TILES = max(max(tiles_of(groups)) for groups in PARTS_OF.values())

VECTORS = ["L0_attn_b_dt", "L0_attn_A_log", "L0_attn_D", "L1_attn_xw", "L1_attn_r_ll", "L1_attn_k_ll",
           "L1_attn_v_ll", "L1_attn_g_ll", "L1_attn_d_ll", "L1_attn_u"]
COL = {n: i for i, n in enumerate(VECTORS)}
COL_WG = len(VECTORS)
COL_LNW = COL_WG + E
COL_LNB = COL_LNW + 1
COLS = COL_LNB + 1

SQUARES = ["Wu", "Wgate", "Wstate", "Wdt", "WC", "Wout", "rW", "kW", "vW", "gW", "oW"]
LORAS = "rkvgd"
SQ = {n: i for i, n in enumerate(SQUARES)}
LA = {"r": (0, 0), "k": (0, 1), "v": (1, 0), "g": (1, 1), "d": (2, 0)}


class Steps:

    def __init__(self, eng, sem, before, held=None):
        self.eng, self.sem, self.before, self.held, self.n = eng, sem, before, held, 0

    def step(self, ins):
        ins.then_inc(self.sem, 1)
        self.n += 1

    def settle(self):
        self.eng.wait_ge(self.sem, self.before + self.n)

    def settle_apart(self):
        self.settle()
        self.eng.sem_inc(self.held, 1)


class Layer:

    def __init__(self, nc, ctx, name):
        self.nc, self.ctx, self.name, self.sems = nc, ctx, name, []
        ctx.callback(self.clear)

    def sb(self, name, shape, dt=F32):
        return self.ctx.enter_context(self.nc.sbuf_tensor(f"{self.name}_{name}", shape, dt))

    def bank(self, name):
        return self.ctx.enter_context(self.nc.psum_tensor(f"{self.name}_{name}", [P, TILE], F32))

    def sem(self, name):
        self.sems.append(self.nc.alloc_semaphore(name=f"{self.name}_{name}"))
        return self.sems[-1]

    def clear(self):
        self.nc.clear_and_free_semaphores(self.sems)
        self.nc.all_engine_barrier()


def row(ap):
    return ap.rearrange("(a n) -> a n", a=1)


def of_tile(x, t):
    return x[:, bass.ds(t * SUB, SUB), :]


def of_group(x, t, s):
    return x[:, bass.ds(t * SUB + s, 1), :].rearrange("p a d -> p (a d)")


def clear(eng, res, slots_x, p, later):
    tiles = tiles_of(PARTS_OF["gelu"])
    start = sum(tiles[:p])
    n = tiles[p] if p < PARTS - 1 else PLACES // P - start
    eng.dma_start(slots_x[start * P:(start + n) * P, :].rearrange("(t p) d -> p t d", p=P),
                  res["zeros"][:, :, :].broadcast_to([P, n, D])).then_inc(later[f"slots_zeroed{p}"], 16)


def setup(nc, ins, x, res, ident, slots_x, later):
    with ExitStack() as ctx:
        L = Layer(nc, ctx, "setup")
        first_in = L.sem("first_in")
        small_in = L.sem("small_in")
        ready = L.sem("ready")
        block = ctx.enter_context(nc.Block())
        FIRST = PARTS_OF["gelu"][0]
        SMALL = 16 * 7

        @block.sync
        def _(sp):
            tokens = ins["L0_attn_x"].rearrange("b (g p) d -> p (b g) d", p=P)

            def small(dst, src):
                sp.dma_start(dst, src).then_inc(small_in, 16)

            sp.dma_start(x[:, 0:FIRST, :], tokens[:, 0:FIRST, :]).then_inc(first_in, 16)
            small(ident[:, :], ins["const_ident"])
            small(res["gate0"][:, :], ins["L0_ffn_gate_w"])
            small(res["gate_bias"][:, :], row(ins["L0_ffn_gate_b"]).broadcast_to([P, E]))
            small(res["before"][:, :], ins["const_before"])
            small(res["tile_start"][:, :], ins["const_tile_start"])
            small(res["post_g"][:, :], row(ins["L0_ffn_ln_g"]).broadcast_to([P, D]))
            small(res["post_b"][:, :], row(ins["L0_ffn_ln_b"]).broadcast_to([P, D]))
            sp.wait_ge(ready, 1)
            clear(sp, res, slots_x, 0, later)
            sp.dma_start(x[:, FIRST:, :], tokens[:, FIRST:, :]).then_inc(later["x_in"], 16)
            clear(sp, res, slots_x, 1, later)
            sp.dma_start(res["w1"][:, :, 0:FF], ins["L0_ffn_w1"].rearrange("e d f -> d e f")).then_inc(later["gelu_in"], 16)
            sp.dma_start(res["w1"][:, :, FF:WIDE], ins["b1_columns"]).then_inc(later["gelu_in"], 16)
            sp.dma_start(res["w2"][:, :, :], ins["L0_ffn_w2"].rearrange("e (c p) d -> p (e c) d", p=P)).then_inc(later["gelu_in"], 16)
            sp.dma_start(res["bias"][:, :], ins["L0_ffn_b2"].rearrange("(a e) f -> a (e f)", a=1).broadcast_to([P, E * D])).then_inc(later["bias_in"], 16)
            sp.wait_ge(first_in, 16)

        @block.gpsimd
        def _(pool):
            pool.memset(res["zeros"][:, :, :], 0.0)
            pool.memset(res["ones"][:, :], 1.0).then_inc(ready, 1)
            pool.memset(res["replace"][:, :, :], BIG)
            pool.memset(res["neg_half"][:, :], -0.5)
            pool.memset(res["e_temp"][:, :], float(2.718281828459045 ** (1.0 / TEMP)))
            pool.memset(res["eps"][:, :], EPS)
            pool.memset(res["e_one"][:, :], 2.718281828459045)
            pool.wait_ge(small_in, SMALL)
            for n in ("post_g", "post_b"):
                pool.tensor_scalar_mul(res[n][:, :], res[n][:, :], 0.5)


QUARTERS = 4
ATTENTION_LOADS = 1 + 1 + 9 + 2 * len(LORAS) + 1 + 2 + len(VECTORS) + 1


def attention_loads(ins, res, block_diag, later):
    raw_sq, raw_la, raw_lb = (res[n] for n in ("raw_sq", "raw_la", "raw_lb"))
    raw_cols = raw_la[LORA:LORA + COLS, 2, :]

    loads = []

    def load(dst, src, sem="attention_in"):
        loads.append(lambda eng: eng.dma_start(dst, src).then_inc(later[sem], 16))

    load(block_diag[:, :], ins["const_block"])
    load(raw_sq[:, 0:2, :], ins["L0_attn_W_in"].rearrange("(a p) d -> p a d", p=P))
    for k, n in enumerate(("L0_attn_W_state", "L0_attn_W_dt", "L0_attn_W_C", "L0_attn_W_out", "L1_attn_rW",
                           "L1_attn_kW", "L1_attn_vW", "L1_attn_gW", "L1_attn_oW")):
        load(raw_sq[:, 2 + k, :], ins[n])
    for q in LORAS:
        pair, half = LA[q]
        load(raw_la[half * LORA:(half + 1) * LORA, pair, :], ins[f"L1_attn_{q}_la"])
        load(raw_lb[:, pair, half * LORA:(half + 1) * LORA], ins[f"L1_attn_{q}_lb"])
    load(res["state0"][:, :], ins["L1_attn_init_state"].rearrange("h i j -> (h i) j"))
    for c, n in ((COL_LNW, "L1_attn_ln_w"), (COL_LNB, "L1_attn_ln_b")):
        load(raw_cols[c:c + 1, :].rearrange("a (h j) -> a h j", j=HD),
             ins[n].rearrange("(a b j) -> a b j", a=1, b=1).broadcast_to([1, HEADS, HD]))
    for n in VECTORS:
        load(raw_cols[COL[n]:COL[n] + 1, :], row(ins[n]))
    load(raw_cols[COL_WG:COL_WG + E, :], ins["L1_ffn_wg"])
    assert len(loads) == ATTENTION_LOADS
    for first in range(0, E, E // QUARTERS):
        es, rows = slice(first, first + E // QUARTERS), slice(first * FI // P, (first + E // QUARTERS) * FI // P)
        for n, w in (("raw_s1", "L1_ffn_w1"), ("raw_s3", "L1_ffn_w3")):
            load(res[n][:, rows, :], ins[w][es].rearrange("e (c p) h -> p (e c) h", p=P), "swiglu_in")
        load(res["raw_s2"][:, es, :], ins["L1_ffn_w2"][es].rearrange("e h i -> h e i"), "swiglu_in")
    return loads


def attention_weights(nc, L, res, ident, block_diag, attention_in):
    raw_sq, raw_la, raw_lb = (res[n] for n in ("raw_sq", "raw_la", "raw_lb"))
    row_of_j = L.sb("row_of_j", [P, HD])
    t1, t2, t3 = (L.sb(n, [P, 1]) for n in ("t1", "t2", "t3"))
    weight_turned = L.sem("weight_turned")
    weight_copied = L.sem("weight_copied")
    acted, summed = L.sem("acted"), L.sem("summed")
    split, misc = L.sem("split"), L.sem("misc")

    jobs = [(raw_la[0:LORA + COLS, 2, :], res["laT"][:, 2, 0:LORA + COLS], LORA + COLS, P)]
    jobs += [(raw_la[:, k, :], res["laT"][:, k, :], P, P) for k in range(2)]
    jobs += [(raw_lb[:, k, :], res["lbT"][:, k, :], P, P) for k in range(2)]
    jobs += [(raw_lb[:, 2, 0:LORA], res["lbT"][0:LORA, 2, :], P, LORA)]
    jobs += [(raw_sq[:, k, :], res["sqT"][:, k, :], P, P) for k in range(len(SQUARES))]
    a_log = res["cols"][:, COL["L0_attn_A_log"]:COL["L0_attn_A_log"] + 1]
    place = lambda banks, k: banks[k // 4][0:jobs[k][3], (k % 4) * P:(k % 4) * P + jobs[k][2]]

    def transposes(pe, banks):
        assert len(jobs) <= 4 * len(banks)
        pe.wait_ge(attention_in, 16 * ATTENTION_LOADS)
        for k, (src, _dst, rows, _cols) in enumerate(jobs):
            pe.transpose(place(banks, k), src, ident[0:rows, 0:rows]).then_inc(weight_turned, 1)

    def copies(act, banks):
        for k, (_src, dst, _rows, _cols) in enumerate(jobs):
            act.wait_ge(weight_turned, min((k // 4 + 1) * 4, len(jobs)))
            act.copy(dst, place(banks, k)).then_inc(weight_copied, 1)

    def rates(act):
        act.wait_ge(weight_copied, 1)
        act.activation(t1[:, :], a_log, ACT.Abs).then_inc(acted, 1)
        act.wait_ge(acted, 1)
        act.activation(t2[:, :], t1[:, :], ACT.Exp, scale=-1.0).then_inc(acted, 1)
        act.wait_ge(acted, 2)
        act.activation(t3[:, :], t2[:, :], ACT.Ln, bias=1.0).then_inc(acted, 1)
        act.wait_ge(summed, 2)
        act.activation(res["floor"][:, :], res["neg_rate"][:, :], ACT.Exp, scale=DT_MAX).then_inc(acted, 1)

    def spreads(dve):
        dve.wait_ge(attention_in, 16 * ATTENTION_LOADS)
        dve.tensor_reduce(row_of_j[:, :], ident[:, :].rearrange("p (h j) -> p j h", j=HD), AX.X, ALU.add).then_inc(split, 1)
        dve.wait_ge(split, 1)
        for j in range(HD):
            dve.tensor_scalar(res["spread"][:, j, :], block_diag[:, :], row_of_j[:, j:j + 1], None, ALU.mult)

    def negated(dve):
        dve.wait_ge(acted, 3)
        dve.scalar_tensor_tensor(t1[:, :], a_log, 0.0, t3[:, :], ALU.max, ALU.add).then_inc(summed, 1)
        dve.wait_ge(summed, 1)
        dve.tensor_scalar(res["neg_rate"][:, :], t1[:, :], RATE_EPS, -1.0, ALU.add, ALU.mult).then_inc(summed, 1)

    def head_matrices(pool):
        pool.wait_ge(attention_in, 16 * ATTENTION_LOADS)
        pool.memset(res["sel"][:, :, :], 0.0).then_inc(misc, 1)
        pool.wait_ge(misc, 1)
        for j in range(HD):
            pool.tensor_copy(res["sel"][:, j, :].rearrange("p (h j) -> p h j", j=HD)[:, :, j],
                             block_diag[:, :].rearrange("p (h j) -> p h j", j=HD)[:, :, j]).then_inc(misc, 1)
        pool.tensor_scalar_mul(res["head_mean"][:, :], block_diag[:, :], 1.0 / HD).then_inc(misc, 1)
        pool.wait_ge(misc, 2 + HD)
        pool.tensor_tensor(res["head_centre"][:, :], ident[:, :], res["head_mean"][:, :], ALU.subtract).then_inc(misc, 1)

    return {"transposes": transposes, "copies": copies, "rates": rates, "spreads": spreads, "negated": negated, "head_matrices": head_matrices}


def mixture(nc, name, kind, x, res, ident, slots_x, slots_y, spare, begun=None, prefetch=(), block_diag=None, out=None):
    gelu = kind == "gelu"
    PART_GROUPS, PART_TILES = PARTS_OF[kind], tiles_of(PARTS_OF[kind])
    GROUP0 = [sum(PART_GROUPS[:p]) for p in range(PARTS + 1)]
    TILE0 = [sum(PART_TILES[:p]) for p in range(PARTS + 1)]
    NTILES = TILE0[PARTS]
    F = FF if gelu else FI
    CH = F // P
    PREFETCH_FROM = 4
    XT = 3
    QUADS = [g // SUB for g in PART_GROUPS]
    QUAD0 = [g // SUB for g in GROUP0]
    SET = BODY // 2
    ITERS = NTILES // BODY
    LAG, RING = (1, 2) if gelu else (2, 4)
    BANKS = BODY
    DIGITS = UNROLL * BODY
    assert ITERS * BODY == NTILES and E ** DIGITS <= 2 ** 24 and 2 * SET == BODY and LAG <= SET and LAG + BODY <= DIGITS
    upto = lambda p: TILE0[p] // BODY
    ROUND = 1.5 * 2 ** 23
    gate_w = res["gate0"][:, :] if gelu else res["cols"][:, COL_WG:COL_WG + E]
    base = res["e_temp"] if gelu else res["e_one"]

    with ExitStack() as ctx:
        L = Layer(nc, ctx, name)
        xn = L.sb("xn", [P, GROUPS, D])
        st, mv = L.sb("st", [P, GROUPS, 6]), L.sb("mv", [P, GROUPS, 2])
        ve, rstd = L.sb("ve", [P, GROUPS]), L.sb("rstd", [P, GROUPS])
        each = lambda n, *shape: [L.sb(f"{n}{p}", [P] + [PART_GROUPS[p] if d is G else d for d in shape]) for p in range(PARTS)]
        G = object()
        lg, cut, first, mask, weight, gate = (each(n, G, E) for n in ("lg", "cut", "first", "mask", "weight", "gate"))
        top = each("top", G, 8)
        diff, e2, den = (each(n, G) for n in ("diff", "e2", "den"))
        count = each("count", 4, E)
        steps = [L.sb(f"steps{p}", [P, E, PART_GROUPS[p] + 1]) for p in range(PARTS)]
        ends = [L.sb(f"ends{p}", [P, E, PART_GROUPS[p] + 1]) for p in range(PARTS)]
        pos, taken, free = (each(n, G, E) for n in ("pos", "taken", "free"))
        place = each("place", TOP, G)
        own = each("own", TOP, G)
        picked = each("picked", TOP, G, E)
        index = [L.sb(f"index{p}", [P, TOP, PART_GROUPS[p]], I32) for p in range(PARTS)]
        xT = L.sb("xT", [P, XT, TILE])
        ended = L.sb("ended", [1, MOST_TILES, E])
        expert = L.sb("expert", [1, LAG + NTILES + BODY])
        packed = L.sb("packed", [1, 2, ITERS])
        words = L.sb("words", [1, ITERS], I32)

        xs = L.sb("xs", [P, 2 * BODY, D])
        xsT = [L.sb(f"xsT{k}", [P, SET, P]) for k in range(2)]
        weights = L.sb("weights", [P, BODY, WIDE if gelu else FF])
        hid = L.sb("hid", [P, RING, F])
        sil = None if gelu else L.sb("sil", [P, BANKS, F])
        ys = [L.sb(f"ys{k}", [P, SET, D]) for k in range(2)]
        st2, mv2, ve2, rstd2 = each("st2", G, 6), each("mv2", G, 2), each("ve2", G), each("rstd2", G)
        small = L.sb("back_small", [P, TOP * PART_GROUPS[0], D])
        halves = lambda t, g: [t[:, k * g:(k + 1) * g, :] for k in range(TOP)]
        back = [halves(small, PART_GROUPS[0]), [t[:, 0:PART_GROUPS[1], :] for t in spare],
                halves(xn, PART_GROUPS[2]), halves(small, PART_GROUPS[3])]

        turn = L.bank("turn")
        hb = [L.bank(f"hb{k}") for k in range(BANKS)]
        ob = [L.bank(f"ob{k}") for k in range(2)]
        side = L.bank("side")
        unused = hb + [turn]
        early = [unused[0:QUADS[0]], unused[QUADS[0]:], [side] * QUADS[2], [side] * QUADS[3]]
        counts = [ob[0], ob[1], side, side]
        CW = [g * E for g in PART_GROUPS]

        chain, held = L.sem("dve_chain"), L.sem("held")
        var_ready, rstd_ready = L.sem("var_ready"), L.sem("rstd_ready")
        xn_ready = L.sem("xn_ready")
        xt_ps, xt_copied, xt_used = L.sem("xt_ps"), L.sem("xt_copied"), L.sem("xt_used")
        diff_ready, e2_ready = L.sem("diff_ready"), L.sem("e2_ready")
        mask_ready, counted = L.sem("mask_ready"), L.sem("counted")
        index_ready, table_ready = L.sem("index_ready"), L.sem("table_ready")
        sent = [L.sem(f"sent{p}") for p in range(PARTS)]
        loaded = L.sem("loaded")
        weights_ready = [L.sem(f"weights_ready{j}") for j in range(BODY)]
        turned = L.sem("turned")
        set_ready = L.sem("set_ready")
        h_ready = L.sem("h_ready")
        sil_ready = L.sem("sil_ready")
        hid_ready = L.sem("hid_ready")
        out_ready, y_done = L.sem("out_ready"), L.sem("y_done")
        stored = [L.sem(f"stored{k}") for k in range(2)]
        came = [[[L.sem(f"came{p}_{q}_{k}") for k in range(TOP)] for q in range(QUADS[p])] for p in range(PARTS)]
        gates_ready = L.sem("gates_ready")
        lower_scaled = L.sem("lower_scaled")
        combined = L.sem("combined")
        stored_out = L.sem("stored_out")
        shifted = L.sem("shifted")
        var2, rstd2_ready = L.sem("var2"), L.sem("rstd2_ready")
        tokens_in, weights_in, bias_in = (begun[n] if begun else None for n in ("x_in", "gelu_in", "bias_in"))
        later_weights = attention_weights(nc, L, res, ident, block_diag, begun["attention_in"]) if begun else None
        block = ctx.enter_context(nc.Block())

        SENT = [16 * g * TOP for g in PART_GROUPS]
        group = lambda t, p: t[:, GROUP0[p]:GROUP0[p + 1]]

        def run(eng, body, beside, breaks=(), prepare=lambda i: None):
            i = 0
            while i < ITERS:
                n = i
                while n < ITERS - 1 and n > 0 and n not in beside and (n == i or n not in breaks):
                    n += 1
                if i in breaks:
                    breaks[i]()
                turns = (n - i) // UNROLL
                if turns > 1:
                    with eng.Fori(0, turns) as k:
                        ready = prepare(k * UNROLL + i)
                        for u in range(UNROLL):
                            body(k * UNROLL + (i + u), False, False, {}, (ready, u, (i + u) % 2))
                    i += turns * UNROLL
                else:
                    body(i, i == 0, i == ITERS - 1, beside.get(i, {}), (prepare(i), 0, i % 2))
                    i += 1

        @block.sync
        def _(sp):
            w1 = res["w1" if gelu else "s13"]
            used = hid_ready if gelu else h_ready

            def load(i):
                sp.dma_start(xs[:, bass.ds((i & 1) * BODY, BODY), :],
                             slots_x[bass.ds(i * (BODY * P), BODY * P), :].rearrange("(j p) d -> p j d", p=P)).then_inc(loaded, 16)

            def experts_of(i):
                word = sp.value_load(words[0:1, bass.ds(i, 1)], min_val=0, max_val=E ** DIGITS - 1)
                return [sp.snap((word >> (3 * (LAG + j))) & (E - 1), min_val=0, max_val=E - 1) for j in range(BODY)]

            def fill(j, e):
                sp.dma_start(weights[:, j, :], w1[:, bass.ds(e, 1), :].rearrange("p a f -> p (a f)")).then_inc(weights_ready[j], 16)

            def body(i, needs=None, loads=True):
                experts = experts_of(i + 1)
                for j in range(BODY):
                    sp.wait_ge(used, i * BODY + (j + 1 + BANKS))
                    sp.sem_inc(held, 1)
                    fill(j, experts[j])
                if needs:
                    sp.wait_ge(sent[needs], SENT[needs])
                    sp.wait_ge(table_ready, needs + 1)
                if loads:
                    sp.wait_ge(turned, i * 2 + 2)
                    sp.wait_ge(loaded, i * 16 + 32)
                    sp.sem_inc(held, 1)
                    load(i + 2)

            sp.wait_ge(sent[0], SENT[0])
            load(0)
            if weights_in:
                sp.wait_ge(weights_in, 48)
            sp.wait_ge(table_ready, 1)
            experts = experts_of(0)
            for j in range(BODY):
                fill(j, experts[j])
            sp.wait_ge(loaded, 16)
            load(1)
            if begun:
                for p in range(EARLY, PARTS):
                    clear(sp, res, slots_x, p, begun)
            i = 0
            for p in range(1, PARTS + 1):
                to = -(-(TILE0[p] - 3 * BODY + 1) // BODY) if p < PARTS else ITERS - 2
                if to > i:
                    with sp.Fori(0, to - i) as k:
                        body(k + i)
                if p < PARTS:
                    body(to, needs=p)
                i = to + 1
            body(ITERS - 2, loads=False)
            if out is not None:
                result = out.rearrange("b (g p) d -> p (b g) d", p=P)
                for q0, q1 in ((0, QUAD0[2]), *((q, q + 1) for q in range(QUAD0[2], QUAD0[PARTS]))):
                    gs = slice(q0 * SUB, q1 * SUB)
                    sp.wait_ge(combined, q1)
                    sp.dma_start(result[:, gs, :], x[:, gs, :]).then_inc(stored_out, 16)
                sp.wait_ge(stored_out, 16 * (QUAD0[PARTS] - QUAD0[2] + 1))

        @block.tensor
        def _(pe):
            def turn_tokens(p, q):
                n = QUAD0[p] + q
                pe.wait_ge(xn_ready, n + 1)
                if p >= EARLY:
                    pe.wait_ge(xt_copied, n)
                if p > EARLY and q == 0:
                    pe.wait_ge(index_ready, p)
                for s in range(SUB):
                    last = pe.transpose(early[p][q][:, s * P:(s + 1) * P], xn[:, n * SUB + s, :], ident[:, :])
                last.then_inc(xt_ps, 1)

            def logits(p, q):
                n = QUAD0[p] + q
                pe.wait_ge(xt_copied, QUAD0[p + 1] if counts[p] is side else n + 1)
                for s in range(SUB):
                    g = q * SUB + s
                    last = pe.matmul(counts[p][:, g * E:(g + 1) * E], xT[:, n % XT, s * P:(s + 1) * P], gate_w, start=True, stop=True)
                last.then_inc(xt_used, 1)

            def count_tokens(p):
                pe.wait_ge(mask_ready, p + 1)
                chosen = mask[p][:, :, :].rearrange("p g e -> p (g e)")
                w = CW[p]
                pe.matmul(counts[p][:, w:2 * w], res["before"][:, :], chosen, start=True, stop=True)
                pe.matmul(counts[p][:, 2 * w:3 * w], res["ones"][:, :], chosen, start=True, stop=True).then_inc(counted, 1)

            def turn_set(k, half, i, odd):
                pe.wait_ge(loaded, i * 16 + 16)
                pe.wait_ge(set_ready, k + 1)
                for j in range(SET):
                    last = pe.transpose(turn[:, j * P:(j + 1) * P], xs[:, odd * BODY + half * SET + j, :], ident[:, :])
                last.then_inc(turned, 1)

            def first_products(s, j, i):
                if j % SET == 0:
                    pe.wait_ge(set_ready, i * 2 + (j // SET + 2))
                pe.wait_ge(weights_ready[j], i * 16 + 16)
                pe.wait_ge(hid_ready, s + 1)
                for c in range(FF // P):
                    last = pe.matmul(hb[j][:, c * P:(c + 1) * P], weights[:, j, c * P:(c + 1) * P], xsT[j // SET][:, j % SET, :],
                                     start=True, stop=True)
                last.then_inc(h_ready, 1)

            def second_products(s, j, e):
                pe.wait_ge(hid_ready, s + (1 + BANKS))
                pe.wait_ge(y_done, s + 1)
                r, o = j % RING, ob[j % 2]
                w2 = res["w2" if gelu else "s2"][:, :, :].rearrange("p (e c) d -> p e c d", e=E)
                for c in range(CH):
                    last = pe.matmul(o[:, 0:D], hid[:, r, c * P:(c + 1) * P], w2[:, bass.ds(e, 1), c, :].rearrange("p a d -> p (a d)"),
                                     start=c == 0, stop=c == CH - 1)
                last.then_inc(out_ready, 1)

            def word_of(i):
                return pe.value_load(words[0:1, bass.ds(i, 1)], min_val=0, max_val=E ** DIGITS - 1)

            def body(i, first, last, beside, ready):
                word, u, odd = ready
                expert_of = lambda d: pe.snap((word >> (3 * (u * BODY + d))) & (E - 1), min_val=0, max_val=E - 1)
                for j in range(BODY):
                    s = i * BODY + j
                    if j == 0:
                        turn_set(i * 2 + 1, 1, i, odd)
                    first_products(s, j, i)
                    if first and j == LAG + 1:
                        pe.wait_ge(table_ready, 2)
                    if not (first and j < LAG):
                        second_products(s - LAG, j - LAG, expert_of(j))
                    if j == 2 and not last:
                        turn_set(i * 2 + 2, 0, i + 1, 1 - odd)
                    for part in beside.get(j, []):
                        part()
                if last:
                    for d in range(LAG):
                        second_products(NTILES - LAG + d, BODY - LAG + d, expert_of(BODY + d))

            pe.sem_inc(xt_used, XT)
            pe.sem_inc(h_ready, 2 * SET)
            pe.sem_inc(out_ready, RING)
            for p in range(EARLY):
                for q in range(QUADS[p]):
                    turn_tokens(p, q)
                    if q:
                        logits(p, q - 1)
                logits(p, QUADS[p] - 1)
                count_tokens(p)
            pe.wait_ge(table_ready, 1)
            if weights_in:
                pe.wait_ge(weights_in, 48)
            turn_set(0, 0, 0, 0)
            at = lambda f, *a: [lambda: f(*a)]
            beside = {0: {2: at(turn_tokens, 2, 0), 3: at(turn_tokens, 2, 1)},
                      1: {0: at(turn_tokens, 2, 2), 2: at(logits, 2, 0) + at(logits, 2, 1) + at(logits, 2, 2)},
                      2: {2: at(count_tokens, 2)},
                      6: {0: at(turn_tokens, 3, 0), 2: at(logits, 3, 0)},
                      7: {2: at(count_tokens, 3)}} if gelu else \
                     {1: {2: at(turn_tokens, 2, 0), 3: at(turn_tokens, 2, 1)},
                      2: {2: at(logits, 2, 0) + at(logits, 2, 1)},
                      3: {2: at(count_tokens, 2)},
                      9: {0: at(turn_tokens, 3, 0), 2: at(logits, 3, 0)},
                      10: {2: at(count_tokens, 3)}}
            run(pe, body, beside,
                {upto(p): (lambda p=p: pe.wait_ge(table_ready, p + 1)) for p in range(1, PARTS)}, word_of)
            if later_weights:
                pe.wait_ge(hid_ready, NTILES + BANKS)
                pe.wait_ge(set_ready, NTILES // SET + 1)
                later_weights["transposes"](pe, unused)

        @block.scalar
        def _(act):
            def copy_set(k, half):
                act.wait_ge(turned, k + 1)
                act.wait_ge(h_ready, k * SET + SET)
                act.copy(xsT[half][:, :, :], turn[:, 0:SET * P].rearrange("p (j d) -> p j d", j=SET)).then_inc(set_ready, 1)

            def nonlinear(s, j):
                act.wait_ge(h_ready, s + 1 + 2 * SET)
                if gelu:
                    act.wait_ge(out_ready, s + 1)
                    for c in range(CH):
                        last = act.activation(hid[:, j % RING, c * P:(c + 1) * P], hb[j][:, c * P:(c + 1) * P], ACT.Gelu,
                                              bias=weights[:, j, FF + c:FF + c + 1])
                    last.then_inc(hid_ready, 1)
                else:
                    act.activation(sil[:, j, :], hb[j][:, 0:FI], ACT.Silu).then_inc(sil_ready, 1)

            def store(k, odd):
                act.wait_ge(y_done, k * SET + SET + 2)
                act.dma_start(slots_y[bass.ds(k * (SET * P), SET * P), :].rearrange("(j p) d -> p j d", p=P), ys[odd][:, :, :])\
                   .then_inc(stored[odd], 16)

            def scale_lower(p, q):
                act.wait_ge(gates_ready, p + 1)
                act.wait_ge(came[p][q][0], 16 * SUB)
                for g in range(q * SUB, (q + 1) * SUB):
                    last = act.activation(back[p][0][:, g, :], back[p][0][:, g, :], ACT.Copy, scale=own[p][:, 0, g:g + 1])
                last.then_inc(lower_scaled, 1)

            def copy_tokens(p, q):
                n = QUAD0[p] + q
                act.wait_ge(xt_ps, n + 1)
                act.wait_ge(xt_used, n + 1)
                act.copy(xT[:, n % XT, :], early[p][q][:, :]).then_inc(xt_copied, 1)

            def body(i, first, last, beside, _ready):
                for j in range(BODY):
                    s = i * BODY + j
                    if j == 0:
                        copy_set(i * 2 + 1, 1)
                    nonlinear(s, j)
                    if j == 2 and not last:
                        copy_set(i * 2 + 2, 0)
                    if (j - LAG) % SET == 0:
                        k = (j - LAG) // SET - 1
                        if not (first and k < 0):
                            store(i * 2 + k, k % 2)
                    for part in beside.get(j, []):
                        part()

            act.sem_inc(set_ready, 1)
            if gelu:
                act.sem_inc(hid_ready, BANKS)
            for p in range(EARLY):
                for q in range(QUADS[p]):
                    copy_tokens(p, q)
            nc.scalar.preload_act_table(ACT.Gelu if gelu else ACT.Silu)
            copy_set(0, 0)
            at = lambda f, *a: [lambda: f(*a)]
            beside = {0: {2: at(copy_tokens, 2, 0), 3: at(copy_tokens, 2, 1)},
                      1: {0: at(copy_tokens, 2, 2)},
                      6: {0: at(copy_tokens, 3, 0)},
                      12: {1: at(scale_lower, 0, 0)},
                      16: {1: at(scale_lower, 1, 0)},
                      17: {1: at(scale_lower, 1, 1)},
                      18: {1: at(scale_lower, 1, 2)},
                      22: {1: at(scale_lower, 2, 0)}} if gelu else \
                     {1: {2: at(copy_tokens, 2, 0), 3: at(copy_tokens, 2, 1)},
                      9: {0: at(copy_tokens, 3, 0)},
                      13: {0: at(scale_lower, 0, 0), 1: at(scale_lower, 0, 1)},
                      18: {3: at(scale_lower, 1, 0)},
                      19: {1: at(scale_lower, 1, 1), 3: at(scale_lower, 1, 2)}}
            small = ATTENTION_LOADS
            for n, load in enumerate(prefetch):
                i, j = divmod(n, BODY) if n < small else (-(-small // BODY) + (n - small) // 2, (n - small) % 2 * 2)
                beside.setdefault(PREFETCH_FROM + i, {}).setdefault(j, []).append(lambda load=load: load(act))
            run(act, body, beside)
            for k in range(NTILES // SET - LAG, NTILES // SET):
                store(k, k % 2)
            for p, q in ((2, 1), (2, 2), (3, 0)) if gelu else ((2, 0), (2, 1), (3, 0)):
                if later_weights and p == 3:
                    later_weights["copies"](act, unused)
                scale_lower(p, q)
            if later_weights:
                later_weights["rates"](act)

        @block.vector
        def _(dve):
            ch = Steps(dve, chain, 0, held)

            def stats(p):
                if p == 1 and tokens_in:
                    dve.wait_ge(tokens_in, 16)
                for g in range(GROUP0[p], GROUP0[p + 1]):
                    last = dve.bn_stats(st[:, g, :], x[:, g, :])
                ch.step(last)
                ch.settle()
                for g in range(GROUP0[p], GROUP0[p + 1]):
                    last = dve.bn_aggr(mv[:, g, :], st[:, g, :])
                ch.step(last)
                ch.settle()
                dve.tensor_scalar(group(ve, p), mv[:, GROUP0[p]:GROUP0[p + 1], 1], EPS, None, ALU.add).then_inc(var_ready, 1)

            def normalise(p):
                dve.wait_ge(rstd_ready, p + 1)
                for n in range(QUAD0[p], QUAD0[p + 1]):
                    for g in range(n * SUB, (n + 1) * SUB):
                        last = dve.tensor_scalar(xn[:, g, :], x[:, g, :], mv[:, g, 0:1], rstd[:, g:g + 1], ALU.subtract, ALU.mult)
                    last.then_inc(xn_ready, 1)

            def route(p):
                dve.wait_ge(xt_used, QUAD0[p + 1] + XT)
                lg_ps = counts[p][:, 0:CW[p]].rearrange("p (g e) -> p g e", e=E)
                if gelu:
                    ch.step(dve.tensor_tensor(lg[p][:, :, :], lg_ps, res["gate_bias"][:, :].rearrange("p (a e) -> p a e", a=1)
                                              .broadcast_to([P, PART_GROUPS[p], E]), ALU.add))
                else:
                    ch.step(dve.tensor_copy(lg[p][:, :, :], lg_ps))
                ch.settle()
                for g in range(PART_GROUPS[p]):
                    last = dve.max(top[p][:, g, :], lg[p][:, g, :])
                ch.step(last)
                ch.settle()
                dve.tensor_tensor(diff[p][:, :], top[p][:, :, 1], top[p][:, :, 0], ALU.subtract).then_inc(diff_ready, 1)
                ch.step(dve.tensor_copy(res["replace"][:, GROUP0[p]:GROUP0[p + 1], 0:TOP], top[p][:, :, 0:TOP]))
                ch.settle()
                for g in range(PART_GROUPS[p]):
                    last = dve.match_replace(cut[p][:, g, :], res["replace"][:, GROUP0[p] + g, :], lg[p][:, g, :], -BIG)
                ch.step(last)
                ch.settle()
                dve.tensor_tensor(mask[p][:, :, :], cut[p][:, :, :], lg[p][:, :, :], ALU.not_equal).then_inc(mask_ready, 1)
                ch.step(dve.tensor_tensor(first[p][:, :, :], lg[p][:, :, :], top[p][:, :, 0:1].broadcast_to([P, PART_GROUPS[p], E]), ALU.is_equal))

            def gates(p):
                dve.wait_ge(e2_ready, p + 1)
                ch.settle()
                ch.step(dve.tensor_tensor(weight[p][:, :, :], first[p][:, :, :],
                                          e2[p][:, :].rearrange("p (s a) -> p s a", a=1).broadcast_to([P, PART_GROUPS[p], E]), ALU.max))
                ch.step(dve.tensor_scalar(diff[p][:, :], e2[p][:, :], 1.0, None, ALU.add))
                ch.settle()
                ch.step(dve.tensor_tensor(first[p][:, :, :], weight[p][:, :, :], mask[p][:, :, :], ALU.mult))
                ch.step(dve.reciprocal(den[p][:, :], diff[p][:, :]))
                ch.settle()
                ch.step(dve.tensor_tensor(gate[p][:, :, :], first[p][:, :, :],
                                          den[p][:, :].rearrange("p (s a) -> p s a", a=1).broadcast_to([P, PART_GROUPS[p], E]), ALU.mult))
                ch.settle()
                for k in range(TOP):
                    ch.step(dve.tensor_tensor(picked[p][:, k, :, :], pos[p][:, :, :],
                                              place[p][:, k, :].rearrange("p (g a) -> p g a", a=1).broadcast_to([P, PART_GROUPS[p], E]), ALU.is_equal))
                ch.settle()
                for k in range(TOP):
                    ch.step(dve.tensor_tensor(picked[p][:, k, :, :], picked[p][:, k, :, :], gate[p][:, :, :], ALU.mult))
                ch.settle()
                dve.tensor_reduce(own[p][:, :, :], picked[p][:, :, :, :], AX.X, ALU.add).then_inc(gates_ready, 1)

            def places(p):
                dve.wait_ge(counted, p + 1)
                by_expert = lambda ap: ap.rearrange("p g e -> p e g")
                total = counts[p][:, 2 * CW[p]:3 * CW[p]].rearrange("p (g e) -> p g e", e=E)
                rank = counts[p][:, CW[p]:2 * CW[p]].rearrange("p (g e) -> p g e", e=E)
                n, t1, t2, tiles = (count[p][:, k, :] for k in range(4))
                ch.step(dve.tensor_copy(steps[p][:, :, 0:PART_GROUPS[p]], by_expert(total)))
                ch.settle()
                ch.step(dve.tensor_reduce(n, steps[p][:, :, 0:PART_GROUPS[p]], AX.X, ALU.add))
                ch.settle()
                ch.step(dve.tensor_scalar(t1, n, 1.0 / P, 0.5 - 0.5 / P, ALU.mult, ALU.add))
                ch.settle()
                ch.step(dve.tensor_scalar(t2, t1, ROUND, None, ALU.add))
                ch.settle()
                ch.step(dve.tensor_scalar(tiles, t2, -ROUND, None, ALU.add))
                ch.settle()
                ch.step(dve.scalar_tensor_tensor(steps[p][:, :, PART_GROUPS[p]], tiles, float(P), n, ALU.mult, ALU.subtract))
                ch.settle()
                ch.step(dve.tensor_tensor_scan(ends[p][:, :, :].rearrange("p e g -> p (e g)"),
                                               res["ones"][:, 0:1].broadcast_to([P, E * (PART_GROUPS[p] + 1)]),
                                               steps[p][:, :, :].rearrange("p e g -> p (e g)"), 0.0, ALU.mult, ALU.add))
                ch.settle()
                ch.step(dve.tensor_tensor(by_expert(pos[p][:, :, :]), ends[p][:, :, 0:PART_GROUPS[p]], steps[p][:, :, 0:PART_GROUPS[p]], ALU.subtract))
                ch.settle()
                ch.step(dve.scalar_tensor_tensor(taken[p][:, :, :], rank, float(TILE0[p] * P + 1), pos[p][:, :, :], ALU.add, ALU.add))
                ch.step(dve.tensor_scalar(free[p][:, :, :], mask[p][:, :, :], -float(2 ** 20), float(2 ** 20), ALU.mult, ALU.add))
                ch.settle()
                ch.step(dve.tensor_tensor(pos[p][:, :, :], taken[p][:, :, :], mask[p][:, :, :], ALU.mult))
                ch.settle()
                ch.step(dve.tensor_reduce(place[p][:, 1, :], pos[p][:, :, :], AX.X, ALU.max))
                ch.step(dve.tensor_tensor(free[p][:, :, :], free[p][:, :, :], pos[p][:, :, :], ALU.add))
                ch.settle()
                ch.step(dve.tensor_reduce(place[p][:, 0, :], free[p][:, :, :], AX.X, ALU.min))
                ch.settle()
                dve.tensor_scalar(index[p][:, :, :], place[p][:, :, :], -1.0, None, ALU.add).then_inc(index_ready, 1)

            def table(p):
                tiles = PART_TILES[p]
                ch.step(dve.tensor_tensor(ended[:, 0:tiles, :], res["tile_start"][:, 0:tiles].rearrange("p (t a) -> p t a", a=1)
                                          .broadcast_to([1, tiles, E]), ends[p][0:1, :, PART_GROUPS[p]:].rearrange("p e a -> p a e")
                                          .broadcast_to([1, tiles, E]), ALU.is_ge))
                ch.settle()
                tile_expert = expert[:, LAG + TILE0[p]:LAG + TILE0[p + 1]]
                ch.step(dve.tensor_reduce(tile_expert, ended[:, 0:tiles, :], AX.X, ALU.add))
                ch.settle()
                ch.step(dve.tensor_scalar(tile_expert, tile_expert, float(E - 1), None, ALU.min))
                ch.settle()
                lo, hi = upto(p), upto(p + 1)
                digit = lambda d: expert[:, lo * BODY + d:(hi - 1) * BODY + d + 1:BODY]
                so_far = digit(DIGITS - 1)
                for d in reversed(range(DIGITS - 1)):
                    to = packed[:, d % 2, lo:hi] if d else words[:, lo:hi]
                    ins = dve.scalar_tensor_tensor(to, so_far, float(E), digit(d), ALU.mult, ALU.add)
                    if d:
                        ch.step(ins)
                        ch.settle()
                    else:
                        ins.then_inc(table_ready, 1)
                    so_far = to

            def multiply(s, j):
                dve.wait_ge(sil_ready, s + 1)
                dve.wait_ge(out_ready, s + 1)
                dve.tensor_tensor(hid[:, j % RING, :], sil[:, j, :], hb[j][:, FI:2 * FI], ALU.mult).then_inc(hid_ready, 1)

            def output(s, j, kk, e):
                dve.wait_ge(out_ready, s + 1 + RING)
                if j % SET == 0:
                    dve.wait_ge(stored[j // SET], kk * 16 + 16)
                y, o = ys[j // SET][:, j % SET, :], ob[j % 2][:, 0:D]
                if gelu:
                    dve.tensor_tensor(y, o, res["bias"][:, bass.ds(e * D, D)], ALU.add).then_inc(y_done, 1)
                else:
                    dve.tensor_copy(y, o).then_inc(y_done, 1)

            def experts_of(i):
                if not gelu:
                    return [None] * DIGITS
                word = dve.value_load(words[0:1, bass.ds(i, 1)], min_val=0, max_val=E ** DIGITS - 1)
                return [dve.snap((word >> (3 * d)) & (E - 1), min_val=0, max_val=E - 1) for d in range(DIGITS)]

            def body(i, first, last, beside, ready):
                experts, u, _odd = ready
                for j in range(BODY):
                    s = i * BODY + j
                    if not gelu:
                        multiply(s, j)
                    if not (first and j < LAG):
                        output(s - LAG, (j - LAG) % BODY, i if j >= LAG else i - 1, experts[u * BODY + j])
                    for part in beside.get(j, []):
                        part()
                if last:
                    for d in range(LAG):
                        output(NTILES - LAG + d, BODY - LAG + d, ITERS - 1, experts[BODY + d])

            def await_table(p):
                dve.wait_ge(table_ready, p + 1)
                dve.sem_inc(held, 1)

            def combine(p, q):
                gs = range(q * SUB, (q + 1) * SUB)
                y = back[p]
                dve.wait_ge(came[p][q][1], 16 * SUB)
                dve.wait_ge(lower_scaled, QUAD0[p] + q + 1)
                for g in gs:
                    last = dve.scalar_tensor_tensor(y[0][:, g, :], y[1][:, g, :], own[p][:, 1, g:g + 1], y[0][:, g, :], ALU.mult, ALU.add)
                ch.step(last)
                ch.settle()
                wide = slice(q * SUB, (q + 1) * SUB)
                if not gelu:
                    xt = x[:, GROUP0[p] + q * SUB:GROUP0[p] + (q + 1) * SUB, :]
                    dve.scalar_tensor_tensor(xt, y[0][:, wide, :], 0.5, xt, ALU.mult, ALU.add).then_inc(combined, 1)

            def norm(p, q):
                if not gelu:
                    return
                gs = range(q * SUB, (q + 1) * SUB)
                wide = slice(q * SUB, (q + 1) * SUB)
                y = back[p]
                for g in gs:
                    last = dve.bn_stats(st2[p][:, g, :], y[0][:, g, :])
                ch.step(last)
                ch.settle()
                for g in gs:
                    last = dve.bn_aggr(mv2[p][:, g, :], st2[p][:, g, :])
                ch.step(last)
                ch.settle()
                dve.tensor_scalar(ve2[p][:, wide], mv2[p][:, wide, 1], EPS, None, ALU.add).then_inc(var2, 1)
                for g in gs:
                    last = dve.scalar_tensor_tensor(y[1][:, g, :], y[0][:, g, :], mv2[p][:, g, 0:1], res["post_g"][:, :], ALU.subtract, ALU.mult)
                ch.step(last)

            def finish(p, q):
                if not gelu:
                    return
                gs = range(q * SUB, (q + 1) * SUB)
                y = back[p]
                dve.wait_ge(rstd2_ready, QUAD0[p] + q + 1)
                ch.settle()
                if q == 0:
                    dve.wait_ge(shifted, p + 1)
                for g in gs:
                    xg = x[:, GROUP0[p] + g, :]
                    last = dve.scalar_tensor_tensor(xg, y[1][:, g, :], rstd2[p][:, g:g + 1], xg, ALU.mult, ALU.add)
                last.then_inc(combined, 1)

            dve.sem_inc(y_done, 2)
            for k in range(2):
                dve.sem_inc(stored[k], 16)
            if not gelu:
                dve.sem_inc(hid_ready, BANKS)
            dve.memset(expert[:, :], 0.0)
            stats(0)
            normalise(0)
            stats(1)
            route(0)
            places(0)
            normalise(1)
            table(0)
            stats(2)
            route(1)
            places(1)
            table(1)
            if gelu:
                normalise(2)
                stats(3)
            at = lambda f, *a: [lambda: f(*a)]
            beside = {2: {0: at(route, 2)},
                      3: {0: at(places, 2), 2: at(table, 2)},
                      5: {0: at(normalise, 3), 2: at(gates, 0)},
                      7: {0: at(route, 3)},
                      8: {0: at(places, 3), 2: at(table, 3)},
                      9: {0: at(gates, 1)},
                      11: {0: at(gates, 2)},
                      12: {2: at(combine, 0, 0), 3: at(norm, 0, 0)},
                      14: {0: at(gates, 3)},
                      16: {0: at(finish, 0, 0), 2: at(combine, 1, 0), 3: at(norm, 1, 0)},
                      17: {0: at(finish, 1, 0), 2: at(combine, 1, 1), 3: at(norm, 1, 1)},
                      18: {0: at(finish, 1, 1), 2: at(combine, 1, 2), 3: at(norm, 1, 2)},
                      19: {0: at(finish, 1, 2)},
                      22: {2: at(combine, 2, 0), 3: at(norm, 2, 0)}} if gelu else \
                     {1: {0: at(normalise, 2)},
                      3: {0: at(route, 2)},
                      4: {0: at(places, 2), 2: at(table, 2)},
                      5: {2: at(gates, 0)},
                      6: {0: at(stats, 3)},
                      7: {0: at(gates, 1)},
                      8: {0: at(normalise, 3)},
                      10: {0: at(route, 3)},
                      11: {0: at(places, 3), 2: at(table, 3)},
                      12: {0: at(gates, 2)},
                      13: {1: at(combine, 0, 0), 2: at(combine, 0, 1)},
                      15: {0: at(gates, 3)},
                      19: {0: at(combine, 1, 0), 2: at(combine, 1, 1)},
                      20: {0: at(combine, 1, 2)}}
            if gelu:
                dve.wait_ge(table_ready, 1)
                if bias_in:
                    dve.wait_ge(bias_in, 16)
                dve.sem_inc(held, 1)
            if later_weights:
                beside[20] = {1: at(later_weights["spreads"], dve)}
            run(dve, body, beside, {upto(p): (lambda p=p: await_table(p)) for p in range(1, PARTS)} if gelu else {}, experts_of)
            if gelu:
                combine(2, 1)
                norm(2, 1)
                combine(2, 2)
                norm(2, 2)
                finish(2, 0)
                combine(3, 0)
                norm(3, 0)
                finish(2, 1)
                finish(2, 2)
                if later_weights:
                    later_weights["negated"](dve)
                finish(3, 0)
            else:
                for p, q in ((2, 0), (2, 1), (3, 0)):
                    combine(p, q)

        @block.gpsimd
        def _(pool):
            def power(p):
                pool.wait_ge(var_ready, p + 1)
                pool.tensor_tensor(group(rstd, p), group(ve, p), res["neg_half"][:, 0:PART_GROUPS[p]], ALU.pow).then_inc(rstd_ready, 1)

            def gate_power(p):
                pool.wait_ge(diff_ready, p + 1)
                pool.tensor_tensor(e2[p][:, :], base[:, 0:PART_GROUPS[p]], diff[p][:, :], ALU.pow).then_inc(e2_ready, 1)

            def send(p):
                pool.wait_ge(index_ready, p + 1)
                if begun:
                    pool.wait_ge(begun[f"slots_zeroed{p}"], 16)
                for g in range(PART_GROUPS[p]):
                    for k in range(TOP):
                        pool.indirect_dma_start(slots_x[:, :], bass.IndirectOffsetOnAxis(index[p][:, k, g:g + 1], 0),
                                                xn[:, GROUP0[p] + g, :], None).then_inc(sent[p], 16)

            def shift(p):
                xt = x[:, GROUP0[p]:GROUP0[p + 1], :]
                pool.tensor_tensor(xt, xt, res["post_b"][:, :].rearrange("p (a d) -> p a d", a=1).broadcast_to([P, PART_GROUPS[p], D]), ALU.add)\
                    .then_inc(shifted, 1)

            def fetch(p, q):
                for k in range(TOP):
                    for g in range(q * SUB, (q + 1) * SUB):
                        pool.indirect_dma_start(back[p][k][:, g, :], None, slots_y[0:TILE0[p + 1] * P, :],
                                                bass.IndirectOffsetOnAxis(index[p][:, k, g:g + 1], 0)).then_inc(came[p][q][k], 16)

            def final_power(p, q):
                if gelu:
                    pool.wait_ge(var2, QUAD0[p] + q + 1)
                    wide = slice(q * SUB, (q + 1) * SUB)
                    pool.tensor_tensor(rstd2[p][:, wide], ve2[p][:, wide], res["neg_half"][:, wide], ALU.pow).then_inc(rstd2_ready, 1)

            def await_sets(sets):
                pool.wait_ge(stored[0], (sets + 1) // 2 * 16 + 16)
                pool.wait_ge(stored[1], sets // 2 * 16 + 16)

            power(0)
            power(1)
            send(0)
            power(2)
            send(1)
            gate_power(0)
            gate_power(1)
            if gelu:
                power(3)
            send(2)
            gate_power(2)
            if not gelu:
                power(3)
            await_sets(-(-TILE0[1] // SET))
            for q in range(QUADS[0]):
                fetch(0, q)
            send(3)
            gate_power(3)
            if gelu:
                for p in range(PARTS):
                    shift(p)
            await_sets(-(-TILE0[2] // SET))
            for q in range(QUADS[1]):
                fetch(1, q)
            for p in range(2):
                for q in range(QUADS[p]):
                    final_power(p, q)
            if later_weights:
                later_weights["head_matrices"](pool)
            for p in range(PARTS):
                pool.wait_ge(sent[p], SENT[p])
            await_sets(-(-TILE0[3] // SET))
            for q in range(QUADS[2]):
                fetch(2, q)
            final_power(2, 0)
            pool.wait_ge(combined, QUAD0[1])
            await_sets(NTILES // SET)
            fetch(3, 0)
            for q in range(1, QUADS[2]):
                final_power(2, q)
            final_power(3, 0)


def state_space(nc, x, res, ident, swiglu_in):
    STEPS_OF_TIME = SEQ // TILE
    PAIRS = [range(b, b + 2) for b in range(0, NB, 2)]
    col = lambda n: res["cols"][:, COL[n]:COL[n] + 1]
    w = lambda n: res["sqT"][:, SQ[n], :]
    with ExitStack() as ctx:
        L = Layer(nc, ctx, "ssm")
        per_batch = lambda n, shape=(P, TILE): [L.sb(f"{n}{b}", list(shape)) for b in range(NB)]
        xn = per_batch("xn", (P, SUB, D))
        xT, u, sg, ab, dt, nbt = (per_batch(n) for n in ("xT", "u", "sg", "ab", "dt", "nbt"))
        shift = per_batch("shift", (P, SUB))
        h = ab
        carry = per_batch("carry", (P, 1))
        per_step = lambda n, *shape: [per_batch(f"{n}{k}_", (P, *shape)) for k in range(STEPS_OF_TIME)]
        st, mv, ve, rstd = per_step("st", SUB, 6), per_step("mv", SUB, 2), per_step("ve", SUB), per_step("rstd", SUB)
        bank_a = [L.bank(f"bank_a{b}") for b in range(NB)]
        bank_b = [L.bank(f"bank_b{b}") for b in range(NB)]
        names = ("var_ready", "rstd_ready", "xn_ready", "xt_ps", "xt_ready", "ug_ready", "u_ready", "tanh_done", "sg_done",
                 "dt_ready", "bt_ready", "abs_done", "exp_done", "ln_done", "max_done", "dt_done", "decay_done",
                 "scan_done", "y_ready", "gated", "z_ready", "out_ready", "added", "chain")
        (var_ready, rstd_ready, xn_ready, xt_ps, xt_ready, ug_ready, u_ready, tanh_done, sg_done, dt_ready, bt_ready,
         abs_done, exp_done, ln_done, max_done, dt_done, decay_done, scan_done, y_ready, gated, z_ready, out_ready,
         added, chain) = (L.sem(n) for n in names)
        shift_ready = L.sem("shift_ready")
        weights_turned, weights_copied = L.sem("weights_turned"), L.sem("weights_copied")
        weights = []
        for half, raw in enumerate(("raw_s1", "raw_s3")):
            for k in range(0, E * FI // P, 4):
                e = slice(k * P // FI, (k + 4) * P // FI)
                weights.append(([res[raw][:, k + j, :] for j in range(4)], res["s13"][:, e, half * FI:(half + 1) * FI]))
        for k in range(0, E * FI // P, 4):
            weights.append(([res["raw_s2"][:, (k + j) // 2, ((k + j) % 2) * P:((k + j) % 2 + 1) * P] for j in range(4)],
                            res["s2"][:, k:k + 4, :]))
        banks = bank_a + bank_b
        block = ctx.enter_context(nc.Block())

        @block.tensor
        def _(pe):
            pe.wait_ge(swiglu_in, 16 * 3 * QUARTERS)
            for n, (srcs, _dst) in enumerate(weights):
                if n >= len(banks):
                    pe.wait_ge(weights_copied, n - len(banks) + 1)
                for j, src in enumerate(srcs):
                    last = pe.transpose(banks[n % len(banks)][:, j * P:(j + 1) * P], src, ident[:, :])
                last.then_inc(weights_turned, 1)
            pe.wait_ge(weights_copied, len(weights))
            with pe.Fori(0, STEPS_OF_TIME) as k:
                c = k * NB
                for b in range(NB):
                    pe.wait_ge(xn_ready, c + b + 1)
                    for s in range(SUB):
                        last = pe.transpose(bank_a[b][:, s * P:(s + 1) * P], xn[b][:, s, :], ident[:, :])
                    last.then_inc(xt_ps, 1)
                for b in range(NB):
                    pe.wait_ge(xt_ready, c + b + 1)
                    pe.matmul(bank_a[b][:, :], w("Wu"), xT[b][:, :], start=True, stop=True)
                    pe.wait_ge(added, c + b + 1)
                    pe.matmul(bank_b[b][:, :], w("Wgate"), xT[b][:, :], start=True, stop=True).then_inc(ug_ready, 1)
                for b in range(NB):
                    pe.wait_ge(u_ready, c + b + 1)
                    pe.matmul(bank_a[b][:, :], w("Wdt"), u[b][:, :], start=True, stop=True).then_inc(dt_ready, 1)
                for b in range(NB):
                    pe.wait_ge(sg_done, c + b + 1)
                    pe.matmul(bank_b[b][:, :], w("Wstate"), u[b][:, :], start=True, stop=True).then_inc(bt_ready, 1)
                for b in range(NB):
                    pe.wait_ge(scan_done, c + b + 1)
                    pe.matmul(bank_a[b][:, :], w("WC"), h[b][:, :], start=True, stop=True).then_inc(y_ready, 1)
                for b in range(NB):
                    pe.wait_ge(z_ready, c + b + 1)
                    for s in range(SUB):
                        last = pe.matmul(bank_b[b][:, s * P:(s + 1) * P], sg[b][:, s * P:(s + 1) * P], w("Wout"), start=True, stop=True)
                    last.then_inc(out_ready, 1)

        @block.scalar
        def _(act):
            for n, (_srcs, dst) in enumerate(weights):
                act.wait_ge(weights_turned, n + 1)
                act.copy(dst, banks[n % len(banks)][:, :].rearrange("p (c d) -> p c d", d=dst.shape[-1])).then_inc(weights_copied, 1)
            for k in range(STEPS_OF_TIME):
                c = k * NB
                for b in range(NB):
                    act.wait_ge(xt_ps, c + b + 1)
                    act.copy(xT[b][:, :], bank_a[b][:, :]).then_inc(xt_ready, 1)
                for b in range(NB):
                    act.wait_ge(ug_ready, c + b + 1)
                    act.copy(u[b][:, :], bank_a[b][:, :]).then_inc(u_ready, 1)
                    act.activation(sg[b][:, :], bank_b[b][:, :], ACT.Tanh, scale=0.5).then_inc(tanh_done, 1)
                for b in range(NB):
                    act.wait_ge(dt_ready, c + b + 1)
                    act.activation(ab[b][:, :], bank_a[b][:, :], ACT.Abs, bias=col("L0_attn_b_dt")).then_inc(abs_done, 1)
                for b in range(NB):
                    act.wait_ge(abs_done, c + b + 1)
                    act.activation(ab[b][:, :], ab[b][:, :], ACT.Exp, scale=-1.0).then_inc(exp_done, 1)
                for b in range(NB):
                    act.wait_ge(exp_done, c + b + 1)
                    act.activation(ab[b][:, :], ab[b][:, :], ACT.Ln, bias=1.0).then_inc(ln_done, 1)
                for b in range(NB):
                    act.wait_ge(dt_done, c + b + 1)
                    act.activation(dt[b][:, :], dt[b][:, :], ACT.Exp, scale=res["neg_rate"][:, 0:1]).then_inc(decay_done, 1)
                if k + 1 < STEPS_OF_TIME:
                    for b in range(NB):
                        act.wait_ge(shift_ready, c + b + 1)
                        act.wait_ge(xt_ps, c + b + 1)
                        for s in range(SUB):
                            last = act.activation(xn[b][:, s, :], of_group(x, k + 1 + b * STEPS_OF_TIME, s), ACT.Identity,
                                                  bias=shift[b][:, s:s + 1], scale=rstd[k + 1][b][:, s:s + 1])
                        last.then_inc(xn_ready, 1)

        @block.vector
        def _(dve):
            for b in range(NB):
                last = dve.memset(carry[b][:, :], 0.0)
            last.then_inc(chain, 1)
            dve.sem_inc(added, NB)
            ch = Steps(dve, chain, 1)

            def stats(k, batches):
                for b in batches:
                    for s in range(SUB):
                        last = dve.bn_stats(st[k][b][:, s, :], of_group(x, k + b * STEPS_OF_TIME, s))
                ch.step(last)
                ch.settle()
                for b in batches:
                    for s in range(SUB):
                        last = dve.bn_aggr(mv[k][b][:, s, :], st[k][b][:, s, :])
                ch.step(last)
                ch.settle()
                for b in batches:
                    dve.tensor_scalar(ve[k][b][:, :], mv[k][b][:, :, 1], EPS, None, ALU.add).then_inc(var_ready, 1)

            def normalise(b):
                dve.wait_ge(rstd_ready, b + 1)
                for s in range(SUB):
                    last = dve.tensor_scalar(xn[b][:, s, :], of_group(x, b * STEPS_OF_TIME, s), mv[0][b][:, s, 0:1],
                                             rstd[0][b][:, s:s + 1], ALU.subtract, ALU.mult)
                last.then_inc(xn_ready, 1)

            stats(0, range(NB))
            for b in range(NB):
                normalise(b)
            for k in range(STEPS_OF_TIME):
                c = k * NB
                for b in range(NB):
                    dve.wait_ge(tanh_done, c + b + 1)
                    dve.scalar_tensor_tensor(sg[b][:, :], sg[b][:, :], 1.0, bank_b[b][:, :], ALU.add, ALU.mult).then_inc(sg_done, 1)
                    if k + 1 < STEPS_OF_TIME:
                        stats(k + 1, [b])
                for b in range(NB):
                    dve.wait_ge(dt_ready, c + b + 1)
                    dve.wait_ge(abs_done, c + b + 1)
                    dve.tensor_scalar(dt[b][:, :], bank_a[b][:, :], col("L0_attn_b_dt"), 0.0, ALU.add, ALU.max).then_inc(max_done, 1)
                for b in range(NB):
                    dve.wait_ge(ln_done, c + b + 1)
                    dve.wait_ge(max_done, c + b + 1)
                    dve.tensor_tensor(dt[b][:, :], dt[b][:, :], ab[b][:, :], ALU.add).then_inc(dt_done, 1)
                if k + 1 < STEPS_OF_TIME:
                    for b in range(NB):
                        dve.wait_ge(rstd_ready, (k + 1) * NB + b + 1)
                        dve.scalar_tensor_tensor(shift[b][:, :], mv[k + 1][b][:, :, 0], -1.0, rstd[k + 1][b][:, :], ALU.mult, ALU.mult)\
                            .then_inc(shift_ready, 1)
                for pair in PAIRS:
                    for b in pair:
                        dve.wait_ge(decay_done, c + b + 1)
                        ch.step(dve.tensor_scalar(dt[b][:, :], dt[b][:, :], res["floor"][:, 0:1], 1.0, ALU.max, ALU.min))
                    ch.settle()
                    for b in pair:
                        dve.wait_ge(bt_ready, c + b + 1)
                        ch.step(dve.scalar_tensor_tensor(nbt[b][:, :], dt[b][:, :], 1.0, bank_b[b][:, :], ALU.subtract, ALU.mult))
                    ch.settle()
                    for b in pair:
                        dve.tensor_tensor_scan(h[b][:, :], dt[b][:, :], nbt[b][:, :], carry[b][:, 0:1], ALU.mult, ALU.subtract)\
                            .then_inc(scan_done, 1)
                for b in range(NB):
                    dve.wait_ge(scan_done, c + b + 1)
                    ch.step(dve.tensor_copy(carry[b][:, :], h[b][:, TILE - 1:TILE]))
                for b in range(NB + 1):
                    if b < NB:
                        dve.wait_ge(y_ready, c + b + 1)
                        dve.scalar_tensor_tensor(sg[b][:, :], bank_a[b][:, :], 0.5, sg[b][:, :], ALU.mult, ALU.mult).then_inc(gated, 1)
                    if b > 0:
                        dve.wait_ge(gated, c + b)
                        dve.scalar_tensor_tensor(sg[b - 1][:, :], xT[b - 1][:, :], col("L0_attn_D"), sg[b - 1][:, :], ALU.mult, ALU.add)\
                            .then_inc(z_ready, 1)
                for b in range(NB):
                    dve.wait_ge(out_ready, c + b + 1)
                    xt = of_tile(x, k + b * STEPS_OF_TIME)
                    dve.tensor_tensor(xt, xt, bank_b[b][:, :].rearrange("p (s d) -> p s d", s=SUB), ALU.add).then_inc(added, 1)

        @block.gpsimd
        def _(pool):
            for k in range(STEPS_OF_TIME):
                for b in range(NB):
                    pool.wait_ge(var_ready, k * NB + b + 1)
                    pool.tensor_tensor(rstd[k][b][:, :], ve[k][b][:, :], res["neg_half"][:, 0:SUB], ALU.pow).then_inc(rstd_ready, 1)


def receptance(nc, x, res, ident, block_diag):
    STEPS_OF_TIME = SEQ // TILE
    col = lambda n: res["cols"][:, COL[n]:COL[n] + 1]
    w = lambda n: res["sqT"][:, SQ[n], :]
    with ExitStack() as ctx:
        L = Layer(nc, ctx, "rwkv")
        per_batch = lambda n, shape=(P, TILE): [L.sb(f"{n}{b}", list(shape)) for b in range(NB)]
        xn = per_batch("xn", (P, SUB, D))
        xT = per_batch("xT", (P, TILE + 1))
        spare = lambda n: [res[n][:, :, :].rearrange("p a b -> p (a b)")[:, b * TILE:(b + 1) * TILE] for b in range(NB)]
        dx, lx = spare("raw_s1"), spare("raw_s3")
        tw = per_batch("tw", (P, 3, TILE + 1))
        q = {p: per_batch("q" + p) for p in LORAS}
        v = spare("raw_s2")
        vh, vl = ([L.sb(f"{n}{b}", [P, TILE], F32R) for b in range(NB)] for n in ("vh", "vl"))
        carry = per_batch("carry", (P, HD))
        y = [t[:, :] for t in per_batch("y")]
        per_step = lambda n, *shape: [per_batch(f"{n}{k}_", (P, *shape)) for k in range(STEPS_OF_TIME)]
        st, mv, ve, rstd = per_step("st", SUB, 6), per_step("mv", SUB, 2), per_step("ve", SUB), per_step("rstd", SUB)
        bank_a = [L.bank(f"bank_a{b}") for b in range(NB)]
        bank_b = [L.bank(f"bank_b{b}") for b in range(NB)]
        S = {}
        for n in ("var_ready", "rstd_ready", "xn_ready", "xt_ps", "xt_ready", "dx_ready", "lx_ready", "la_rk", "la_vg", "la_d",
                  "tanh_rk", "tanh_vg", "tanh_d", "lb_ready", "scaled", "xin_ready", "proj_ready", "copied", "tanh_g", "sg_done",
                  "la_d2", "tanh_d2", "lb_d2", "exp1", "w_ready", "ruk_done", "bonus_ps", "bonus_done",
                  "vh_ready", "vl_ready", "ve_ready", "kv_done", "first_ready", "scan_done", "carried", "m_done", "sum_done", "y_done", "centred", "squared", "var_ps",
                  "ln_done", "rs_done", "normed", "shifted", "o_ready", "out_ready", "added", "chain", "acts"):
            S[n] = L.sem(n)
        block = ctx.enter_context(nc.Block())
        NP = len(LORAS)
        mid = lambda b: xT[b][:, 1:TILE + 1]
        T = lambda b, k: tw[b][:, k, 0:TILE]

        @block.tensor
        def _(pe):
            with pe.Fori(0, STEPS_OF_TIME) as k:
                c = k * NB
                for b in range(NB):
                    pe.wait_ge(S["xn_ready"], c + b + 1)
                    for s in range(SUB):
                        last = pe.transpose(bank_a[b][:, s * P:(s + 1) * P], xn[b][:, s, :], ident[:, :])
                    last.then_inc(S["xt_ps"], 1)
                for b in range(NB):
                    pe.wait_ge(S["lx_ready"], c + b + 1)
                    pe.matmul(bank_a[b][:, :], res["laT"][:, 0, :], lx[b][:, :], start=True, stop=True).then_inc(S["la_rk"], 1)
                    pe.wait_ge(S["added"], c + b + 1)
                    pe.matmul(bank_b[b][:, :], res["laT"][:, 1, :], lx[b][:, :], start=True, stop=True).then_inc(S["la_vg"], 1)
                for b in range(NB):
                    pe.wait_ge(S["tanh_rk"], c + b + 1)
                    pe.matmul(bank_a[b][0:LORA, :], res["laT"][:, 2, 0:LORA], lx[b][:, :], start=True, stop=True).then_inc(S["la_d"], 1)

                def expand(n, p):
                    pair, half = LA[p]
                    rows = slice(half * LORA, (half + 1) * LORA)
                    for b in range(NB):
                        if n == 0:
                            pe.wait_ge(S["tanh_d"], c + b + 1)
                        else:
                            pe.wait_ge(S["scaled"], k * (NP * NB) + (n - 1) * NB + b + 1)
                        pe.matmul(bank_a[b][:, :], res["lbT"][rows, pair, :], tw[b][rows, pair, 0:TILE], start=True, stop=True)\
                            .then_inc(S["lb_ready"], 1)

                def project(n, p):
                    for b in range(NB):
                        pe.wait_ge(S["xin_ready"], k * (NP * NB) + n * NB + b + 1)
                        if n == 0:
                            pe.wait_ge(S["tanh_vg"], c + b + 1)
                        else:
                            pe.wait_ge(S["copied"], k * (3 * NB) + (n - 1) * NB + b + 1)
                        pe.matmul(bank_b[b][:, :], w(p + "W"), q[p][b][:, :], start=True, stop=True).then_inc(S["proj_ready"], 1)

                for n, p in enumerate(LORAS):
                    expand(n, p)
                    if n >= 1:
                        project(n - 1, LORAS[n - 1])
                for b in range(NB):
                    pe.wait_ge(S["xin_ready"], k * (NP * NB) + 4 * NB + b + 1)
                    pe.matmul(bank_a[b][0:LORA, :], res["laT"][:, 2, 0:LORA], q["d"][b][:, :], start=True, stop=True).then_inc(S["la_d2"], 1)
                for b in range(NB):
                    pe.wait_ge(S["tanh_d2"], c + b + 1)
                    pe.wait_ge(S["sg_done"], c + b + 1)
                    pe.matmul(bank_b[b][:, :], res["lbT"][0:LORA, 2, :], tw[b][0:LORA, 2, 0:TILE], start=True, stop=True).then_inc(S["lb_d2"], 1)
                for b in range(NB):
                    pe.wait_ge(S["ruk_done"], c + b + 1)
                    pe.matmul(bank_a[b][:, :], block_diag[:, :], lx[b][:, :], start=True, stop=True).then_inc(S["bonus_ps"], 1)

                def values(j):
                    for b in range(NB):
                        if j == 0:
                            pe.wait_ge(S["bonus_done"], c + b + 1)
                            pe.wait_ge(S["vl_ready"], c + b + 1)
                        else:
                            pe.wait_ge(S["kv_done"], k * (HD * NB) + (j - 1) * NB + b + 1)
                        pe.matmul(bank_a[b][:, :], res["spread"][:, j, :], vh[b][:, :], start=True, stop=False)
                        pe.matmul(bank_a[b][:, :], res["spread"][:, j, :], vl[b][:, :], start=False, stop=True).then_inc(S["ve_ready"], 1)

                def head_sums(j):
                    for b in range(NB):
                        pe.wait_ge(S["m_done"], k * (HD * NB) + j * NB + b + 1)
                        pe.matmul(bank_b[b][:, :], res["sel"][:, j, :], T(b, 2), start=j == 0, stop=j == HD - 1).then_inc(S["sum_done"], 1)

                for j in range(HD):
                    values(j)
                    if j >= 1:
                        head_sums(j - 1)
                head_sums(HD - 1)
                for b in range(NB):
                    pe.wait_ge(S["y_done"], c + b + 1)
                    pe.matmul(bank_a[b][:, :], res["head_centre"][:, :], y[b], start=True, stop=True).then_inc(S["centred"], 1)
                for b in range(NB):
                    pe.wait_ge(S["squared"], c + b + 1)
                    pe.matmul(bank_b[b][:, :], res["head_mean"][:, :], lx[b][:, :], start=True, stop=True).then_inc(S["var_ps"], 1)
                for b in range(NB):
                    pe.wait_ge(S["o_ready"], c + b + 1)
                    for s in range(SUB):
                        last = pe.matmul(bank_b[b][:, s * P:(s + 1) * P], y[b][:, s * P:(s + 1) * P], w("oW"), start=True, stop=True)
                    last.then_inc(S["out_ready"], 1)

        @block.scalar
        def _(act):
            for b in range(NB):
                last = act.activation(xT[b][:, TILE:TILE + 1], ident[:, 0:1], ACT.Copy, scale=0.0)
            last.then_inc(S["acts"], 1)
            act.wait_ge(S["acts"], 1)
            with act.Fori(0, STEPS_OF_TIME) as k:
                c = k * NB
                for b in range(NB):
                    act.wait_ge(S["xt_ps"], c + b + 1)
                    act.copy(xT[b][:, 0:1], xT[b][:, TILE:TILE + 1]).then_inc(S["acts"], 1)
                    act.wait_ge(S["acts"], c + b + 2)
                    act.copy(mid(b), bank_a[b][:, :]).then_inc(S["xt_ready"], 1)
                for b in range(NB):
                    act.wait_ge(S["la_rk"], c + b + 1)
                    act.activation(T(b, 0), bank_a[b][:, :], ACT.Tanh).then_inc(S["tanh_rk"], 1)
                    act.wait_ge(S["la_vg"], c + b + 1)
                    act.activation(T(b, 1), bank_b[b][:, :], ACT.Tanh).then_inc(S["tanh_vg"], 1)
                for b in range(NB):
                    act.wait_ge(S["la_d"], c + b + 1)
                    act.activation(tw[b][0:LORA, 2, 0:TILE], bank_a[b][0:LORA, :], ACT.Tanh).then_inc(S["tanh_d"], 1)
                for n, p in enumerate("rkv"):
                    for b in range(NB):
                        act.wait_ge(S["proj_ready"], k * (4 * NB) + n * NB + b + 1)
                        act.copy({"r": q["r"], "k": q["k"], "v": v}[p][b][:, :], bank_b[b][:, :]).then_inc(S["copied"], 1)
                for b in range(NB):
                    act.wait_ge(S["copied"], k * (3 * NB) + 2 * NB + b + 1)
                    act.copy(vh[b][:, :], v[b][:, :]).then_inc(S["vh_ready"], 1)
                for b in range(NB):
                    act.wait_ge(S["proj_ready"], k * (4 * NB) + 3 * NB + b + 1)
                    act.activation(q["g"][b][:, :], bank_b[b][:, :], ACT.Tanh, scale=0.5).then_inc(S["tanh_g"], 1)
                for b in range(NB):
                    act.wait_ge(S["la_d2"], c + b + 1)
                    act.activation(tw[b][0:LORA, 2, 0:TILE], bank_a[b][0:LORA, :], ACT.Tanh).then_inc(S["tanh_d2"], 1)
                for b in range(NB):
                    act.wait_ge(S["lb_d2"], c + b + 1)
                    act.activation(q["d"][b][:, :], bank_b[b][:, :], ACT.Exp, bias=col("L1_attn_d_ll")).then_inc(S["exp1"], 1)
                for b in range(NB):
                    act.wait_ge(S["exp1"], c + b + 1)
                    act.activation(q["d"][b][:, :], q["d"][b][:, :], ACT.Exp, scale=-1.0).then_inc(S["w_ready"], 1)
                for j in range(HD):
                    n = k * (HD * NB) + j * NB
                    for b in range(NB):
                        if j == 0 and b == 0:
                            act.wait_ge(S["carried"], k * (HD * NB) + 1)
                        if j >= 2:
                            act.wait_ge(S["m_done"], k * (HD * NB) + (j - 2) * NB + b + 1)
                        act.copy(tw[b][:, j % 2, 0:1], carry[b][:, j:j + 1]).then_inc(S["first_ready"], 1)
                    for b in range(NB):
                        act.wait_ge(S["first_ready"], n + b + 1)
                        act.wait_ge(S["scan_done"], n + b + 1)
                        act.copy(carry[b][:, j:j + 1], tw[b][:, j % 2, TILE:TILE + 1]).then_inc(S["carried"], 1)
                for b in range(NB):
                    act.wait_ge(S["centred"], c + b + 1)
                    act.activation(lx[b][:, :], bank_a[b][:, :], ACT.Square).then_inc(S["squared"], 1)
                for b in range(NB):
                    act.wait_ge(S["var_ps"], c + b + 1)
                    act.activation(lx[b][:, :], bank_b[b][:, :], ACT.Ln, bias=res["eps"][:, 0:1]).then_inc(S["ln_done"], 1)
                for b in range(NB):
                    act.wait_ge(S["ln_done"], c + b + 1)
                    act.activation(lx[b][:, :], lx[b][:, :], ACT.Exp, scale=-0.5).then_inc(S["rs_done"], 1)

        @block.vector
        def _(dve):
            for b in range(NB):
                last = dve.tensor_copy(carry[b][:, :], res["state0"][:, :])
            last.then_inc(S["carried"], 1)
            dve.sem_inc(S["added"], NB)
            ch = Steps(dve, S["chain"], 0)

            def stats(k, batches):
                for b in batches:
                    for s in range(SUB):
                        last = dve.bn_stats(st[k][b][:, s, :], of_group(x, k + b * STEPS_OF_TIME, s))
                ch.step(last)
                ch.settle()
                for b in batches:
                    for s in range(SUB):
                        last = dve.bn_aggr(mv[k][b][:, s, :], st[k][b][:, s, :])
                ch.step(last)
                ch.settle()
                for b in batches:
                    dve.tensor_scalar(ve[k][b][:, :], mv[k][b][:, :, 1], EPS, None, ALU.add).then_inc(S["var_ready"], 1)

            def normalise(k, b):
                dve.wait_ge(S["rstd_ready"], k * NB + b + 1)
                if k:
                    dve.wait_ge(S["xt_ps"], (k - 1) * NB + b + 1)
                for s in range(SUB):
                    last = dve.tensor_scalar(xn[b][:, s, :], of_group(x, k + b * STEPS_OF_TIME, s), mv[k][b][:, s, 0:1],
                                             rstd[k][b][:, s:s + 1], ALU.subtract, ALU.mult)
                last.then_inc(S["xn_ready"], 1)

            stats(0, range(NB))
            for b in range(NB):
                normalise(0, b)
            for k in range(STEPS_OF_TIME):
                c = k * NB
                for n in range(NB + 1):
                    if n < NB:
                        dve.wait_ge(S["xt_ready"], c + n + 1)
                        dve.tensor_tensor(dx[n][:, :], xT[n][:, 0:TILE], mid(n), ALU.subtract).then_inc(S["dx_ready"], 1)
                    if n == 0:
                        continue
                    b = n - 1
                    dve.wait_ge(S["dx_ready"], c + b + 1)
                    dve.scalar_tensor_tensor(lx[b][:, :], dx[b][:, :], col("L1_attn_xw"), mid(b), ALU.mult, ALU.add).then_inc(S["lx_ready"], 1)

                def mix(n, p):
                    for b in range(NB):
                        dve.wait_ge(S["lb_ready"], k * (NP * NB) + n * NB + b + 1)
                        dve.scalar_tensor_tensor(q[p][b][:, :], bank_a[b][:, :], col(f"L1_attn_{p}_ll"), dx[b][:, :], ALU.add, ALU.mult)\
                            .then_inc(S["scaled"], 1)

                for n, p in enumerate(LORAS):
                    mix(n, p)
                    if n == 4:
                        for b in range(NB):
                            dve.wait_ge(S["copied"], k * (3 * NB) + 2 * NB + b + 1)
                            dve.scalar_tensor_tensor(lx[b][:, :], q["r"][b][:, :], col("L1_attn_u"), q["k"][b][:, :], ALU.mult, ALU.mult)\
                                .then_inc(S["ruk_done"], 1)
                for b in range(NB):
                    dve.wait_ge(S["vh_ready"], c + b + 1)
                    dve.tensor_tensor(vl[b][:, :], v[b][:, :], vh[b][:, :].bitcast(F32), ALU.subtract).then_inc(S["vl_ready"], 1)
                for b in range(NB):
                    dve.wait_ge(S["tanh_g"], c + b + 1)
                    dve.scalar_tensor_tensor(q["g"][b][:, :], q["g"][b][:, :], 1.0, bank_b[b][:, :], ALU.add, ALU.mult).then_inc(S["sg_done"], 1)
                for b in range(NB):
                    dve.wait_ge(S["bonus_ps"], c + b + 1)
                    dve.tensor_tensor(v[b][:, :], v[b][:, :], bank_a[b][:, :], ALU.mult).then_inc(S["bonus_done"], 1)
                for j in range(HD):
                    n = k * (HD * NB) + j * NB
                    for b in range(NB):
                        if j >= 1:
                            dve.wait_ge(S["scan_done"], n - NB + (b + 1))
                        dve.wait_ge(S["ve_ready"], n + b + 1)
                        dve.tensor_tensor(dx[b][:, :], q["k"][b][:, :], bank_a[b][:, :], ALU.mult).then_inc(S["kv_done"], 1)
                    for b in range(NB):
                        if j == 0:
                            dve.wait_ge(S["w_ready"], c + b + 1)
                            dve.wait_ge(S["carried"], k * (HD * NB) + 1)
                        if j >= 2:
                            dve.wait_ge(S["m_done"], k * (HD * NB) + (j - 2) * NB + b + 1)
                            dve.wait_ge(S["carried"], k * (HD * NB) + (j - 2) * NB + b + 2)
                        dve.wait_ge(S["kv_done"], n + b + 1)
                        dve.tensor_tensor_scan(tw[b][:, j % 2, 1:TILE + 1], q["d"][b][:, :], dx[b][:, :], carry[b][:, j:j + 1],
                                               ALU.mult, ALU.add).then_inc(S["scan_done"], 1)
                for b in range(NB):
                    dve.wait_ge(S["sum_done"], k * (HD * NB) + (HD - 1) * NB + b + 1)
                    dve.tensor_tensor(y[b], bank_b[b][:, :], v[b][:, :], ALU.add).then_inc(S["y_done"], 1)
                if k + 1 < STEPS_OF_TIME:
                    stats(k + 1, range(NB))
                    for b in range(NB):
                        normalise(k + 1, b)
                for n in range(NB + 2):
                    if n < NB:
                        dve.wait_ge(S["rs_done"], c + n + 1)
                        dve.tensor_tensor(y[n], bank_a[n][:, :], lx[n][:, :], ALU.mult).then_inc(S["normed"], 1)
                    if 0 <= n - 1 < NB:
                        b = n - 1
                        dve.wait_ge(S["normed"], c + b + 1)
                        dve.tensor_scalar(y[b], y[b], res["cols"][:, COL_LNW:COL_LNW + 1], res["cols"][:, COL_LNB:COL_LNB + 1],
                                          ALU.mult, ALU.add).then_inc(S["shifted"], 1)
                    if n >= 2:
                        b = n - 2
                        dve.wait_ge(S["shifted"], c + b + 1)
                        dve.scalar_tensor_tensor(y[b], q["g"][b][:, :], 0.5, y[b], ALU.mult, ALU.mult).then_inc(S["o_ready"], 1)
                for b in range(NB):
                    dve.wait_ge(S["out_ready"], c + b + 1)
                    xt = of_tile(x, k + b * STEPS_OF_TIME)
                    dve.tensor_tensor(xt, xt, bank_b[b][:, :].rearrange("p (s d) -> p s d", s=SUB), ALU.add).then_inc(S["added"], 1)

        @block.gpsimd
        def _(pool):
            for k in range(STEPS_OF_TIME):
                for b in range(NB):
                    pool.wait_ge(S["var_ready"], k * NB + b + 1)
                    pool.tensor_tensor(rstd[k][b][:, :], ve[k][b][:, :], res["neg_half"][:, 0:SUB], ALU.pow).then_inc(S["rstd_ready"], 1)
                for n, p in enumerate(LORAS):
                    for b in range(NB):
                        pool.wait_ge(S["scaled"], k * (NP * NB) + n * NB + b + 1)
                        pool.tensor_tensor(q[p][b][:, :], q[p][b][:, :], mid(b), ALU.add).then_inc(S["xin_ready"], 1)
                for j in range(HD):
                    n = k * (HD * NB) + j * NB
                    for b in range(NB):
                        pool.wait_ge(S["first_ready"], n + b + 1)
                        pool.wait_ge(S["scan_done"], n + b + 1)
                        if j >= 1:
                            pool.wait_ge(S["sum_done"], k * (HD * NB) + (j - 1) * NB + b + 1)
                        pool.tensor_tensor(T(b, 2), tw[b][:, j % 2, 0:TILE], q["r"][b][:, :], ALU.mult).then_inc(S["m_done"], 1)


def build(nc, ins, out, layers=6):
    with ExitStack() as ctx:
        def sb(name, shape, dt=F32):
            return ctx.enter_context(nc.sbuf_tensor(name, shape, dt))

        x = sb("x", [P, NT * SUB, D])
        ident = sb("ident", [P, P])
        block_diag = sb("block_diag", [P, P])
        res = {}
        for n, shape in (("sqT", [P, len(SQUARES), P]), ("laT", [P, 3, P]), ("lbT", [P, 3, P]),
                         ("sel", [P, HD, P]), ("head_mean", [P, P]), ("head_centre", [P, P]),
                         ("state0", [P, HD]), ("neg_rate", [P, 1]), ("floor", [P, 1]), ("eps", [P, 1]), ("neg_half", [P, MOST]),
                         ("e_temp", [P, MOST]), ("e_one", [P, MOST]), ("replace", [P, GROUPS, 8]), ("gate_bias", [P, E]),
                         ("gate0", [P, E]), ("before", [P, P]), ("ones", [P, P]), ("tile_start", [1, MOST_TILES]), ("zeros", [P, 1, D]),
                         ("post_g", [P, D]), ("post_b", [P, D])):
            res[n] = sb(n, shape)
        res["spread"] = sb("spread", [P, HD, P], F32R)
        res["cols"] = res["laT"][:, 2, LORA:LORA + COLS]
        later = {n: nc.alloc_semaphore(name=n) for n in ("x_in", *(f"slots_zeroed{p}" for p in range(PARTS)), "gelu_in", "bias_in", "attention_in", "swiglu_in")}
        slots_x = nc.dram_tensor("slots_x", (PLACES, D), F32).ap()
        slots_y = nc.dram_tensor("slots_y", (PLACES, D), F32).ap()
        with ExitStack() as raw:
            for n, shape in (("raw_s1", [P, E * FI // P, D]), ("raw_s3", [P, E * FI // P, D]), ("raw_s2", [P, E, FI]),
                             ("s13", [P, E, FF]), ("s2", [P, E * FI // P, D])):
                res[n] = raw.enter_context(nc.sbuf_tensor(n, shape, F32))
            as_groups = lambda t: t.rearrange("p e f -> p (e f)").rearrange("p (g d) -> p g d", d=D)
            idle_first = [as_groups(res["s13"][:, k * E // 2:(k + 1) * E // 2, :]) for k in range(TOP)]
            idle = [res[n][:, :, :] for n in ("raw_s1", "raw_s3")]
            with ExitStack() as first:
                for n, shape in (("w1", [P, E, WIDE]), ("w2", [P, E * FF // P, D]), ("bias", [P, E * D]), ("raw_sq", [P, len(SQUARES), P]), ("raw_la", [P, 3, P]), ("raw_lb", [P, 3, P])):
                    res[n] = first.enter_context(nc.sbuf_tensor(n, shape, F32))
                setup(nc, ins, x, res, ident, slots_x, later)
                if layers > 0:
                    mixture(nc, "gelu0", "gelu", x, res, ident, slots_x, slots_y, idle_first, later,
                            attention_loads(ins, res, block_diag, later), block_diag)
                if layers > 1:
                    state_space(nc, x, res, ident, later["swiglu_in"])
                if layers > 2:
                    mixture(nc, "gelu1", "gelu", x, res, ident, slots_x, slots_y, idle)
            if layers > 3:
                mixture(nc, "swiglu0", "swiglu", x, res, ident, slots_x, slots_y, idle)
            if layers > 4:
                receptance(nc, x, res, ident, block_diag)
            if layers > 5:
                mixture(nc, "swiglu1", "swiglu", x, res, ident, slots_x, slots_y, idle, out=out)


_INS = ["L0_attn_x", "L0_attn_W_in", "L0_attn_W_state", "L0_attn_W_dt", "L0_attn_b_dt", "L0_attn_A_log", "L0_attn_W_C",
        "L0_attn_D", "L0_attn_W_out", "L0_ffn_gate_w", "L0_ffn_gate_b", "L0_ffn_w1", "L0_ffn_b1", "L0_ffn_w2", "L0_ffn_b2",
        "L0_ffn_ln_g", "L0_ffn_ln_b", "L1_attn_xw", "L1_attn_rW", "L1_attn_kW", "L1_attn_vW", "L1_attn_gW",
        "L1_attn_r_la", "L1_attn_r_lb", "L1_attn_r_ll", "L1_attn_k_la", "L1_attn_k_lb", "L1_attn_k_ll",
        "L1_attn_v_la", "L1_attn_v_lb", "L1_attn_v_ll", "L1_attn_g_la", "L1_attn_g_lb", "L1_attn_g_ll",
        "L1_attn_d_la", "L1_attn_d_lb", "L1_attn_d_ll", "L1_attn_ln_w", "L1_attn_ln_b", "L1_attn_oW",
        "L1_attn_init_state", "L1_attn_u", "L1_ffn_wg", "L1_ffn_w1", "L1_ffn_w3", "L1_ffn_w2"]


def kernel(**inputs):
    import numpy as _np
    import concourse.bacc as _bacc
    from concourse import mybir as _mybir
    from concourse.bass_utils import run_bass_kernel_spmd as _run

    nc = _bacc.Bacc("TRN2", target_bir_lowering=False, num_devices=1)
    arrays, aps = {}, {}
    given = {n: _np.ascontiguousarray(inputs[n]) for n in _INS}
    given["const_ident"] = _np.eye(P, dtype=_np.float32)
    given["const_block"] = _np.kron(_np.eye(HEADS, dtype=_np.float32), _np.ones((HD, HD), _np.float32))
    given["const_before"] = _np.triu(_np.ones((P, P), _np.float32), 1)
    given["const_tile_start"] = (P * _np.arange(MOST_TILES, dtype=_np.float32)).reshape(1, -1)
    given["b1_columns"] = _np.ascontiguousarray(given.pop("L0_ffn_b1").reshape(E, FF // P, P).transpose(2, 0, 1))
    for n, a in given.items():
        arrays[f"in_{n}"] = a
        aps[n] = nc.dram_tensor(f"in_{n}", a.shape, _mybir.dt.from_np(a.dtype), kind="ExternalInput").ap()
    out = nc.dram_tensor("out_x", (NB, SEQ, D), F32, kind="ExternalOutput").ap()
    build(nc, aps, out)
    r = _run(nc, [arrays], core_ids=[0])
    return r.results[0]["out_x"]
```
